# Optimizing a Trainium2 kernel written in Bass

```python
import numpy as np
import jax
import jax.numpy as jnp

def _softmax(x, axis=-1):
    return jax.nn.softmax(x, axis=axis)

def _gelu(x):
    return jax.nn.gelu(x, approximate=True)

def _silu(x):
    return jax.nn.silu(x)

def _sigmoid(x):
    return jax.nn.sigmoid(x)

def _layernorm(x, axis=-1, eps=1e-05):
    m = jnp.mean(x, axis=axis, keepdims=True)
    v = jnp.var(x, axis=axis, keepdims=True)
    return (x - m) / jnp.sqrt(v + eps)

def _scatter_add(tgt, idx, src, axis=0):
    return tgt.at[idx].add(src)

def _segment_sum(src, seg, n):
    return jax.ops.segment_sum(src, seg, n)
kernel_name = 'mk_decoder_preln_d1_seqx_r2_602f76'

def setup_inputs(seed: int=0):
    np.random.seed(seed)
    _w = jnp.asarray

    def _rec_inputs():
        import jax
        import jax.numpy as jnp
        _rk = jax.random.key(seed)
        x = -0.0003929 + 0.9999 * jax.random.normal(jax.random.fold_in(_rk, 1), (8, 100, 512), jnp.float32)
        _lenS = 100 - jax.random.randint(jax.random.fold_in(_rk, 7), (8,), 0, max(1, 100 // 4) + 1, jnp.int32)
        _lenS2 = 722 - jax.random.randint(jax.random.fold_in(_rk, 8), (8,), 0, max(1, 722 // 4) + 1, jnp.int32)
        _ctx_1024P = jax.random.normal(jax.random.fold_in(_rk, 11), (8, 16, 512), jnp.float32)
        _ctx_1024c = jax.random.dirichlet(jax.random.fold_in(_rk, 511), 0.3 * jnp.ones((16,), jnp.float32), (8, 722))
        _ctx_1024t = jnp.einsum('bsk,bkd->bsd', _ctx_1024c, _ctx_1024P)
        _ctx_1024t = _ctx_1024t * jax.lax.rsqrt(jnp.mean(jnp.square(_ctx_1024t)) + 1e-12) * 0.953939
        ctx_1024 = 2.81802e-05 + 1.00001 * (_ctx_1024t + 0.3 * jax.random.normal(jax.random.fold_in(_rk, 611), (8, 722, 512), jnp.float32))
        _validS = jnp.arange(100)[None, :] < _lenS[:, None]
        _validS2 = jnp.arange(722)[None, :] < _lenS2[:, None]
        _causal = jnp.tril(jnp.ones((100, 100), dtype=bool))
        mask_Bx1xS2_fk0 = jnp.where(jnp.broadcast_to(_validS2[:, None, :], (8, 1, 722)), 0.0, 1.0).astype(jnp.float32)
        return (x, ctx_1024, mask_Bx1xS2_fk0)
    x, ctx_1024, mask_Bx1xS2_fk0 = _rec_inputs()

    def _L0_attn_setup():
        import jax, jax.numpy as jnp
        import numpy as np
        DIM = 512
        H = 16
        DH = DIM // H
        K = 4
        B = 8
        N = 1024
        EPS = 1e-06

        def _depthwise_conv_silu(x, w, n):
            pad = K // 2
            y = jax.lax.conv_general_dilated(x.transpose(0, 2, 1), w, window_strides=(1,), padding=[(pad, pad)], dimension_numbers=('NCH', 'OIH', 'NCH'), feature_group_count=x.shape[-1])
            y = y[..., :n]
            return jax.nn.silu(y).transpose(0, 2, 1)

        def _l2norm(x):
            return x / (jnp.linalg.norm(x, axis=-1, keepdims=True) + EPS)

        def _forward(x, Wq, bq, Wk, bk, Wv, bv, Wa, ba, Wb, bb, conv_q, conv_k, conv_v, Wo, bo):
            b_, n_, c_ = x.shape
            q = _l2norm(_depthwise_conv_silu(jax.nn.silu(x @ Wq.T + bq), conv_q, n_))
            k = _l2norm(_depthwise_conv_silu(jax.nn.silu(x @ Wk.T + bk), conv_k, n_))
            v = _depthwise_conv_silu(jax.nn.silu(x @ Wv.T + bv), conv_v, n_)
            a = jax.nn.sigmoid(x @ Wa.T + ba)
            bgate = jax.nn.sigmoid(x @ Wb.T + bb)
            q = q.reshape(b_, n_, H, DH).transpose(1, 0, 2, 3)
            k = k.reshape(b_, n_, H, DH).transpose(1, 0, 2, 3)
            v = v.reshape(b_, n_, H, DH).transpose(1, 0, 2, 3)
            a = a.transpose(1, 0, 2)
            bgate = bgate.transpose(1, 0, 2)
            S0 = jnp.zeros((b_, H, DH, DH), x.dtype)

            def step(S, inp):
                qt, kt, vt, at, bt = inp
                at = at[..., None, None]
                bt = bt[..., None, None]
                Sk = jnp.einsum('bhde,bhe->bhd', S, kt)
                outer_Sk_k = Sk[..., :, None] * kt[..., None, :]
                outer_v_k = vt[..., :, None] * kt[..., None, :]
                S_new = at * S - at * bt * outer_Sk_k + bt * outer_v_k
                ot = jnp.einsum('bhd,bhde->bhe', qt, S_new)
                return (S_new, ot)
            _, O = jax.lax.scan(step, S0, (q, k, v, a, bgate))
            O = O.transpose(1, 0, 2, 3).reshape(b_, n_, c_)
            return O @ Wo.T + bo
        key = jax.random.key(seed)
        ks = jax.random.split(key, 16)
        s = 1.0 / np.sqrt(DIM)
        d = dict(x=jax.random.normal(ks[0], (B, N, DIM), jnp.float32), Wq=jax.random.normal(ks[1], (DIM, DIM), jnp.float32) * s, bq=jnp.zeros((DIM,), jnp.float32), Wk=jax.random.normal(ks[2], (DIM, DIM), jnp.float32) * s, bk=jnp.zeros((DIM,), jnp.float32), Wv=jax.random.normal(ks[3], (DIM, DIM), jnp.float32) * s, bv=jnp.zeros((DIM,), jnp.float32), Wa=jax.random.normal(ks[4], (H, DIM), jnp.float32) * s, ba=jnp.zeros((H,), jnp.float32), Wb=jax.random.normal(ks[5], (H, DIM), jnp.float32) * s, bb=jnp.zeros((H,), jnp.float32), conv_q=jax.random.normal(ks[6], (DIM, 1, K), jnp.float32) * 0.5, conv_k=jax.random.normal(ks[7], (DIM, 1, K), jnp.float32) * 0.5, conv_v=jax.random.normal(ks[8], (DIM, 1, K), jnp.float32) * 0.5, Wo=jax.random.normal(ks[9], (DIM, DIM), jnp.float32) * s, bo=jnp.zeros((DIM,), jnp.float32))
        return d
    _L0_attn_all = _L0_attn_setup()
    _L0_attn_in = {k: v for k, v in _L0_attn_all.items() if k in ('Wq', 'bq', 'Wk', 'bk', 'Wv', 'bv', 'Wa', 'ba', 'Wb', 'bb', 'conv_q', 'conv_k', 'conv_v', 'Wo', 'bo')}
    del _L0_attn_all

    def _L0_xattn_setup():
        import jax, jax.numpy as jnp
        import numpy as np
        B, S, D = (8, 1024, 512)
        NEG = -1000000000.0
        key = jax.random.key(seed)
        kq, kk, kv, km = jax.random.split(key, 4)
        q = jax.random.normal(kq, (B, S, D), dtype=jnp.float32)
        k = jax.random.normal(kk, (B, S, D), dtype=jnp.float32)
        v = jax.random.normal(kv, (B, S, D), dtype=jnp.float32)
        mask = (jax.random.uniform(km, (B, 1, S)) < 0.1).astype(jnp.float32)
        return {'q': q, 'k': k, 'v': v, 'mask': mask}
    _L0_xattn_all = _L0_xattn_setup()
    _L0_xattn_in = {k: v for k, v in _L0_xattn_all.items() if k in ()}
    del _L0_xattn_all

    def _L0_ffn_setup():
        import jax, jax.numpy as jnp
        import numpy as np
        DIM = 512
        HID = 1408
        E = 8
        TOP_K = 2
        EPS = 1e-06

        def _rmsnorm(x, w):
            var = jnp.mean(jnp.square(x), axis=-1, keepdims=True)
            return x * jax.lax.rsqrt(var + EPS) * w
        key = jax.random.key(seed)
        ks = jax.random.split(key, 5)
        x = jax.random.normal(ks[0], (4, 1024, DIM), dtype=jnp.float32)
        norm_weight = jnp.ones((DIM,), dtype=jnp.float32)
        router_weight = jax.random.normal(ks[1], (E, DIM), dtype=jnp.float32) * 0.02
        gate_up_weight = jax.random.normal(ks[2], (E, 2 * HID, DIM), dtype=jnp.float32) * (0.02 / np.sqrt(E))
        down_weight = jax.random.normal(ks[3], (E, DIM, HID), dtype=jnp.float32) * (0.02 / np.sqrt(E))
        residual_alpha = jnp.float32(1.0)
        return {'x': x, 'norm_weight': norm_weight, 'router_weight': router_weight, 'gate_up_weight': gate_up_weight, 'down_weight': down_weight, 'residual_alpha': residual_alpha}
    _L0_ffn_all = _L0_ffn_setup()
    _L0_ffn_in = {k: v for k, v in _L0_ffn_all.items() if k in ('norm_weight', 'router_weight', 'gate_up_weight', 'down_weight', 'residual_alpha')}
    del _L0_ffn_all
    return {'x': x, 'ctx_1024': ctx_1024, 'mask_Bx1xS2_fk0': mask_Bx1xS2_fk0, 'L0_attn_Wq': _L0_attn_in['Wq'], 'L0_attn_bq': _L0_attn_in['bq'], 'L0_attn_Wk': _L0_attn_in['Wk'], 'L0_attn_bk': _L0_attn_in['bk'], 'L0_attn_Wv': _L0_attn_in['Wv'], 'L0_attn_bv': _L0_attn_in['bv'], 'L0_attn_Wa': _L0_attn_in['Wa'], 'L0_attn_ba': _L0_attn_in['ba'], 'L0_attn_Wb': _L0_attn_in['Wb'], 'L0_attn_bb': _L0_attn_in['bb'], 'L0_attn_conv_q': _L0_attn_in['conv_q'], 'L0_attn_conv_k': _L0_attn_in['conv_k'], 'L0_attn_conv_v': _L0_attn_in['conv_v'], 'L0_attn_Wo': _L0_attn_in['Wo'], 'L0_attn_bo': _L0_attn_in['bo'], 'L0_ffn_norm_weight': _L0_ffn_in['norm_weight'], 'L0_ffn_router_weight': _L0_ffn_in['router_weight'], 'L0_ffn_gate_up_weight': _L0_ffn_in['gate_up_weight'], 'L0_ffn_down_weight': _L0_ffn_in['down_weight'], 'L0_ffn_residual_alpha': _L0_ffn_in['residual_alpha']}

def reference(x, ctx_1024, mask_Bx1xS2_fk0, L0_attn_Wq, L0_attn_bq, L0_attn_Wk, L0_attn_bk, L0_attn_Wv, L0_attn_bv, L0_attn_Wa, L0_attn_ba, L0_attn_Wb, L0_attn_bb, L0_attn_conv_q, L0_attn_conv_k, L0_attn_conv_v, L0_attn_Wo, L0_attn_bo, L0_ffn_norm_weight, L0_ffn_router_weight, L0_ffn_gate_up_weight, L0_ffn_down_weight, L0_ffn_residual_alpha):
    import jax
    import jax.numpy as jnp

    def _L0_attn_ref(x, Wq, bq, Wk, bk, Wv, bv, Wa, ba, Wb, bb, conv_q, conv_k, conv_v, Wo, bo):
        import jax, jax.numpy as jnp
        import numpy as np
        DIM = 512
        H = 16
        DH = DIM // H
        K = 4
        B = 8
        N = 1024
        EPS = 1e-06

        def _depthwise_conv_silu(x, w, n):
            pad = K // 2
            y = jax.lax.conv_general_dilated(x.transpose(0, 2, 1), w, window_strides=(1,), padding=[(pad, pad)], dimension_numbers=('NCH', 'OIH', 'NCH'), feature_group_count=x.shape[-1])
            y = y[..., :n]
            return jax.nn.silu(y).transpose(0, 2, 1)

        def _l2norm(x):
            return x / (jnp.linalg.norm(x, axis=-1, keepdims=True) + EPS)

        def _forward(x, Wq, bq, Wk, bk, Wv, bv, Wa, ba, Wb, bb, conv_q, conv_k, conv_v, Wo, bo):
            b_, n_, c_ = x.shape
            q = _l2norm(_depthwise_conv_silu(jax.nn.silu(x @ Wq.T + bq), conv_q, n_))
            k = _l2norm(_depthwise_conv_silu(jax.nn.silu(x @ Wk.T + bk), conv_k, n_))
            v = _depthwise_conv_silu(jax.nn.silu(x @ Wv.T + bv), conv_v, n_)
            a = jax.nn.sigmoid(x @ Wa.T + ba)
            bgate = jax.nn.sigmoid(x @ Wb.T + bb)
            q = q.reshape(b_, n_, H, DH).transpose(1, 0, 2, 3)
            k = k.reshape(b_, n_, H, DH).transpose(1, 0, 2, 3)
            v = v.reshape(b_, n_, H, DH).transpose(1, 0, 2, 3)
            a = a.transpose(1, 0, 2)
            bgate = bgate.transpose(1, 0, 2)
            S0 = jnp.zeros((b_, H, DH, DH), x.dtype)

            def step(S, inp):
                qt, kt, vt, at, bt = inp
                at = at[..., None, None]
                bt = bt[..., None, None]
                Sk = jnp.einsum('bhde,bhe->bhd', S, kt)
                outer_Sk_k = Sk[..., :, None] * kt[..., None, :]
                outer_v_k = vt[..., :, None] * kt[..., None, :]
                S_new = at * S - at * bt * outer_Sk_k + bt * outer_v_k
                ot = jnp.einsum('bhd,bhde->bhe', qt, S_new)
                return (S_new, ot)
            _, O = jax.lax.scan(step, S0, (q, k, v, a, bgate))
            O = O.transpose(1, 0, 2, 3).reshape(b_, n_, c_)
            return O @ Wo.T + bo
        return _forward(x, Wq, bq, Wk, bk, Wv, bv, Wa, ba, Wb, bb, conv_q, conv_k, conv_v, Wo, bo)

    def _L0_xattn_ref(q, k, v, mask):
        import jax, jax.numpy as jnp
        import numpy as np
        B, S, D = (8, 1024, 512)
        NEG = -1000000000.0
        scale = jnp.asarray(D ** (-0.5), dtype=q.dtype)
        logits = jnp.einsum('bqd,bkd->bqk', q, k) * scale
        logits = logits + mask * NEG
        attn = jax.nn.softmax(logits, axis=-1)
        return jnp.einsum('bqk,bkd->bqd', attn, v)

    def _L0_ffn_ref(x, norm_weight, router_weight, gate_up_weight, down_weight, residual_alpha):
        import jax, jax.numpy as jnp
        import numpy as np
        DIM = 512
        HID = 1408
        E = 8
        TOP_K = 2
        EPS = 1e-06

        def _rmsnorm(x, w):
            var = jnp.mean(jnp.square(x), axis=-1, keepdims=True)
            return x * jax.lax.rsqrt(var + EPS) * w
        normed = _rmsnorm(x, norm_weight)
        logits = jnp.einsum('bsd,ed->bse', normed, router_weight)
        probs = jax.nn.softmax(logits, axis=-1)
        topk_w, topk_idx = jax.lax.top_k(probs, TOP_K)
        topk_w = topk_w / jnp.sum(topk_w, axis=-1, keepdims=True)
        combine = jnp.sum(jax.nn.one_hot(topk_idx, E, dtype=normed.dtype) * topk_w[..., None], axis=-2)
        moe_out = jnp.zeros_like(x)
        for e in range(E):
            gu = jnp.einsum('bsd,hd->bsh', normed, gate_up_weight[e])
            gate, up = (gu[..., :HID], gu[..., HID:])
            hidden = jax.nn.silu(gate) * up
            out_e = jnp.einsum('bsh,dh->bsd', hidden, down_weight[e])
            moe_out = moe_out + combine[..., e, None] * out_e
        alpha = jnp.clip(residual_alpha, -0.5, 2.0)
        return x + alpha * moe_out
    x = x + _L0_attn_ref(_layernorm(x, axis=-1), L0_attn_Wq, L0_attn_bq, L0_attn_Wk, L0_attn_bk, L0_attn_Wv, L0_attn_bv, L0_attn_Wa, L0_attn_ba, L0_attn_Wb, L0_attn_bb, L0_attn_conv_q, L0_attn_conv_k, L0_attn_conv_v, L0_attn_Wo, L0_attn_bo)
    x = x + _L0_xattn_ref(_layernorm(x, axis=-1), ctx_1024, ctx_1024, mask_Bx1xS2_fk0)
    x = x + _L0_ffn_ref(_layernorm(x, axis=-1), L0_ffn_norm_weight, L0_ffn_router_weight, L0_ffn_gate_up_weight, L0_ffn_down_weight, L0_ffn_residual_alpha)
    return x

_drawn_inputs = setup_inputs


def setup_inputs(seed=0):
    import zlib

    import numpy as np

    out = dict(_drawn_inputs(seed))
    spreads = {'L0_attn_bq': (0.0, 0.8),
     'L0_attn_bk': (0.0, 0.8),
     'L0_attn_bv': (0.0, 0.8),
     'L0_attn_ba': (0.0, 0.8),
     'L0_attn_bb': (0.0, 0.8),
     'L0_attn_bo': (0.0, 0.1),
     'L0_ffn_norm_weight': (1.0, 0.6)}
    factors = {'L0_attn_Wq': 8.0,
     'L0_attn_Wk': 8.0,
     'L0_attn_Wv': 8.0,
     'L0_attn_Wa': 8.0,
     'L0_attn_Wb': 8.0,
     'L0_attn_conv_q': 8.0,
     'L0_attn_conv_k': 8.0,
     'L0_attn_conv_v': 8.0,
     'L0_attn_Wo': 8.0,
     'L0_ffn_router_weight': 8.0,
     'L0_ffn_gate_up_weight': 8.0,
     'L0_ffn_down_weight': 8.0}
    for name, (base, spread) in spreads.items():
        noise = np.random.default_rng([zlib.crc32(name.encode()), seed]).standard_normal(out[name].shape)
        drawn = base * np.exp(spread * noise) if base else spread * noise
        out[name] = jnp.asarray(drawn.astype(out[name].dtype))
    for name, factor in factors.items():
        out[name] = (out[name] * factor).astype(out[name].dtype)
    return out
```

```python
from contextlib import ExitStack

import concourse.bass as bass
from concourse import mybir

ALU = mybir.AluOpType
ACT = mybir.ActivationFunctionType
F32 = mybir.dt.float32
I32 = mybir.dt.int32
AX_X = mybir.AxisListType.X

P = 128
NEG = -1.0e9


class Handoff:

    def __init__(self, eng, sem):
        self.eng, self.sem, self.n = eng, sem, 0

    def __call__(self, ins):
        self.n += 1
        ins.then_inc(self.sem, 1)
        self.eng.wait_ge(self.sem, self.n)


def decoder_layer(nc, x, ctx, ctxT, mask, WqT, WkT, WvT, bqkv, WabT, bab, conv, WoT, bo, norm_w, WrT, GU, DN, alpha, out):
    B, T, D = x.shape
    S2 = ctx.shape[1]
    H, DH = 16, 32
    KC = D // P
    NTOK = B * T
    HALF = NTOK // 2
    HB = B // 2
    TAPS = 4
    TP = T + TAPS - 1
    BLK = [(i, 32 * i, min(32, T - 32 * i)) for i in range(4)]
    LAST = BLK[3][2]
    S2H = S2 // 2
    S2T = [(j, P * j, min(P, S2 - P * j)) for j in range(-(-S2 // P))]
    E, HID = DN.shape[0], DN.shape[2] * P
    HC = HID // P
    CH = [(0, 384), (384, 384), (768, 384), (1152, 256)]
    MAXNT = -(-NTOK // P)
    NITEM = (2 * NTOK + E * (P - 1)) // P + 1
    ZPARTS = 7
    LN_EPS, RMS_EPS, L2_EPS = 1e-5, 1e-6, 1e-6
    SCALE = float(D) ** -0.5
    LEAST_DECAY = 2.0 ** -63

    with ExitStack() as stack:
        sems = {}

        def S(name):
            if name not in sems:
                sems[name] = stack.enter_context(nc.semaphore(name))
            return sems[name]

        base = [16512]

        def at(name, shape, offset, dt=F32):
            return nc.alloc_sbuf_tensor_at(name, list(shape), dt, offset=offset)

        def size(shape):
            n = 4
            for s in shape[1:]:
                n *= s
            return -(-n // 32) * 32

        def place(cursor, name, shape, dt=F32):
            t = at(name, shape, cursor[0], dt)
            cursor[0] += size(shape)
            assert cursor[0] <= 229368, (name, cursor[0])
            return t

        X = place(base, "X", [T, B, D])
        ident = place(base, "ident", [P, P])
        later = place(base, "later", [P, P])
        upto = place(base, "upto", [P, P])
        before = place(base, "before", [P, P])
        ones = place(base, "ones", [P, P])
        eps_ln = place(base, "eps_ln", [P, 1])
        eps_rms = place(base, "eps_rms", [P, 1])
        zero_col = place(base, "zero_col", [P, 1])
        stats = place(base, "stats", [T, B, 6])
        mv = place(base, "mv", [T, B, 2])
        rstd = place(base, "rstd", [T, B])
        gtok = place(base, "gtok", [T, B, 32])
        la = place(base, "la", [T, B, H])
        sd = place(base, "sd", [T, B])
        nmax = place(base, "nmax", [T, B])
        rsum = place(base, "rsum", [T, B])
        ss = place(base, "ss", [T, B])
        LG = place(base, "LG", [T, B, E])
        r_names = "rt_p rt_eq rt_io rt_o0 rt_o1 rt_t rt_pos".split()
        rt_p, rt_eq, rt_io, rt_o0, rt_o1, rt_t, rt_pos = [place(base, n, [T, B, E]) for n in r_names]
        rt_m = place(base, "rt_m", [T, B, 8])
        rt_boff = place(base, "rt_boff", [T, B + 1, E])
        rt_nt = place(base, "rt_nt", [T, E])
        rt_bs = place(base, "rt_bs", [T, E + 1])
        gf = place(base, "gf", [T, 2, B])
        gi = place(base, "gi", [T, 2, B], I32)
        nti = place(base, "nti", [T, 2, E], I32)
        al = place(base, "al", [T, 1])
        wa = place(base, "wa", [T, 2, B])
        XN = place(base, "XN", [T, B, D])
        later_phases = base[0]

        cur = [later_phases]
        qT = place(cur, "qT", [P, KC, B, T])
        Wo = place(cur, "Wo", [P, KC, D])
        Kt = place(cur, "Kt", [T, B, D])
        Vt = place(cur, "Vt", [T, B, D])
        after_b = cur[0]
        kT = place(cur, "kT", [P, KC, B, T])
        vT = place(cur, "vT", [P, KC, B, T])
        b_only = cur[0]
        W3 = [place(cur, f"W_{n}", [P, KC, D]) for n in "kqv"]
        xT = place(cur, "xT", [P, KC, B, T])
        PB = place(cur, "PB", [P, KC, B, TP])
        PB2 = at("PB2", [P, KC, B, TP], after_b - 2 * size([T, B, D]))
        SQ = at("SQ", [P, KC, B, T], after_b - size([T, B, D]))
        rn = place(cur, "rn", [P, B, T])
        gT = place(cur, "gT", [32, B, T])
        Wab = place(cur, "Wab", [P, KC, 32])
        b_ab = place(cur, "b_ab", [32, 1])
        b_qkv = place(cur, "b_qkv", [P, 3, KC])
        w_conv = place(cur, "w_conv", [P, 3, KC, TAPS])
        ZR = place(cur, "ZR", [P, NITEM * D // ZPARTS])
        cur = [b_only]
        LR = [place(cur, f"LR{p}", [T, H, T]) for p in (0, 1)]
        MB = [place(cur, f"MB{p}", [T, H, T]) for p in (0, 1)]
        EB = [place(cur, f"EB{p}", [T, H, T]) for p in (0, 1)]
        BB = [place(cur, f"BB{p}", [T, H, T]) for p in (0, 1)]
        cur = [after_b]
        DG = place(cur, "DG", [P, 3, 32, 32])
        MI = place(cur, "MI", [P, 3, 32, 32])
        DG3 = place(cur, "DG3", [P, LAST, LAST])
        MI3 = place(cur, "MI3", [P, LAST, LAST])
        TM = place(cur, "TM", [P, 3 * 32 * 32])
        cur = [after_b]
        bo_b = place(cur, "bo_b", [T, D])
        nw_b = place(cur, "nw_b", [T, D])
        Wr = place(cur, "Wr", [P, KC, E])
        EE = [place(cur, f"EE{p}", [T, H, T]) for p in (0, 1)]
        BC = [place(cur, f"BC{p}", [T, H, T]) for p in (0, 1)]
        MT = [place(cur, f"MT{p}", [T, H, 32]) for p in (0, 1)]
        UU = [place(cur, f"UU{p}", [T, D]) for p in (0, 1)]
        RR = [place(cur, f"RR{p}", [T, D]) for p in (0, 1)]
        TR = [place(cur, f"TR{p}", [P, KC, T]) for p in (0, 1)]
        CT = [place(cur, f"CT{p}", [P, KC, S2]) for p in (0, 1)]
        CN = place(cur, "CN", [P, len(S2T), D])
        MN = [place(cur, f"MN{p}", [T, S2]) for p in (0, 1)]
        PR = [place(cur, f"PR{p}", [T, S2]) for p in (0, 1)]
        PT = [place(cur, f"PT{p}", [P, len(S2T), T]) for p in (0, 1)]
        cur = [later_phases]
        GW = [place(cur, f"GW{p}", [P, KC, 2 * HID]) for p in (0, 1)]
        DW = [place(cur, f"DW{p}", [P, HC, D]) for p in (0, 1)]
        XG = place(cur, "XG", [P, D])
        XGT = place(cur, "XGT", [P, KC, P])
        HS = place(cur, "HS", [P, HID])
        HH = place(cur, "HH", [P, HID])
        HT = place(cur, "HT", [P, HC, P])
        YS = place(cur, "YS", [P, D])
        YG = at("YG", [T, 2, B, D], later_phases)

        PS = [stack.enter_context(nc.psum_tensor(f"PS{i}", [P, 512], F32)) for i in range(8)]

        def dram(name, shape, dt=F32):
            return nc.dram_tensor(name, list(shape), dt, kind="Internal").ap()

        Ed = dram("Ed", [B, T, H, T])
        Bd = dram("Bd", [B, T, H, T])
        Md = dram("Md", [B * H, 3, 32, 32])
        Md3 = dram("Md3", [B * H, LAST, LAST])
        XGd = dram("XGd", [NITEM * P, D])
        YGd = dram("YGd", [NITEM * P, D])

        block = stack.enter_context(nc.Block())

        @block.sync
        def _(sp):
            for b in range(B):
                sp.dma_start(X[:, b, :], x[b]).then_inc(S(f"x_in{b}"), 16)
            sp.dma_start(W3[0][:], WkT.rearrange("(k p) n -> p k n", p=P)).then_inc(S("wk_in"), 16)
            sp.dma_start(W3[2][:], WvT.rearrange("(k p) n -> p k n", p=P)).then_inc(S("wv_in"), 16)
            sp.dma_start(W3[1][:], WqT.rearrange("(k p) n -> p k n", p=P)).then_inc(S("wq_in"), 16)
            sp.dma_start(Wo[:], WoT.rearrange("(k p) n -> p k n", p=P)).then_inc(S("wo_in"), 16)
            sp.wait_ge(S("zr_set"), 1)
            for j in range(ZPARTS):
                n = NITEM * P // ZPARTS
                for rows in (XGd, YGd):
                    sp.dma_start(rows[j * n:(j + 1) * n, :].rearrange("(p r) d -> p (r d)", p=P), ZR[:, :]).then_inc(S("rows_zero"), 16)
            for b in range(B):
                p = b % 2
                sp.wait_ge(S("e_done"), b + 1)
                sp.dma_start(Ed[b], EB[p][:]).then_inc(S(f"ed_out{p}"), 16)
                sp.wait_ge(S("bb_done"), b + 1)
                sp.dma_start(Bd[b], BB[p][:]).then_inc(S(f"bd_out{p}"), 16)
            sp.wait_ge(S("bb_done"), B)
            sp.wait_ge(S("kv_tok"), 2 * B)
            for p in (0, 1):
                sp.wait_ge(S(f"ed_out{p}"), 16 * B // 2)
                sp.wait_ge(S(f"bd_out{p}"), 16 * B // 2)
            for b in range(B):
                for i, s0, w in BLK:
                    src = Bd[b][s0:s0 + w, :, s0:s0 + w].rearrange("r h s -> h r s")
                    dst = DG[b * H:(b + 1) * H, i] if i < 3 else DG3[b * H:(b + 1) * H]
                    sp.dma_start(dst, src).then_inc(S("dg_in"), 16)
            sp.wait_ge(S("mi_done"), 1)
            sp.dma_start(Md[:], MI[:]).then_inc(S("md_out"), 16)
            sp.dma_start(Md3[:], MI3[:]).then_inc(S("md_out"), 16)
            sp.wait_ge(S("md_out"), 32)
            sp.dma_start(bo_b[:], bo.partition_broadcast(T)).then_inc(S("cw_in"), 16)
            sp.dma_start(nw_b[:], norm_w.partition_broadcast(T)).then_inc(S("cw_in"), 16)
            sp.dma_start(al[:], alpha.partition_broadcast(T)).then_inc(S("al_in"), 16)
            sp.dma_start(Wr[:], WrT.rearrange("(k p) n -> p k n", p=P)).then_inc(S("cw_in"), 16)
            for b in range(B):
                p = b % 2
                if b >= 2:
                    sp.wait_ge(S("o_done"), b - 1)
                for i, s0, w in BLK:
                    m = Md[b * H:(b + 1) * H, i] if i < 3 else Md3[b * H:(b + 1) * H]
                    sp.dma_start(MT[p][s0:s0 + w, :, 0:w], m.rearrange("h r s -> r h s")).then_inc(S(f"mt_in{p}"), 16)
                sp.dma_start(BC[p][:], Bd[b]).then_inc(S(f"bc_in{p}"), 16)
                sp.dma_start(EE[p][:], Ed[b]).then_inc(S(f"ee_in{p}"), 16)
                if b >= 2:
                    sp.wait_ge(S("sc_pe"), b - 1)
                    sp.wait_ge(S("sc_dve"), b - 1)
                sp.dma_start(CT[p][:], ctxT[b].rearrange("(k p) s -> p k s", p=P)).then_inc(S(f"ct_in{p}"), 16)
                sp.dma_start(MN[p][:], mask[b].partition_broadcast(T).rearrange("t o s -> t (o s)")).then_inc(S(f"mn_in{p}"), 16)
                if b >= 1:
                    sp.wait_ge(S("pv_pe"), b)
                full = S2T[-1][0]
                sp.dma_start(CN[:, 0:full, :], ctx[b][0:full * P, :].rearrange("(j p) d -> p j d", p=P)).then_inc(S("cn_in"), 16)
                sp.dma_start(CN[0:S2 - full * P, full, :], ctx[b][full * P:S2, :]).then_inc(S("cn_in"), 16)

            sp.wait_ge(S("xn_all"), B)
            sp.wait_ge(S("xy_done"), B)
            sp.wait_ge(S("lg_done"), B)
            for e in (0, 1):
                sp.dma_start(GW[e][:], GU[e]).then_inc(S(f"gw_in{e}"), 16)
                sp.dma_start(DW[e][:], DN[e]).then_inc(S(f"dw_in{e}"), 16)
            sp.wait_ge(S("rows_zero"), 16 * 2 * ZPARTS)
            sp.wait_ge(S("xg_scat"), 16 * 2 * B)
            sp.dma_start(XG[:], XGd[0:P, :]).then_inc(S("xg_in"), 16)
            sp.wait_ge(S("nt_set"), 1)
            def tiles_of(e):
                nt = sp.value_load(nti[0:1, 0, bass.ds(e, 1)], min_val=1, max_val=MAXNT)
                first = sp.value_load(nti[0:1, 1, bass.ds(e, 1)], min_val=0, max_val=NITEM - 2)
                done = sp.snap(first + nt)
                with sp.Fori(0, nt) as tile:
                    item = nc.s_assert_within(sp.snap(first + tile), 0, NITEM - 2)
                    sp.wait_ge(S("xg_tr"), item + 1)
                    sp.dma_start(XG[:], XGd[bass.ds((item + 1) * P, P), :]).then_inc(S("xg_in"), 16)
                    sp.wait_ge(S("y_out"), item + 1)
                    sp.dma_start(YGd[bass.ds(item * P, P), :], YS[:]).then_inc(S("y_stored"), 16)
                return done

            with sp.Fori(0, E // 2 - 1) as pair:
                for q in (0, 1):
                    e = sp.snap(pair * 2 + q)
                    done = tiles_of(e)
                    sp.wait_ge(S("y_pe"), done)
                    sp.dma_start(GW[q][:], GU[bass.ds(e + 2, 1)].rearrange("o p k n -> p (o k) n")).then_inc(S(f"gw_in{q}"), 16)
                    sp.dma_start(DW[q][:], DN[bass.ds(e + 2, 1)].rearrange("o p k n -> p (o k) n")).then_inc(S(f"dw_in{q}"), 16)
            for e in (E - 2, E - 1):
                tiles_of(e)
            for b in range(B):
                sp.wait_ge(S("fin"), b + 1)
                sp.dma_start(out[b], X[:, b, :]).then_inc(S("out_st"), 16)
            sp.wait_ge(S("out_st"), 16 * B)

        @block.gpsimd
        def _(pool):
            own = Handoff(pool, S("pool_own"))
            for t, v in ((ident, 0.0), (later, 0.0), (upto, 0.0), (before, 0.0)):
                last = pool.memset(t[:], v)
            own(last)
            for t, sign, op in ((ident, 1, ALU.not_equal), (later, -1, ALU.is_ge), (upto, 1, ALU.is_gt), (before, 1, ALU.is_ge)):
                pool.affine_select(out=t[:], in_=t[:], compare_op=op, fill=1.0, base=0, pattern=[[-sign, P]],
                                   channel_multiplier=sign).then_inc(S("masks"), 1)
            pool.memset(ones[:], 1.0).then_inc(S("masks"), 1)
            pool.iota(rt_io[:], [[0, B], [1, E]], base=0, channel_multiplier=0,
                      allow_small_or_imprecise_dtypes=True).then_inc(S("iota_e"), 1)
            pool.wait_ge(S("la_done"), 1)
            pool.wait_ge(S("masks"), 5)
            pool.wait_ge(S("qkv_done"), 1)
            for b in range(B):
                p = b % 2
                if b >= 2:
                    pool.wait_ge(S("ld_pe"), b - 1)
                pool.tensor_tensor(LR[p][:], la[:, b, :].unsqueeze(2).broadcast_to([T, H, T]),
                                   upto[0:T, 0:T].unsqueeze(1).broadcast_to([T, H, T]), ALU.mult).then_inc(S("lr_done"), 1)
                if b >= 2:
                    pool.wait_ge(S("e_done"), b - 1)
                pool.tensor_tensor(MB[p][:], gtok[:, b, H:].unsqueeze(2).broadcast_to([T, H, T]),
                                   upto[0:T, 0:T].unsqueeze(1).broadcast_to([T, H, T]), ALU.mult).then_inc(S("mb_done"), 1)
            pool.wait_ge(S("cw_in"), 48)
            for b in range(B):
                pool.tensor_tensor(X[:, b, :], X[:, b, :], bo_b[:], ALU.add).then_inc(S("xb_done"), 1)
            for b0 in range(0, B, 2):
                for b, p in ((b0, 0), (b0 + 1, 1)):
                    pool.wait_ge(S(f"mn_in{p}"), 16 * (b // 2 + 1))
                    pool.tensor_scalar(MN[p][:], MN[p][:], NEG, None, ALU.mult).then_inc(S("mn_done"), 1)
                for b, p in ((b0, 0), (b0 + 1, 1)):
                    pool.wait_ge(S("y_norm"), b + 1)
                    pool.tensor_tensor(X[:, b, :], X[:, b, :], UU[p][:], ALU.add).then_inc(S("xy_done"), 1)
            pool.wait_ge(S("rows_zero"), 16 * 2 * ZPARTS)
            pool.wait_ge(S("xn_all"), B)
            pool.wait_ge(S("gi_set"), 1)
            for c in (0, 1):
                for b in range(B):
                    pool.indirect_dma_start(XGd[:, :], bass.IndirectOffsetOnAxis(gi[:, c, b:b + 1], 0), XN[:, b, :], None)\
                        .then_inc(S("xg_scat"), 16)
            pool.wait_ge(S("moe_end"), 1)
            for b in range(B):
                for c in (0, 1):
                    pool.indirect_dma_start(YG[:, c, b, :], None, YGd[:, :], bass.IndirectOffsetOnAxis(gi[:, c, b:b + 1], 0))\
                        .then_inc(S(f"yg_in{b % 2}"), 16)
                if b % 2:
                    pool.wait_ge(S("yg_in0"), 16 * 2 * (b // 2 + 1))
                    pool.wait_ge(S("yg_in1"), 16 * 2 * (b // 2 + 1))

        @block.tensor
        def _(pe):
            def mm(o, l, r, start, stop):
                return pe.matmul(o, l, r, start=start, stop=stop)

            pe.wait_ge(S("masks"), 5)
            for b in range(B):
                pe.wait_ge(S("xn_a"), b + 1)
                if b >= 2:
                    pe.wait_ge(S("xt_ev"), b - 1)
                for k in range(KC):
                    last = pe.transpose(PS[b % 2][:, k * T:(k + 1) * T], XN[:, b, k * P:(k + 1) * P], ident[0:T, 0:T])
                last.then_inc(S("xt_pe"), 1)
            pe.wait_ge(S("xt_ev"), B)

            def project(n, w, wsem):
                pe.wait_ge(S(wsem), 16)
                for c in range(KC):
                    for hf in (0, 1):
                        g = n * 8 + c * 2 + hf
                        if g >= 4:
                            pe.wait_ge(S("pj_ev"), g - 3)
                        for k in range(KC):
                            last = mm(PS[4 + g % 4][:, 0:HALF], W3[w][:, k, c * P:(c + 1) * P],
                                      xT[:, k, hf * HB:(hf + 1) * HB, :], k == 0, k == KC - 1)
                        last.then_inc(S("pj_pe"), 1)

            def square_sums(n):
                pe.wait_ge(S("sq_act"), n + 1)
                if n:
                    pe.wait_ge(S("nr_act"), 2 * n)
                for hf in (0, 1):
                    for k in range(KC):
                        last = mm(PS[hf][:, 0:HALF], ones[:], SQ[:, k, hf * HB:(hf + 1) * HB, :], k == 0, k == KC - 1)
                    last.then_inc(S("ns_pe"), 1)

            project(0, 0, "wk_in")
            pe.wait_ge(S("small_in"), 16 * 4)
            for hf in (0, 1):
                for k in range(KC):
                    last = mm(PS[2 + hf][0:32, 0:HALF], Wab[:, k, :], xT[:, k, hf * HB:(hf + 1) * HB, :], k == 0, k == KC - 1)
                last.then_inc(S("gate_pe"), 1)
            project(1, 1, "wq_in")
            pe.wait_ge(S("gate_act"), 2)
            for b in range(B):
                last = pe.transpose(PS[2][0:T, b * 32:(b + 1) * 32], gT[:, b, :], ident[0:32, 0:32])
            last.then_inc(S("gtok_pe"), 1)
            square_sums(0)
            project(2, 2, "wv_in")
            square_sums(1)

            pe.wait_ge(S("qkv_done"), 1)
            for b in range(B):
                p = b % 2
                pe.wait_ge(S("lr_done"), b + 1)
                if b >= 1:
                    pe.wait_ge(S("ex_act"), b)
                for i in range(4):
                    last = mm(PS[i][0:T, 0:4 * T], later[0:T, 0:T], LR[p][:, 4 * i:4 * i + 4, :], True, True)
                last.then_inc(S("ld_pe"), 1)
                for n, src in ((0, kT), (1, vT)):
                    if b >= 1:
                        pe.wait_ge(S("bb_done"), b)
                    for c in range(KC):
                        last = pe.transpose(PS[4 + n][0:T, c * P:(c + 1) * P], src[:, c, b, :], ident[:])
                    last.then_inc(S("kv_pe"), 1)
                pe.wait_ge(S("kv_tok"), 2 * b + 2)
                for i in range(4):
                    for c in range(KC):
                        kk = kT[32 * i:32 * i + 32, c, b, :]
                        last = pe.matmul(PS[4 + i][0:T, c * T:(c + 1) * T], kk, kk, start=True, stop=True)
                last.then_inc(S("g_pe"), 1)

            pe.wait_ge(S("wo_in"), 16)
            pe.wait_ge(S("cw_in"), 48)

            def transposed(src, b, bank, sem):
                for k in range(KC):
                    last = pe.transpose(bank[:, k * T:(k + 1) * T], src[:, k * P:(k + 1) * P], ident[0:T, 0:T])
                last.then_inc(S(sem), 1)

            for b0 in range(0, B, 2):
                two = [(b0 + p, p, PS[4 * p:4 * p + 4]) for p in (0, 1)]
                for i, s0, w in BLK:
                    if i:
                        for b, p, bank in two:
                            pe.wait_ge(S(f"bc_in{p}"), 16 * (b // 2 + 1))
                            pe.wait_ge(S("u_ev"), 4 * b0 + 2 * (i - 1) + p + 1)
                            for h in range(H):
                                c, g = h // 4, h % 4
                                last = mm(bank[1][s0:s0 + w, h * DH:(h + 1) * DH], BC[p][0:s0, g * 4 + c, s0:s0 + w],
                                          UU[p][0:s0, h * DH:(h + 1) * DH], True, True)
                            last.then_inc(S("acc_pe"), 1)
                    for b, p, bank in two:
                        if i:
                            pe.wait_ge(S("r_done"), 3 * b0 + 2 * (i - 1) + p + 1)
                        else:
                            pe.wait_ge(S(f"mt_in{p}"), 64 * (b // 2 + 1))
                            if b0:
                                pe.wait_ge(S("lg_done"), b - 1)
                        for h in range(H):
                            c, g = h // 4, h % 4
                            rhs = RR[p][s0:s0 + w, h * DH:(h + 1) * DH] if i else Vt[0:w, b, h * DH:(h + 1) * DH]
                            last = mm(bank[0][s0:s0 + w, h * DH:(h + 1) * DH], MT[p][s0:s0 + w, g * 4 + c, 0:w], rhs, True, True)
                        last.then_inc(S("u_pe"), 1)
                for b, p, bank in two:
                    pe.wait_ge(S("u_ev"), 4 * b0 + 6 + p + 1)
                    transposed(UU[p], b, bank[2], "ut_pe")
                for b, p, bank in two:
                    pe.wait_ge(S("ut_ev"), b + 1)
                    for g in range(4):
                        for c in range(KC):
                            last = pe.matmul(bank[g][0:T, c * T:(c + 1) * T], TR[p][32 * g:32 * g + 32, c, :],
                                             qT[32 * g:32 * g + 32, c, b, :], start=True, stop=True)
                    last.then_inc(S("w_pe"), 1)
                for b, p, bank in two:
                    pe.wait_ge(S("wm_done"), b + 1)
                    for h in range(H):
                        c, g = h // 4, h % 4
                        last = mm(bank[0][0:T, h * DH:(h + 1) * DH], BC[p][:, g * 4 + c, :], Kt[:, b, h * DH:(h + 1) * DH], True, True)
                    last.then_inc(S("o_pe"), 1)
                for b, p, bank in two:
                    pe.wait_ge(S("o_done"), b + 1)
                    transposed(RR[p], b, bank[1], "ot_pe")
                for b, p, bank in two:
                    pe.wait_ge(S("ot_ev"), b + 1)
                    for k in range(KC):
                        last = mm(bank[2][0:T, :], TR[p][:, k, :], Wo[:, k, :], k == 0, k == KC - 1)
                    last.then_inc(S("wo_pe"), 1)
                for b, p, bank in two:
                    pe.wait_ge(S("xh_done"), b + 1)
                    transposed(UU[p], b, bank[3], "xh_pe")
                for b, p, bank in two:
                    pe.wait_ge(S("xh_ev"), b + 1)
                    pe.wait_ge(S(f"ct_in{p}"), 16 * (b // 2 + 1))
                    for hf in (0, 1):
                        for k in range(KC):
                            last = mm(bank[hf][0:T, 0:S2H], TR[p][:, k, :], CT[p][:, k, hf * S2H:(hf + 1) * S2H], k == 0, k == KC - 1)
                    last.then_inc(S("sc_pe"), 1)
                for b, p, bank in two:
                    pe.wait_ge(S("pr_done"), b + 1)
                    for j, s0, w in S2T:
                        last = pe.transpose(bank[2 + j // 4][0:w, (j % 4) * T:(j % 4 + 1) * T], PR[p][:, s0:s0 + w], ident[0:T, 0:T])
                    last.then_inc(S("pt_pe"), 1)
                for b, p, bank in two:
                    pe.wait_ge(S("pt_ev"), b + 1)
                    pe.wait_ge(S("cn_in"), 32 * (b + 1))
                    for j, s0, w in S2T:
                        last = mm(bank[0][0:T, :], PT[p][0:w, j, :], CN[0:w, j, :], j == 0, j == len(S2T) - 1)
                    last.then_inc(S("pv_pe"), 1)
                for b, p, bank in two:
                    pe.wait_ge(S("xn_all"), b + 1)
                    for k in range(KC):
                        last = pe.transpose(bank[1][:, k * T:(k + 1) * T], XN[:, b, k * P:(k + 1) * P], ident[0:T, 0:T])
                    last.then_inc(S("nt_pe"), 1)
                for b, p, bank in two:
                    pe.wait_ge(S("nt_ev"), b + 1)
                    for k in range(KC):
                        last = mm(bank[2][0:T, 0:E], TR[p][:, k, :], Wr[:, k, :], k == 0, k == KC - 1)
                    last.then_inc(S("lg_pe"), 1)

            pe.wait_ge(S("sel_done"), 1)
            mm(PS[0][0:T, 0:B * E], before[0:T, 0:T], rt_eq[:].rearrange("t b e -> t (b e)"), True, True)
            mm(PS[1][0:T, 0:B * E], ones[0:T, 0:T], rt_eq[:].rearrange("t b e -> t (b e)"), True, True).then_inc(S("cnt_pe"), 1)

            def tile_transposed():
                for k in range(KC):
                    last = pe.transpose(PS[6][:, k * P:(k + 1) * P], XG[:, k * P:(k + 1) * P], ident[:])
                last.then_inc(S("xg_tr"), 1)

            pe.wait_ge(S("nt_set"), 1)
            pe.wait_ge(S("xg_in"), 16)
            tile_transposed()
            with pe.Fori(0, E // 2) as pair:
                for q in (0, 1):
                    nt = pe.value_load(nti[0:1, 0, bass.ds(pair * 2 + q, 1)], min_val=1, max_val=MAXNT)
                    first = pe.value_load(nti[0:1, 1, bass.ds(pair * 2 + q, 1)], min_val=0, max_val=NITEM - 2)
                    gw, dw = GW[q], DW[q]
                    loads = pe.snap((pair + 1) * 16)
                    with pe.Fori(0, nt) as tile:
                        item = pe.snap(first + tile, min_val=0, max_val=NITEM - 2)

                        def hidden_transposed(c):
                            o, w = CH[c]
                            pe.wait_ge(S("h_done"), item * 4 + (c + 3))
                            pe.wait_ge(S("ht_ev"), item * 4 + (c + 1))
                            for j in range(w // P):
                                last = pe.transpose(PS[4 + c % 2][:, j * P:(j + 1) * P], HH[:, o + j * P:o + (j + 1) * P], ident[:])
                            last.then_inc(S("ht_pe"), 1)

                        pe.wait_ge(S(f"gw_in{q}"), loads)
                        pe.wait_ge(S("xt_done"), item + 1)
                        for c, (o, w) in enumerate(CH):
                            pe.wait_ge(S("h_done"), item * 4 + (c + 1))
                            for half in (0, 1):
                                for k in range(KC):
                                    last = mm(PS[2 * (c % 2) + half][:, 0:w], XGT[:, k, :],
                                              gw[:, k, half * HID + o:half * HID + o + w], k == 0, k == KC - 1)
                            last.then_inc(S("gu_pe"), 1)
                            if c:
                                hidden_transposed(c - 1)
                        pe.wait_ge(S("xg_in"), (item + 2) * 16)
                        tile_transposed()
                        hidden_transposed(3)
                        pe.wait_ge(S("ht_ev"), item * 4 + 6)
                        pe.wait_ge(S(f"dw_in{q}"), loads)
                        pe.wait_ge(S("y_ev"), item + 1)
                        for j in range(HC):
                            last = mm(PS[7][:, :], HT[:, j, :], dw[:, j, :], j == 0, j == HC - 1)
                        last.then_inc(S("y_pe"), 1)

        @block.scalar
        def _(act):
            own = Handoff(act, S("act_own"))
            act.dma_start(Wab[:], WabT.rearrange("(k p) n -> p k n", p=P)).then_inc(S("small_in"), 16)
            act.dma_start(b_ab[:], bab).then_inc(S("small_in"), 16)
            act.dma_start(b_qkv[:], bqkv).then_inc(S("small_in"), 16)
            act.dma_start(w_conv[:], conv).then_inc(S("small_in"), 16)
            act.wait_ge(S("consts"), 1)
            act.wait_ge(S("mv_a"), 1)
            act.activation(rstd[:], mv[:, :, 1], ACT.Sqrt, bias=eps_ln[0:T, :]).then_inc(S("sd_a"), 1)
            for b in range(B):
                act.wait_ge(S("xt_pe"), b + 1)
                act.activation(xT[:, :, b, :], PS[b % 2][:, 0:KC * T].rearrange("p (k t) -> p k t", k=KC), ACT.Copy).then_inc(S("xt_ev"), 1)
            act.wait_ge(S("small_in"), 16 * 4)
            act.wait_ge(S("pads"), 1)

            def silu_in(n, w, buf):
                for c in range(KC):
                    for hf in (0, 1):
                        act.wait_ge(S("pj_pe"), n * 8 + c * 2 + hf + 1)
                        act.activation(buf[:, c, hf * HB:(hf + 1) * HB, 2:2 + T],
                                       PS[4 + (c * 2 + hf) % 4][:, 0:HALF].rearrange("p (b t) -> p b t", b=HB), ACT.Silu,
                                       bias=b_qkv[:, w, c:c + 1]).then_inc(S("pj_ev"), 1)

            def silu_out(n, t, squares):
                for c in range(KC):
                    act.wait_ge(S("cv_done"), n * KC + c + 1)
                    last = act.activation(t[:, c], t[:, c], ACT.Silu)
                last.then_inc(S("post_act"), 1)
                if squares:
                    act.wait_ge(S("post_act"), n + 1)
                    if n:
                        act.wait_ge(S("ns_pe"), 2 * n)
                    act.activation(SQ[:], t[:], ACT.Square).then_inc(S("sq_act"), 1)
                    for hf in (0, 1):
                        act.wait_ge(S("ns_pe"), 2 * n + hf + 1)
                        if n and hf == 0:
                            act.wait_ge(S("nrm_done"), n)
                        act.activation(rn[:, hf * HB:(hf + 1) * HB, :], PS[hf][:, 0:HALF].rearrange("p (b t) -> p b t", b=HB),
                                       ACT.Sqrt).then_inc(S("nr_act"), 1)

            silu_in(0, 0, PB)
            for hf in (0, 1):
                act.wait_ge(S("gate_pe"), hf + 1)
                act.activation(gT[:, hf * HB:(hf + 1) * HB, :], PS[2 + hf][0:32, 0:HALF].rearrange("p (b t) -> p b t", b=HB),
                               ACT.Sigmoid, bias=b_ab[:]).then_inc(S("gate_act"), 1)
            silu_in(1, 1, PB2)
            silu_out(0, kT, True)
            act.wait_ge(S("ga_done"), 1)
            act.activation(la[:], la[:], ACT.Ln).then_inc(S("la_done"), 1)
            act.wait_ge(S("cv_done"), KC)
            silu_in(2, 2, PB)
            silu_out(1, qT, True)
            silu_out(2, vT, False)
            for b in range(B):
                p = b % 2
                act.wait_ge(S("ld_pe"), b + 1)
                if b >= 2:
                    act.wait_ge(S(f"ed_out{p}"), 16 * (b // 2))
                for i in range(4):
                    last = act.activation(EB[p][:, 4 * i:4 * i + 4, :], PS[i][0:T, 0:4 * T].rearrange("p (h t) -> p h t", h=4), ACT.Exp)
                last.then_inc(S("ex_act"), 1)
                for n, dst in ((0, Kt), (1, Vt)):
                    act.wait_ge(S("kv_pe"), 2 * b + n + 1)
                    if b == 0:
                        act.wait_ge(S("qkv_done"), 1)
                    act.activation(dst[:, b, :], PS[4 + n][0:T, :], ACT.Copy).then_inc(S("kv_tok"), 1)
            for b0 in range(0, B, 2):
                two = [(b0 + p, p, PS[4 * p:4 * p + 4]) for p in (0, 1)]
                if b0 == 0:
                    act.wait_ge(S("md_out"), 32)
                for i, s0, w in BLK:
                    for b, p, bank in two:
                        act.wait_ge(S("u_pe"), 4 * b0 + 2 * i + p + 1)
                        if b0 and i == 0:
                            act.wait_ge(S("xy_done"), b - 1)
                        act.activation(UU[p][s0:s0 + w, :], bank[0][s0:s0 + w, :], ACT.Copy).then_inc(S("u_ev"), 1)

                def evacuated(pe_sem, bank, b, p, sem):
                    act.wait_ge(S(pe_sem), b + 1)
                    act.activation(TR[p][:], bank[:, 0:KC * T].rearrange("p (k t) -> p k t", k=KC), ACT.Copy).then_inc(S(sem), 1)

                for b, p, bank in two:
                    evacuated("ut_pe", bank[2], b, p, "ut_ev")
                for b, p, bank in two:
                    act.wait_ge(S("o_pe"), b + 1)
                    act.activation(RR[p][:], bank[0][0:T, :], ACT.Copy).then_inc(S("o_done"), 1)
                for b, p, bank in two:
                    evacuated("ot_pe", bank[1], b, p, "ot_ev")
                for b, p, bank in two:
                    act.wait_ge(S("mv_c"), 2 * b0 + p + 1)
                    act.activation(sd[:, b:b + 1], mv[:, b, 1:2], ACT.Sqrt, bias=eps_ln[0:T, :]).then_inc(S("sd_c"), 1)
                for b, p, bank in two:
                    evacuated("xh_pe", bank[3], b, p, "xh_ev")
                for b, p, bank in two:
                    act.wait_ge(S("sc_dve"), b + 1)
                    act.activation(PR[p][:], PR[p][:], ACT.Exp, bias=nmax[:, b:b + 1], accum_out=rsum[:, b:b + 1]).then_inc(S("pr_done"), 1)
                for b, p, bank in two:
                    act.wait_ge(S("pt_pe"), b + 1)
                    for j, s0, w in S2T:
                        last = act.activation(PT[p][0:w, j, :], bank[2 + j // 4][0:w, (j % 4) * T:(j % 4 + 1) * T], ACT.Copy)
                    last.then_inc(S("pt_ev"), 1)
                for b, p, bank in two:
                    act.wait_ge(S("mv_c"), 2 * b0 + p + 3)
                    act.activation(sd[:, b:b + 1], mv[:, b, 1:2], ACT.Sqrt, bias=eps_ln[0:T, :]).then_inc(S("sd_c"), 1)
                for b, p, bank in two:
                    act.wait_ge(S("y_norm"), b + 1)
                    own(act.activation(RR[p][:], UU[p][:], ACT.Square, accum_out=ss[:, b:b + 1]))
                    act.activation(ss[:, b:b + 1], ss[:, b:b + 1], ACT.Sqrt, bias=eps_rms[0:T, :], scale=1.0 / D).then_inc(S("ss_done"), 1)
                for b, p, bank in two:
                    evacuated("nt_pe", bank[1], b, p, "nt_ev")
                for b, p, bank in two:
                    act.wait_ge(S("lg_pe"), b + 1)
                    act.activation(LG[:, b, :], bank[2][0:T, 0:E], ACT.Copy).then_inc(S("lg_done"), 1)
            act.wait_ge(S("rt_sub"), 1)
            act.activation(rt_p[:], rt_p[:], ACT.Exp).then_inc(S("rt_exp"), 1)
            act.wait_ge(S("nt_set"), 1)
            act.sem_inc(S("ht_ev"), 2)
            with act.Fori(0, E // 2) as pair:
                for q in (0, 1):
                    nt = act.value_load(nti[0:1, 0, bass.ds(pair * 2 + q, 1)], min_val=1, max_val=MAXNT)
                    first = act.value_load(nti[0:1, 1, bass.ds(pair * 2 + q, 1)], min_val=0, max_val=NITEM - 2)
                    with act.Fori(0, nt) as tile:
                        chunk = act.snap((first + tile) * 4)

                        def hidden_evacuated(c):
                            o, w = CH[c]
                            act.wait_ge(S("ht_pe"), chunk + (c + 1))
                            act.activation(HT[:, o // P:(o + w) // P, :], PS[4 + c % 2][:, 0:w].rearrange("p (j t) -> p j t", t=P),
                                           ACT.Copy).then_inc(S("ht_ev"), 1)

                        for c, (o, w) in enumerate(CH):
                            act.wait_ge(S("gu_pe"), chunk + (c + 1))
                            act.activation(HS[:, o:o + w], PS[2 * (c % 2)][:, 0:w], ACT.Silu).then_inc(S("silu_done"), 1)
                            if c:
                                hidden_evacuated(c - 1)
                        hidden_evacuated(3)

        @block.vector
        def _(dve):
            own = Handoff(dve, S("dve_own"))
            tt, ts, stt = dve.tensor_tensor, dve.tensor_scalar, dve.scalar_tensor_tensor
            dve.memset(eps_ln[:], LN_EPS)
            dve.memset(eps_rms[:], RMS_EPS)
            dve.memset(zero_col[:], 0.0).then_inc(S("consts"), 1)
            dve.memset(ZR[:], 0.0).then_inc(S("zr_set"), 1)
            for buf in (PB, PB2):
                dve.memset(buf[:, :, :, 0:2], 0.0)
                last = dve.memset(buf[:, :, :, 2 + T:TP], 0.0)
            last.then_inc(S("pads"), 1)
            for b in range(B):
                dve.wait_ge(S(f"x_in{b}"), 16)
                last = dve.bn_stats(stats[:, b, :], X[:, b, :])
            own(last)
            for b in range(B):
                last = dve.bn_aggr(mv[:, b, :], stats[:, b, :])
            last.then_inc(S("mv_a"), 1)
            dve.wait_ge(S("sd_a"), 1)
            dve.wait_ge(S("mv_a"), 1)
            own(dve.reciprocal(rstd[:], rstd[:]))
            for b in range(B):
                ts(XN[:, b, :], X[:, b, :], mv[:, b, 0:1], rstd[:, b:b + 1], ALU.subtract, ALU.mult).then_inc(S("xn_a"), 1)

            def convolve(n, w, buf, t):
                for c in range(KC):
                    dve.wait_ge(S("pj_ev"), n * 8 + 2 * c + 2)
                    own(ts(t[:, c], buf[:, c, :, 0:T], w_conv[:, w, c, 0:1], None, ALU.mult))
                    for j in range(1, TAPS):
                        last = stt(t[:, c], buf[:, c, :, j:j + T], w_conv[:, w, c, j:j + 1], t[:, c], ALU.mult, ALU.add)
                        if j < TAPS - 1:
                            own(last)
                    last.then_inc(S("cv_done"), 1)

            def normalise(n, t):
                dve.wait_ge(S("nr_act"), 2 * n + 2)
                own(ts(rn[:], rn[:], L2_EPS, None, ALU.add))
                own(dve.reciprocal(rn[:], rn[:]))
                for c in range(KC):
                    last = tt(t[:, c], t[:, c], rn[:], ALU.mult)
                last.then_inc(S("nrm_done"), 1)

            dve.wait_ge(S("small_in"), 16 * 4)
            convolve(0, 0, PB, kT)
            dve.wait_ge(S("gtok_pe"), 1)
            own(dve.tensor_copy(gtok[:], PS[2][0:T, 0:B * 32].rearrange("t (b g) -> t b g", b=B)))
            ts(la[:], gtok[:, :, 0:H], LEAST_DECAY, None, ALU.max).then_inc(S("ga_done"), 1)
            convolve(1, 1, PB2, qT)
            dve.wait_ge(S("post_act"), 1)
            normalise(0, kT)
            convolve(2, 2, PB, vT)
            normalise(1, qT)
            dve.wait_ge(S("post_act"), 3)
            dve.wait_ge(S("nrm_done"), 2)
            dve.sem_inc(S("qkv_done"), 1)
            for b in range(B):
                p = b % 2
                dve.wait_ge(S("ex_act"), b + 1)
                dve.wait_ge(S("mb_done"), b + 1)
                tt(EB[p][:], EB[p][:], MB[p][:], ALU.mult).then_inc(S("e_done"), 1)
                dve.wait_ge(S("g_pe"), b + 1)
                dve.wait_ge(S("e_done"), b + 1)
                if b >= 2:
                    dve.wait_ge(S(f"bd_out{p}"), 16 * (b // 2))
                for i in range(4):
                    last = tt(BB[p][:, 4 * i:4 * i + 4, :], PS[4 + i][0:T, 0:4 * T].rearrange("p (h t) -> p h t", h=4),
                              EB[p][:, 4 * i:4 * i + 4, :], ALU.mult)
                last.then_inc(S("bb_done"), 1)
            dve.wait_ge(S("bb_done"), B)
            dve.wait_ge(S("kv_tok"), 2 * B)
            dve.wait_ge(S("g_pe"), B)
            dve.wait_ge(S("ed_out0"), 16 * B // 2)
            dve.wait_ge(S("ed_out1"), 16 * B // 2)
            dve.wait_ge(S("bd_out0"), 16 * B // 2)
            dve.wait_ge(S("bd_out1"), 16 * B // 2)
            dve.memset(MI[:], 0.0)
            own(dve.memset(MI3[:], 0.0))
            dve.memset(MI[:].rearrange("p i r s -> p i (r s)")[:, :, ::33], 1.0)
            own(dve.memset(MI3[:].rearrange("p r s -> p (r s)")[:, ::LAST + 1], 1.0))
            dve.wait_ge(S("dg_in"), 16 * 4 * B)
            for s in range(1, 32):
                tm = TM[:, 0:3 * s * s].rearrange("p (i a r) -> p i a r", i=3, a=s)
                own(tt(tm, MI[:, :, 0:s, 0:s], DG[:, :, 0:s, s].unsqueeze(2).broadcast_to([P, 3, s, s]), ALU.mult))
                last = dve.tensor_reduce(MI[:, :, 0:s, s], tm, AX_X, ALU.add, negate=True)
                own(last)
            for s in range(1, LAST):
                tm = TM[:, 0:s * s].rearrange("p (a r) -> p a r", a=s)
                own(tt(tm, MI3[:, 0:s, 0:s], DG3[:, 0:s, s].unsqueeze(1).broadcast_to([P, s, s]), ALU.mult))
                own(dve.tensor_reduce(MI3[:, 0:s, s], tm, AX_X, ALU.add, negate=True))
            dve.sem_inc(S("mi_done"), 1)
            dve.wait_ge(S("md_out"), 32)
            dve.wait_ge(S("cw_in"), 48)
            for b0 in range(0, B, 2):
                two = [(b0 + p, p, PS[4 * p:4 * p + 4]) for p in (0, 1)]
                for i, s0, w in BLK[1:]:
                    for b, p, bank in two:
                        dve.wait_ge(S("acc_pe"), 3 * b0 + 2 * (i - 1) + p + 1)
                        tt(RR[p][s0:s0 + w, :], Vt[s0:s0 + w, b, :], bank[1][s0:s0 + w, :], ALU.subtract).then_inc(S("r_done"), 1)
                for b, p, bank in two:
                    dve.wait_ge(S("w_pe"), b + 1)
                    dve.wait_ge(S(f"ee_in{p}"), 16 * (b // 2 + 1))
                    for g in range(4):
                        last = tt(BC[p][:, 4 * g:4 * g + 4, :], bank[g][0:T, 0:4 * T].rearrange("p (h t) -> p h t", h=4),
                                  EE[p][:, 4 * g:4 * g + 4, :], ALU.mult)
                    last.then_inc(S("wm_done"), 1)

                def layer_norm(b, p):
                    own(dve.bn_stats(stats[:, b, :], X[:, b, :]))
                    dve.bn_aggr(mv[:, b, :], stats[:, b, :]).then_inc(S("mv_c"), 1)

                def normed(b, p, n, sem):
                    dve.wait_ge(S("sd_c"), 2 * b0 + 2 * n + p + 1)
                    dve.wait_ge(S("mv_c"), 2 * b0 + 2 * n + p + 1)
                    own(dve.reciprocal(rstd[:, b:b + 1], sd[:, b:b + 1]))
                    ts(UU[p][:], X[:, b, :], mv[:, b, 0:1], rstd[:, b:b + 1], ALU.subtract, ALU.mult).then_inc(S(sem), 1)

                for b, p, bank in two:
                    dve.wait_ge(S("wo_pe"), b + 1)
                    dve.wait_ge(S("xb_done"), b + 1)
                    own(tt(X[:, b, :], X[:, b, :], bank[2][0:T, :], ALU.add))
                    layer_norm(b, p)
                for b, p, bank in two:
                    normed(b, p, 0, "xh_done")
                for b, p, bank in two:
                    dve.wait_ge(S("sc_pe"), b + 1)
                    dve.wait_ge(S("mn_done"), b + 1)
                    for hf in (0, 1):
                        last = stt(PR[p][:, hf * S2H:(hf + 1) * S2H], bank[hf][0:T, 0:S2H], SCALE, MN[p][:, hf * S2H:(hf + 1) * S2H],
                                   ALU.mult, ALU.add)
                    own(last)
                    dve.tensor_reduce(nmax[:, b:b + 1], PR[p][:], AX_X, ALU.max, negate=True).then_inc(S("sc_dve"), 1)
                for b, p, bank in two:
                    dve.wait_ge(S("pv_pe"), b + 1)
                    own(dve.reciprocal(rsum[:, b:b + 1], rsum[:, b:b + 1]))
                    own(stt(X[:, b, :], bank[0][0:T, :], rsum[:, b:b + 1], X[:, b, :], ALU.mult, ALU.add))
                    layer_norm(b, p)
                for b, p, bank in two:
                    normed(b, p, 1, "y_norm")
                for b, p, bank in two:
                    dve.wait_ge(S("ss_done"), b + 1)
                    dve.wait_ge(S("y_norm"), b + 1)
                    own(dve.reciprocal(ss[:, b:b + 1], ss[:, b:b + 1]))
                    stt(XN[:, b, :], UU[p][:], ss[:, b:b + 1], nw_b[:], ALU.mult, ALU.mult).then_inc(S("xn_all"), 1)

            def bc(col):
                return col.unsqueeze(2).broadcast_to([T, B, E])

            dve.wait_ge(S("lg_done"), B)
            dve.wait_ge(S("iota_e"), 1)
            own(dve.tensor_reduce(rt_m[:, :, 0], LG[:], AX_X, ALU.max))
            tt(rt_p[:], LG[:], bc(rt_m[:, :, 0]), ALU.subtract).then_inc(S("rt_sub"), 1)
            dve.wait_ge(S("rt_exp"), 1)
            own(dve.tensor_reduce(rt_m[:, :, 6], rt_p[:], AX_X, ALU.add))
            own(dve.reciprocal(rt_m[:, :, 6], rt_m[:, :, 6]))
            own(tt(rt_p[:], rt_p[:], bc(rt_m[:, :, 6]), ALU.mult))
            for c, oh in ((0, rt_o0), (1, rt_o1)):
                own(dve.tensor_reduce(rt_m[:, :, 2 * c], rt_p[:], AX_X, ALU.max))
                own(tt(rt_t[:], rt_p[:], bc(rt_m[:, :, 2 * c]), ALU.is_lt))
                own(stt(rt_t[:], rt_t[:], 100.0, rt_io[:], ALU.mult, ALU.add))
                own(dve.tensor_reduce(rt_m[:, :, 2 * c + 1], rt_t[:], AX_X, ALU.min))
                own(tt(oh[:], rt_io[:], bc(rt_m[:, :, 2 * c + 1]), ALU.is_equal))
                if c == 0:
                    own(stt(rt_p[:], oh[:], -2.0, rt_p[:], ALU.mult, ALU.add))
            tt(rt_eq[:], rt_o0[:], rt_o1[:], ALU.add).then_inc(S("sel_done"), 1)
            own(tt(rt_m[:, :, 6], rt_m[:, :, 0], rt_m[:, :, 2], ALU.add))
            own(dve.reciprocal(rt_m[:, :, 6], rt_m[:, :, 6]))
            dve.wait_ge(S("al_in"), 16)
            own(ts(al[:], al[:], -0.5, 2.0, ALU.max, ALU.min))
            own(ts(rt_m[:, :, 6], rt_m[:, :, 6], al[:], None, ALU.mult))
            for c in (0, 1):
                last = tt(wa[:, c, :], rt_m[:, :, 2 * c], rt_m[:, :, 6], ALU.mult)
            own(last)
            dve.wait_ge(S("cnt_pe"), 1)
            own(dve.memset(rt_boff[:, 0, :], 0.0))
            for b in range(B):
                own(tt(rt_boff[:, b + 1, :], rt_boff[:, b, :], PS[1][0:T, b * E:(b + 1) * E], ALU.add))
            own(dve.memset(rt_nt[:], 1.0))
            for m in range(1, MAXNT):
                own(stt(rt_nt[:], rt_boff[:, B, :], float(P * m), rt_nt[:], ALU.is_gt, ALU.add))
            own(dve.memset(rt_bs[:, 0:1], 0.0))
            for e in range(E):
                own(tt(rt_bs[:, e + 1:e + 2], rt_bs[:, e:e + 1], rt_nt[:, e:e + 1], ALU.add))
            dve.tensor_copy(nti[:, 0, :], rt_nt[:])
            dve.tensor_copy(nti[:, 1, :], rt_bs[:, 0:E]).then_inc(S("nt_set"), 1)
            own(tt(rt_pos[:], PS[0][0:T, 0:B * E].rearrange("t (b e) -> t b e", b=B), rt_boff[:, 0:B, :], ALU.add))
            own(stt(rt_pos[:], rt_bs[:, 0:E].unsqueeze(1).broadcast_to([T, B, E]), float(P), rt_pos[:], ALU.mult, ALU.add))
            for c, oh in ((0, rt_o0), (1, rt_o1)):
                own(tt(rt_t[:], rt_pos[:], oh[:], ALU.mult))
                own(dve.tensor_reduce(gf[:, c, :], rt_t[:], AX_X, ALU.add))
            dve.tensor_copy(gi[:], gf[:]).then_inc(S("gi_set"), 1)

            dve.sem_inc(S("h_done"), 2)
            dve.sem_inc(S("y_ev"), 1)
            dve.sem_inc(S("y_stored"), 16)

            def tile_evacuated(n):
                dve.wait_ge(S("xg_tr"), n)
                dve.tensor_copy(XGT[:], PS[6][:, :].rearrange("p (k t) -> p k t", k=KC)).then_inc(S("xt_done"), 1)

            tile_evacuated(1)
            dve.wait_ge(S("nt_set"), 1)
            with dve.Fori(0, E // 2) as pair:
                for q in (0, 1):
                    nt = dve.value_load(nti[0:1, 0, bass.ds(pair * 2 + q, 1)], min_val=1, max_val=MAXNT)
                    first = dve.value_load(nti[0:1, 1, bass.ds(pair * 2 + q, 1)], min_val=0, max_val=NITEM - 2)
                    with dve.Fori(0, nt) as tile:
                        item = dve.snap(first + tile, min_val=0, max_val=NITEM - 2)
                        for c, (o, w) in enumerate(CH):
                            dve.wait_ge(S("silu_done"), item * 4 + (c + 1))
                            tt(HH[:, o:o + w], HS[:, o:o + w], PS[2 * (c % 2) + 1][:, 0:w], ALU.mult).then_inc(S("h_done"), 1)
                        tile_evacuated(item + 2)
                        dve.wait_ge(S("y_pe"), item + 1)
                        dve.wait_ge(S("y_stored"), (item + 1) * 16)
                        dve.tensor_copy(YS[:], PS[7][:, :])\
                            .then_inc(S("y_ev"), 1)
                        dve.wait_ge(S("y_ev"), item + 2)
                        dve.sem_inc(S("y_out"), 1)
                    last_item = dve.snap(first + nt)
            dve.wait_ge(S("xy_done"), B)
            dve.wait_ge(S("y_stored"), (last_item + 1) * 16)
            dve.sem_inc(S("moe_end"), 1)
            for b in range(B):
                dve.wait_ge(S(f"yg_in{b % 2}"), 32 * (b // 2 + 1))
                own(stt(X[:, b, :], YG[:, 0, b, :], wa[:, 0, b:b + 1], X[:, b, :], ALU.mult, ALU.add))
                stt(X[:, b, :], YG[:, 1, b, :], wa[:, 1, b:b + 1], X[:, b, :], ALU.mult, ALU.add).then_inc(S("fin"), 1)


def kernel(x, ctx_1024, mask_Bx1xS2_fk0, L0_attn_Wq, L0_attn_bq, L0_attn_Wk, L0_attn_bk, L0_attn_Wv, L0_attn_bv,
           L0_attn_Wa, L0_attn_ba, L0_attn_Wb, L0_attn_bb, L0_attn_conv_q, L0_attn_conv_k, L0_attn_conv_v, L0_attn_Wo,
           L0_attn_bo, L0_ffn_norm_weight, L0_ffn_router_weight, L0_ffn_gate_up_weight, L0_ffn_down_weight,
           L0_ffn_residual_alpha):
    import numpy as np
    import concourse.bacc as bacc
    from concourse.bass_utils import run_bass_kernel_spmd

    c = np.ascontiguousarray
    D, H, P = 512, 16, 128
    heads = [4 * (j % 4) + j // 4 for j in range(H)]
    arrays = {
        "x": c(x), "ctx": c(ctx_1024), "ctxT": c(np.transpose(np.asarray(ctx_1024), (0, 2, 1))), "mask": c(mask_Bx1xS2_fk0),
        "WqT": c(np.asarray(L0_attn_Wq).T), "WkT": c(np.asarray(L0_attn_Wk).T), "WvT": c(np.asarray(L0_attn_Wv).T),
        "bqkv": c(np.stack([np.asarray(v).reshape(D // P, P).T for v in (L0_attn_bk, L0_attn_bq, L0_attn_bv)], 1)),
        "WabT": c(np.concatenate([np.asarray(L0_attn_Wa)[heads], np.asarray(L0_attn_Wb)[heads]], 0).T),
        "bab": c(np.concatenate([np.asarray(L0_attn_ba)[heads], np.asarray(L0_attn_bb)[heads]])[:, None]),
        "conv": c(np.stack([np.asarray(v).reshape(D // P, P, 4).transpose(1, 0, 2)
                            for v in (L0_attn_conv_k, L0_attn_conv_q, L0_attn_conv_v)], 1)),
        "WoT": c(np.asarray(L0_attn_Wo).T), "bo": c(L0_attn_bo), "norm_w": c(L0_ffn_norm_weight),
        "WrT": c(np.asarray(L0_ffn_router_weight).T),
        "GU": c(np.asarray(L0_ffn_gate_up_weight).transpose(0, 2, 1).reshape(8, D // P, P, -1).transpose(0, 2, 1, 3)),
        "DN": c(np.asarray(L0_ffn_down_weight).transpose(0, 2, 1).reshape(8, -1, P, D).transpose(0, 2, 1, 3)),
        "alpha": c(np.asarray(L0_ffn_residual_alpha).reshape(1)),
    }
    nc = bacc.Bacc("TRN2", target_bir_lowering=False, num_devices=1)
    args = [nc.dram_tensor(f"in_{n}", a.shape, mybir.dt.from_np(a.dtype), kind="ExternalInput").ap() for n, a in arrays.items()]
    out = nc.dram_tensor("out", (8, 100, D), F32, kind="ExternalOutput").ap()
    decoder_layer(nc, *args, out)
    r = run_bass_kernel_spmd(nc, [{f"in_{n}": a for n, a in arrays.items()}], core_ids=[0])
    return r.results[0]["out"]
```

```python
from contextlib import ExitStack

import concourse.bass as bass
from concourse import mybir

ALU = mybir.AluOpType
ACT = mybir.ActivationFunctionType
F32 = mybir.dt.float32
I32 = mybir.dt.int32
F32R = mybir.dt.float32r
AX_X = mybir.AxisListType.X

P = 128
NEG = -1.0e9


class Handoff:

    def __init__(self, eng, sem):
        self.eng, self.sem, self.n = eng, sem, 0

    def __call__(self, ins):
        self.n += 1
        ins.then_inc(self.sem, 1)
        self.eng.wait_ge(self.sem, self.n)


def decoder_layer(nc, x, ctx, ctxT, mask, WqT, WkT, WvT, bqkv, WabT, bab, conv, WoT, bo, norm_w, WrT, GU, DN, alpha, out):
    B, T, D = x.shape
    S2 = ctx.shape[1]
    H, DH = 16, 32
    KC = D // P
    NTOK = B * T
    HALF = NTOK // 2
    HB = B // 2
    TAPS = 4
    TP = T + TAPS - 1
    BLK = [(i, 32 * i, min(32, T - 32 * i)) for i in range(4)]
    LAST = BLK[3][2]
    S2H = S2 // 2
    S2T = [(j, P * j, min(P, S2 - P * j)) for j in range(-(-S2 // P))]
    E, HID = DN.shape[0], DN.shape[2] * P
    HC = HID // P
    CH = [(0, 384), (384, 384), (768, 384), (1152, 256)]
    MAXNT = -(-NTOK // P)
    NITEM = (2 * NTOK + E * (P - 1)) // P + 1
    ZPARTS = 7
    PIECES, SLOTS = 12, 4
    LN_EPS, RMS_EPS, L2_EPS = 1e-5, 1e-6, 1e-6
    SCALE = float(D) ** -0.5
    LEAST_DECAY = 2.0 ** -63

    with ExitStack() as stack:
        sems = {}

        def S(name):
            if name not in sems:
                sems[name] = stack.enter_context(nc.semaphore(name))
            return sems[name]

        base = [16512]

        def at(name, shape, offset, dt=F32):
            return nc.alloc_sbuf_tensor_at(name, list(shape), dt, offset=offset)

        def size(shape):
            n = 4
            for s in shape[1:]:
                n *= s
            return -(-n // 32) * 32

        def place(cursor, name, shape, dt=F32):
            t = at(name, shape, cursor[0], dt)
            cursor[0] += size(shape)
            assert cursor[0] <= 229368, (name, cursor[0])
            return t

        X = place(base, "X", [T, B, D])
        ident = place(base, "ident", [P, P])
        later = place(base, "later", [P, P])
        upto = place(base, "upto", [P, P])
        before = place(base, "before", [P, P])
        ones = place(base, "ones", [P, P])
        eps_ln = place(base, "eps_ln", [P, 1])
        eps_rms = place(base, "eps_rms", [P, 1])
        zero_col = place(base, "zero_col", [P, 1])
        stats = place(base, "stats", [T, B, 6])
        mv = place(base, "mv", [T, B, 2])
        rstd = place(base, "rstd", [T, B])
        gtok = place(base, "gtok", [T, B, 32])
        la = place(base, "la", [T, B, H])
        sd = place(base, "sd", [T, B])
        nmax = place(base, "nmax", [T, B])
        rsum = place(base, "rsum", [T, B])
        ss = place(base, "ss", [T, B])
        LG = place(base, "LG", [T, B, E])
        r_names = "rt_p rt_eq rt_io rt_o0 rt_o1 rt_t rt_pos".split()
        rt_p, rt_eq, rt_io, rt_o0, rt_o1, rt_t, rt_pos = [place(base, n, [T, B, E]) for n in r_names]
        rt_m = place(base, "rt_m", [T, B, 8])
        rt_boff = place(base, "rt_boff", [T, B + 1, E])
        rt_nt = place(base, "rt_nt", [T, E])
        rt_bs = place(base, "rt_bs", [T, E + 1])
        gf = place(base, "gf", [T, 2, B])
        gi = place(base, "gi", [T, 2, B], I32)
        nti = place(base, "nti", [T, 2, E], I32)
        al = place(base, "al", [T, 1])
        wa = place(base, "wa", [T, 2, B])
        XN = place(base, "XN", [T, B, D])
        later_phases = base[0]

        cur = [later_phases]
        qT = place(cur, "qT", [P, KC, B, T])
        Wo = place(cur, "Wo", [P, KC, D])
        Kt = place(cur, "Kt", [T, B, D])
        Vt = place(cur, "Vt", [T, B, D])
        after_b = cur[0]
        kT = place(cur, "kT", [P, KC, B, T])
        vT = place(cur, "vT", [P, KC, B, T])
        b_only = cur[0]
        W3 = [place(cur, f"W_{n}", [P, KC, D]) for n in "kqv"]
        xT = place(cur, "xT", [P, KC, B, T])
        PB = place(cur, "PB", [P, KC, B, TP])
        PB2 = at("PB2", [P, KC, B, TP], after_b - 2 * size([T, B, D]))
        SQ = at("SQ", [P, KC, B, T], after_b - size([T, B, D]))
        rn = place(cur, "rn", [P, B, T])
        gT = place(cur, "gT", [32, B, T])
        Wab = place(cur, "Wab", [P, KC, 32])
        b_ab = place(cur, "b_ab", [32, 1])
        b_qkv = place(cur, "b_qkv", [P, 3, KC])
        w_conv = place(cur, "w_conv", [P, 3, KC, TAPS])
        ZR = place(cur, "ZR", [P, NITEM * D // ZPARTS])
        cur = [b_only]
        LR = [place(cur, f"LR{p}", [T, H, T]) for p in (0, 1)]
        MB = [place(cur, f"MB{p}", [T, H, T]) for p in (0, 1)]
        EB = [place(cur, f"EB{p}", [T, H, T]) for p in (0, 1)]
        BB = [place(cur, f"BB{p}", [T, H * T]) for p in (0, 1)]
        cur = [after_b]
        DG = place(cur, "DG", [P, 3, 32, 32])
        MI = place(cur, "MI", [P, 3, 32, 32])
        DG3 = place(cur, "DG3", [P, LAST, LAST])
        MI3 = place(cur, "MI3", [P, LAST, LAST])
        TM = place(cur, "TM", [P, 3 * 32 * 32])
        cur = [after_b]
        bo_b = place(cur, "bo_b", [T, D])
        nw_b = place(cur, "nw_b", [T, D])
        Wr = place(cur, "Wr", [P, KC, E])
        EE = [place(cur, f"EE{p}", [T, H, T]) for p in (0, 1)]
        BC = [place(cur, f"BC{p}", [T, H * T]) for p in (0, 1)]
        WM = [BC[p][:].rearrange("t (h s) -> t h s", h=H) for p in (0, 1)]
        MT = [place(cur, f"MT{p}", [T, H, 32]) for p in (0, 1)]
        UU = [place(cur, f"UU{p}", [T, D]) for p in (0, 1)]
        RR = [place(cur, f"RR{p}", [T, D]) for p in (0, 1)]
        TR = [place(cur, f"TR{p}", [P, KC, T]) for p in (0, 1)]
        CT = [place(cur, f"CT{p}", [P, KC, S2]) for p in (0, 1)]
        CN = place(cur, "CN", [P, len(S2T), D])
        MN = [place(cur, f"MN{p}", [T, S2]) for p in (0, 1)]
        PR = [place(cur, f"PR{p}", [T, S2]) for p in (0, 1)]
        PT = [place(cur, f"PT{p}", [P, len(S2T), T]) for p in (0, 1)]
        cur = [later_phases]
        GWH = place(cur, "GWH", [P, KC, 2 * HID], F32R)
        GWL = place(cur, "GWL", [P, KC, 2 * HID], F32R)
        DWH = place(cur, "DWH", [P, HC, D], F32R)
        DWL = place(cur, "DWL", [P, HC, D], F32R)
        ST = [place(cur, f"ST{n}", [P, 4 * 384]) for n in range(SLOTS)]
        XG = place(cur, "XG", [P, D])
        HH = [place(cur, f"HH{n}", [P, 384]) for n in (0, 1)]
        YS = place(cur, "YS", [P, D])
        YG = at("YG", [T, 2, B, D], later_phases)
        cur = [later_phases - size([T, B, D])]
        XTH = place(cur, "XTH", [P, KC, P], F32R)
        XTL = place(cur, "XTL", [P, KC, P], F32R)
        HTH = place(cur, "HTH", [P, HC, P], F32R)
        HTL = place(cur, "HTL", [P, HC, P], F32R)
        assert cur[0] <= later_phases

        DOWN = [(1, range(0, 3)), (2, range(3, 6)), (3, range(6, 9)), (4, range(9, HC))]
        ORDER = [("w", 0), ("w", 1), ("w", 2), ("w", 3), ("y", 0), ("w", 4), ("h", 0), ("w", 5), ("w", 6), ("h", 1), ("t", 0),
                 ("w", 7), ("w", 8), ("h", 2), ("t", 1), ("w", 9), ("h", 3), ("t", 2), ("x", 0), ("w", 10), ("t", 3), ("w", 11)]

        def piece(n):
            if n < 8:
                o, w = CH[n // 2]
                o += HID * (n % 2)
                return ST[n % SLOTS][:, 0:KC * w].rearrange("p (k w) -> p k w", k=KC), GWH[:, :, o:o + w], GWL[:, :, o:o + w]
            j = 3 * (n - 8)
            m = min(3, HC - j)
            return ST[n % SLOTS][:, 0:m * D].rearrange("p (j d) -> p j d", j=m), DWH[:, j:j + m, :], DWL[:, j:j + m, :]

        PS = [stack.enter_context(nc.psum_tensor(f"PS{i}", [P, 512], F32)) for i in range(8)]

        def dram(name, shape, dt=F32):
            return nc.dram_tensor(name, list(shape), dt, kind="Internal").ap()

        Ed = dram("Ed", [B, T, H, T])
        Bd = dram("Bd", [B, T, H * T])
        Md = dram("Md", [B * H, 3, 32, 32])
        Md3 = dram("Md3", [B * H, LAST, LAST])
        XGd = dram("XGd", [NITEM * P, D])
        YGd = dram("YGd", [NITEM * P, D])

        def diag_cols(rows, i):
            if i < 3:
                return rows[:, i * H * 32:(i + 1) * H * 32].rearrange("r (h s) -> r h s", h=H)
            return rows[:, 3 * H * 32:].rearrange("r (h s) -> r h s", h=H)

        block = stack.enter_context(nc.Block())

        @block.sync
        def _(sp):
            for b in range(B):
                sp.dma_start(X[:, b, :], x[b]).then_inc(S(f"x_in{b}"), 16)
            sp.dma_start(W3[0][:], WkT.rearrange("(k p) n -> p k n", p=P)).then_inc(S("wk_in"), 16)
            sp.dma_start(W3[2][:], WvT.rearrange("(k p) n -> p k n", p=P)).then_inc(S("wv_in"), 16)
            sp.dma_start(W3[1][:], WqT.rearrange("(k p) n -> p k n", p=P)).then_inc(S("wq_in"), 16)
            sp.dma_start(Wo[:], WoT.rearrange("(k p) n -> p k n", p=P)).then_inc(S("wo_in"), 16)
            sp.wait_ge(S("zr_set"), 1)
            for j in range(ZPARTS):
                n = NITEM * P // ZPARTS
                for rows in (XGd, YGd):
                    sp.dma_start(rows[j * n:(j + 1) * n, :].rearrange("(p r) d -> p (r d)", p=P), ZR[:, :]).then_inc(S("rows_zero"), 16)
            for b in range(B):
                p = b % 2
                sp.wait_ge(S("e_done"), b + 1)
                sp.dma_start(Ed[b], EB[p][:]).then_inc(S(f"ed_out{p}"), 16)
                sp.wait_ge(S("bb_done"), b + 1)
                sp.dma_start(Bd[b], BB[p][:]).then_inc(S(f"bd_out{p}"), 16)
            sp.wait_ge(S("bb_done"), B)
            sp.wait_ge(S("kv_tok"), 2 * B)
            for p in (0, 1):
                sp.wait_ge(S(f"ed_out{p}"), 16 * B // 2)
                sp.wait_ge(S(f"bd_out{p}"), 16 * B // 2)
            for b in range(B):
                for i, s0, w in BLK:
                    src = diag_cols(Bd[b], i)[s0:s0 + w].rearrange("r h s -> h r s")
                    dst = DG[b * H:(b + 1) * H, i] if i < 3 else DG3[b * H:(b + 1) * H]
                    sp.dma_start(dst, src).then_inc(S("dg_in"), 16)
            sp.wait_ge(S("mi_done"), 1)
            sp.dma_start(Md[:], MI[:]).then_inc(S("md_out"), 16)
            sp.dma_start(Md3[:], MI3[:]).then_inc(S("md_out"), 16)
            sp.wait_ge(S("md_out"), 32)
            sp.dma_start(bo_b[:], bo.partition_broadcast(T)).then_inc(S("cw_in"), 16)
            sp.dma_start(nw_b[:], norm_w.partition_broadcast(T)).then_inc(S("cw_in"), 16)
            sp.dma_start(al[:], alpha.partition_broadcast(T)).then_inc(S("al_in"), 16)
            sp.dma_start(Wr[:], WrT.rearrange("(k p) n -> p k n", p=P)).then_inc(S("cw_in"), 16)
            for b in range(B):
                p = b % 2
                if b >= 2:
                    sp.wait_ge(S("o_done"), b - 1)
                for i, s0, w in BLK:
                    m = Md[b * H:(b + 1) * H, i] if i < 3 else Md3[b * H:(b + 1) * H]
                    sp.dma_start(MT[p][s0:s0 + w, :, 0:w], m.rearrange("h r s -> r h s")).then_inc(S(f"mt_in{p}"), 16)
                sp.dma_start(BC[p][:], Bd[b]).then_inc(S(f"bc_in{p}"), 16)
                sp.dma_start(EE[p][:], Ed[b]).then_inc(S(f"ee_in{p}"), 16)
                if b >= 2:
                    sp.wait_ge(S("sc_pe"), b - 1)
                    sp.wait_ge(S("sc_dve"), b - 1)
                sp.dma_start(CT[p][:], ctxT[b].rearrange("(k p) s -> p k s", p=P)).then_inc(S(f"ct_in{p}"), 16)
                sp.dma_start(MN[p][:], mask[b].partition_broadcast(T).rearrange("t o s -> t (o s)")).then_inc(S(f"mn_in{p}"), 16)
                if b >= 1:
                    sp.wait_ge(S("pv_pe"), b)
                full = S2T[-1][0]
                sp.dma_start(CN[:, 0:full, :], ctx[b][0:full * P, :].rearrange("(j p) d -> p j d", p=P)).then_inc(S("cn_in"), 16)
                sp.dma_start(CN[0:S2 - full * P, full, :], ctx[b][full * P:S2, :]).then_inc(S("cn_in"), 16)

            sp.wait_ge(S("xn_all"), B)
            sp.wait_ge(S("xy_done"), B)
            sp.wait_ge(S("lg_done"), B)
            with sp.Fori(0, E) as e:
                for n in range(PIECES):
                    raw = piece(n)[0]
                    if n < 8:
                        o, w = CH[n // 2]
                        o += HID * (n % 2)
                        src = GU[bass.ds(e, 1), :, :, o:o + w].rearrange("o p k n -> p (o k) n")
                    else:
                        src = DN[bass.ds(e, 1), :, 3 * (n - 8):min(3 * (n - 7), HC), :].rearrange("o p k n -> p (o k) n")
                    sp.wait_ge(S("lo_done"), e * PIECES + (n + 1))
                    sp.dma_start(raw, src).then_inc(S(f"w_in{n % SLOTS}"), 16)
            for b in range(B):
                sp.wait_ge(S("fin"), b + 1)
                sp.dma_start(out[b], X[:, b, :]).then_inc(S("out_st"), 16)
            sp.wait_ge(S("out_st"), 16 * B)

        @block.gpsimd
        def _(pool):
            own = Handoff(pool, S("pool_own"))
            for t, v in ((ident, 0.0), (later, 0.0), (upto, 0.0), (before, 0.0)):
                last = pool.memset(t[:], v)
            own(last)
            for t, sign, op in ((ident, 1, ALU.not_equal), (later, -1, ALU.is_ge), (upto, 1, ALU.is_gt), (before, 1, ALU.is_ge)):
                pool.affine_select(out=t[:], in_=t[:], compare_op=op, fill=1.0, base=0, pattern=[[-sign, P]],
                                   channel_multiplier=sign).then_inc(S("masks"), 1)
            pool.memset(ones[:], 1.0).then_inc(S("masks"), 1)
            pool.iota(rt_io[:], [[0, B], [1, E]], base=0, channel_multiplier=0,
                      allow_small_or_imprecise_dtypes=True).then_inc(S("iota_e"), 1)
            pool.wait_ge(S("la_done"), 1)
            pool.wait_ge(S("masks"), 5)
            pool.wait_ge(S("qkv_done"), 1)
            for b in range(B):
                p = b % 2
                if b >= 2:
                    pool.wait_ge(S("ld_pe"), b - 1)
                pool.tensor_tensor(LR[p][:], la[:, b, :].unsqueeze(2).broadcast_to([T, H, T]),
                                   upto[0:T, 0:T].unsqueeze(1).broadcast_to([T, H, T]), ALU.mult).then_inc(S("lr_done"), 1)
                if b >= 2:
                    pool.wait_ge(S("e_done"), b - 1)
                pool.tensor_tensor(MB[p][:], gtok[:, b, H:].unsqueeze(2).broadcast_to([T, H, T]),
                                   upto[0:T, 0:T].unsqueeze(1).broadcast_to([T, H, T]), ALU.mult).then_inc(S("mb_done"), 1)
            pool.wait_ge(S("cw_in"), 48)
            for b in range(B):
                pool.tensor_tensor(X[:, b, :], X[:, b, :], bo_b[:], ALU.add).then_inc(S("xb_done"), 1)
            for b0 in range(0, B, 2):
                for b, p in ((b0, 0), (b0 + 1, 1)):
                    pool.wait_ge(S(f"mn_in{p}"), 16 * (b // 2 + 1))
                    pool.tensor_scalar(MN[p][:], MN[p][:], NEG, None, ALU.mult).then_inc(S("mn_done"), 1)
                for b, p in ((b0, 0), (b0 + 1, 1)):
                    pool.wait_ge(S("y_norm"), b + 1)
                    pool.tensor_tensor(X[:, b, :], X[:, b, :], UU[p][:], ALU.add).then_inc(S("xy_done"), 1)
            pool.wait_ge(S("rows_zero"), 16 * 2 * ZPARTS)
            pool.wait_ge(S("xn_all"), B)
            pool.wait_ge(S("gi_set"), 1)
            for c in (0, 1):
                for b in range(B):
                    pool.indirect_dma_start(XGd[:, :], bass.IndirectOffsetOnAxis(gi[:, c, b:b + 1], 0), XN[:, b, :], None)\
                        .then_inc(S("xg_scat"), 16)
            pool.wait_ge(S("xg_scat"), 16 * 2 * B)
            pool.dma_start(XG[:], XGd[0:P, :]).then_inc(S("xg_in"), 16)
            pool.wait_ge(S("nt_set"), 1)
            with pool.Fori(0, E) as e:
                nt = pool.value_load(nti[0:1, 0, bass.ds(e, 1)], min_val=1, max_val=MAXNT)
                first = pool.value_load(nti[0:1, 1, bass.ds(e, 1)], min_val=0, max_val=NITEM - 2)
                with pool.Fori(0, nt) as tile:
                    item = nc.s_assert_within(pool.snap(first + tile), 0, NITEM - 2)
                    pool.wait_ge(S("xg_tr"), item + 1)
                    pool.sem_inc(S("pool_io"), 1)
                    pool.dma_start(XG[:], XGd[bass.ds((item + 1) * P, P), :]).then_inc(S("xg_in"), 16)
                    pool.wait_ge(S("y_ev"), item + 2)
                    pool.sem_inc(S("pool_io"), 1)
                    pool.dma_start(YGd[bass.ds(item * P, P), :], YS[:]).then_inc(S("y_stored"), 16)
                    pool.wait_ge(S("y_stored"), item * 16 + 16)
                    pool.sem_inc(S("y_free"), 1)
            pool.wait_ge(S("moe_end"), 1)
            for b in range(B):
                for c in (0, 1):
                    pool.indirect_dma_start(YG[:, c, b, :], None, YGd[:, :], bass.IndirectOffsetOnAxis(gi[:, c, b:b + 1], 0))\
                        .then_inc(S(f"yg_in{b % 2}"), 16)
                if b % 2:
                    pool.wait_ge(S("yg_in0"), 16 * 2 * (b // 2 + 1))
                    pool.wait_ge(S("yg_in1"), 16 * 2 * (b // 2 + 1))

        @block.tensor
        def _(pe):
            def mm(o, l, r, start, stop):
                return pe.matmul(o, l, r, start=start, stop=stop)

            pe.wait_ge(S("masks"), 5)
            for b in range(B):
                pe.wait_ge(S("xn_a"), b + 1)
                if b >= 2:
                    pe.wait_ge(S("xt_ev"), b - 1)
                for k in range(KC):
                    last = pe.transpose(PS[b % 2][:, k * T:(k + 1) * T], XN[:, b, k * P:(k + 1) * P], ident[0:T, 0:T])
                last.then_inc(S("xt_pe"), 1)
            pe.wait_ge(S("xt_ev"), B)

            def project(n, w, wsem):
                pe.wait_ge(S(wsem), 16)
                for c in range(KC):
                    for hf in (0, 1):
                        g = n * 8 + c * 2 + hf
                        if g >= 4:
                            pe.wait_ge(S("pj_ev"), g - 3)
                        for k in range(KC):
                            last = mm(PS[4 + g % 4][:, 0:HALF], W3[w][:, k, c * P:(c + 1) * P],
                                      xT[:, k, hf * HB:(hf + 1) * HB, :], k == 0, k == KC - 1)
                        last.then_inc(S("pj_pe"), 1)

            def square_sums(n):
                pe.wait_ge(S("sq_act"), n + 1)
                if n:
                    pe.wait_ge(S("nr_act"), 2 * n)
                for hf in (0, 1):
                    for k in range(KC):
                        last = mm(PS[hf][:, 0:HALF], ones[:], SQ[:, k, hf * HB:(hf + 1) * HB, :], k == 0, k == KC - 1)
                    last.then_inc(S("ns_pe"), 1)

            project(0, 0, "wk_in")
            pe.wait_ge(S("small_in"), 16 * 4)
            for hf in (0, 1):
                for k in range(KC):
                    last = mm(PS[2 + hf][0:32, 0:HALF], Wab[:, k, :], xT[:, k, hf * HB:(hf + 1) * HB, :], k == 0, k == KC - 1)
                last.then_inc(S("gate_pe"), 1)
            project(1, 1, "wq_in")
            pe.wait_ge(S("gate_act"), 2)
            for b in range(B):
                last = pe.transpose(PS[2][0:T, b * 32:(b + 1) * 32], gT[:, b, :], ident[0:32, 0:32])
            last.then_inc(S("gtok_pe"), 1)
            square_sums(0)
            project(2, 2, "wv_in")
            square_sums(1)

            pe.wait_ge(S("qkv_done"), 1)
            for b in range(B):
                p = b % 2
                pe.wait_ge(S("lr_done"), b + 1)
                if b >= 1:
                    pe.wait_ge(S("ex_act"), b)
                for i in range(4):
                    last = mm(PS[i][0:T, 0:4 * T], later[0:T, 0:T], LR[p][:, 4 * i:4 * i + 4, :], True, True)
                last.then_inc(S("ld_pe"), 1)
                for n, src in ((0, kT), (1, vT)):
                    if b >= 1:
                        pe.wait_ge(S("bb_done"), b)
                    for c in range(KC):
                        last = pe.transpose(PS[4 + n][0:T, c * P:(c + 1) * P], src[:, c, b, :], ident[:])
                    last.then_inc(S("kv_pe"), 1)
                pe.wait_ge(S("kv_tok"), 2 * b + 2)
                for i in range(4):
                    for c in range(KC):
                        kk = kT[32 * i:32 * i + 32, c, b, :]
                        last = pe.matmul(PS[4 + i][0:T, c * T:(c + 1) * T], kk, kk, start=True, stop=True)
                last.then_inc(S("g_pe"), 1)

            pe.wait_ge(S("wo_in"), 16)
            pe.wait_ge(S("cw_in"), 48)

            def transposed(src, b, bank, sem):
                for k in range(KC):
                    last = pe.transpose(bank[:, k * T:(k + 1) * T], src[:, k * P:(k + 1) * P], ident[0:T, 0:T])
                last.then_inc(S(sem), 1)

            for b0 in range(0, B, 2):
                two = [(b0 + p, p, PS[4 * p:4 * p + 4]) for p in (0, 1)]
                for i, s0, w in BLK:
                    if i:
                        for b, p, bank in two:
                            pe.wait_ge(S(f"bc_in{p}"), 16 * (b // 2 + 1))
                            pe.wait_ge(S("u_ev"), 4 * b0 + 2 * (i - 1) + p + 1)
                            for h in range(H):
                                last = mm(bank[1][s0:s0 + w, h * DH:(h + 1) * DH], diag_cols(BC[p], i)[0:s0, h, :],
                                          UU[p][0:s0, h * DH:(h + 1) * DH], True, True)
                            last.then_inc(S("acc_pe"), 1)
                    for b, p, bank in two:
                        if i:
                            pe.wait_ge(S("r_done"), 3 * b0 + 2 * (i - 1) + p + 1)
                        else:
                            pe.wait_ge(S(f"mt_in{p}"), 64 * (b // 2 + 1))
                            if b0:
                                pe.wait_ge(S("lg_done"), b - 1)
                        for h in range(H):
                            rhs = RR[p][s0:s0 + w, h * DH:(h + 1) * DH] if i else Vt[0:w, b, h * DH:(h + 1) * DH]
                            last = mm(bank[0][s0:s0 + w, h * DH:(h + 1) * DH], MT[p][s0:s0 + w, h, 0:w], rhs, True, True)
                        last.then_inc(S("u_pe"), 1)
                for b, p, bank in two:
                    pe.wait_ge(S("u_ev"), 4 * b0 + 6 + p + 1)
                    transposed(UU[p], b, bank[2], "ut_pe")
                for b, p, bank in two:
                    pe.wait_ge(S("ut_ev"), b + 1)
                    for g in range(4):
                        for c in range(KC):
                            last = pe.matmul(bank[g][0:T, c * T:(c + 1) * T], TR[p][32 * g:32 * g + 32, c, :],
                                             qT[32 * g:32 * g + 32, c, b, :], start=True, stop=True)
                    last.then_inc(S("w_pe"), 1)
                for b, p, bank in two:
                    pe.wait_ge(S("wm_done"), b + 1)
                    for h in range(H):
                        last = mm(bank[0][0:T, h * DH:(h + 1) * DH], WM[p][:, h, :], Kt[:, b, h * DH:(h + 1) * DH], True, True)
                    last.then_inc(S("o_pe"), 1)
                for b, p, bank in two:
                    pe.wait_ge(S("o_done"), b + 1)
                    transposed(RR[p], b, bank[1], "ot_pe")
                for b, p, bank in two:
                    pe.wait_ge(S("ot_ev"), b + 1)
                    for k in range(KC):
                        last = mm(bank[2][0:T, :], TR[p][:, k, :], Wo[:, k, :], k == 0, k == KC - 1)
                    last.then_inc(S("wo_pe"), 1)
                for b, p, bank in two:
                    pe.wait_ge(S("xh_done"), b + 1)
                    transposed(UU[p], b, bank[3], "xh_pe")
                for b, p, bank in two:
                    pe.wait_ge(S("xh_ev"), b + 1)
                    pe.wait_ge(S(f"ct_in{p}"), 16 * (b // 2 + 1))
                    for hf in (0, 1):
                        for k in range(KC):
                            last = mm(bank[hf][0:T, 0:S2H], TR[p][:, k, :], CT[p][:, k, hf * S2H:(hf + 1) * S2H], k == 0, k == KC - 1)
                    last.then_inc(S("sc_pe"), 1)
                for b, p, bank in two:
                    pe.wait_ge(S("pr_done"), b + 1)
                    for j, s0, w in S2T:
                        last = pe.transpose(bank[2 + j // 4][0:w, (j % 4) * T:(j % 4 + 1) * T], PR[p][:, s0:s0 + w], ident[0:T, 0:T])
                    last.then_inc(S("pt_pe"), 1)
                for b, p, bank in two:
                    pe.wait_ge(S("pt_ev"), b + 1)
                    pe.wait_ge(S("cn_in"), 32 * (b + 1))
                    for j, s0, w in S2T:
                        last = mm(bank[0][0:T, :], PT[p][0:w, j, :], CN[0:w, j, :], j == 0, j == len(S2T) - 1)
                    last.then_inc(S("pv_pe"), 1)
                for b, p, bank in two:
                    pe.wait_ge(S("xn_all"), b + 1)
                    for k in range(KC):
                        last = pe.transpose(bank[1][:, k * T:(k + 1) * T], XN[:, b, k * P:(k + 1) * P], ident[0:T, 0:T])
                    last.then_inc(S("nt_pe"), 1)
                for b, p, bank in two:
                    pe.wait_ge(S("nt_ev"), b + 1)
                    for k in range(KC):
                        last = mm(bank[2][0:T, 0:E], TR[p][:, k, :], Wr[:, k, :], k == 0, k == KC - 1)
                    last.then_inc(S("lg_pe"), 1)

            pe.wait_ge(S("sel_done"), 1)
            mm(PS[0][0:T, 0:B * E], before[0:T, 0:T], rt_eq[:].rearrange("t b e -> t (b e)"), True, True)
            mm(PS[1][0:T, 0:B * E], ones[0:T, 0:T], rt_eq[:].rearrange("t b e -> t (b e)"), True, True).then_inc(S("cnt_pe"), 1)

            def tile_transposed():
                for k in range(KC):
                    last = pe.transpose(PS[6][:, k * P:(k + 1) * P], XG[:, k * P:(k + 1) * P], ident[:])
                last.then_inc(S("xg_tr"), 1)

            pe.wait_ge(S("nt_set"), 1)
            pe.wait_ge(S("xg_in"), 16)
            tile_transposed()
            pe.sem_inc(S("gu_pe"), 4)
            pe.sem_inc(S("y_pe"), 1)
            pe.sem_inc(S("ht_pe"), 2)
            with pe.Fori(0, E) as e:
                nt = pe.value_load(nti[0:1, 0, bass.ds(e, 1)], min_val=1, max_val=MAXNT)
                first = pe.value_load(nti[0:1, 1, bass.ds(e, 1)], min_val=0, max_val=NITEM - 2)
                split = pe.snap(e * PIECES + SLOTS)
                with pe.Fori(0, nt) as tile:
                    item = pe.snap(first + tile, min_val=0, max_val=NITEM - 2)

                    def product(o, xh, xl, wh, wl, start, stop):
                        mm(o, xh, wh, start, False)
                        mm(o, xh, wl, False, False)
                        return mm(o, xl, wh, False, stop)

                    def hidden_transposed(c):
                        o, w = CH[c]
                        pe.wait_ge(S("h_done"), item * 4 + (c + 3))
                        pe.wait_ge(S("ht_lo"), item * 4 + (c + 1))
                        for j in range(w // P):
                            last = pe.transpose(PS[4 + c % 2][:, j * P:(j + 1) * P], HH[c % 2][:, j * P:(j + 1) * P], ident[:])
                        last.then_inc(S("ht_pe"), 1)

                    pe.wait_ge(S("xt_lo"), item + 1)
                    for c, (o, w) in enumerate(CH):
                        pe.wait_ge(S("lo_done"), split + (2 * c + 2))
                        pe.wait_ge(S("h_done"), item * 4 + (c + 1))
                        for half in (0, 1):
                            at_w = half * HID + o
                            for k in range(KC):
                                last = product(PS[2 * (c % 2) + half][:, 0:w], XTH[:, k, :], XTL[:, k, :],
                                               GWH[:, k, at_w:at_w + w], GWL[:, k, at_w:at_w + w], k == 0, k == KC - 1)
                        last.then_inc(S("gu_pe"), 1)
                        if c:
                            hidden_transposed(c - 1)
                    pe.wait_ge(S("xg_in"), (item + 2) * 16)
                    tile_transposed()
                    pe.wait_ge(S("y_ev"), item + 1)
                    for n, (chunks, rows) in enumerate(DOWN):
                        pe.wait_ge(S("ht_lo"), item * 4 + (chunks + 2))
                        pe.wait_ge(S("lo_done"), split + (9 + n))
                        for j in rows:
                            last = product(PS[7][:, :], HTH[:, j, :], HTL[:, j, :], DWH[:, j, :], DWL[:, j, :], j == 0, j == HC - 1)
                        if n == 1:
                            hidden_transposed(3)
                    last.then_inc(S("y_pe"), 1)

        @block.scalar
        def _(act):
            own = Handoff(act, S("act_own"))
            act.dma_start(Wab[:], WabT.rearrange("(k p) n -> p k n", p=P)).then_inc(S("small_in"), 16)
            act.dma_start(b_ab[:], bab).then_inc(S("small_in"), 16)
            act.dma_start(b_qkv[:], bqkv).then_inc(S("small_in"), 16)
            act.dma_start(w_conv[:], conv).then_inc(S("small_in"), 16)
            act.wait_ge(S("consts"), 1)
            act.wait_ge(S("mv_a"), 1)
            act.activation(rstd[:], mv[:, :, 1], ACT.Sqrt, bias=eps_ln[0:T, :]).then_inc(S("sd_a"), 1)
            for b in range(B):
                act.wait_ge(S("xt_pe"), b + 1)
                act.activation(xT[:, :, b, :], PS[b % 2][:, 0:KC * T].rearrange("p (k t) -> p k t", k=KC), ACT.Copy).then_inc(S("xt_ev"), 1)
            act.wait_ge(S("small_in"), 16 * 4)
            act.wait_ge(S("pads"), 1)

            def silu_in(n, w, buf):
                for c in range(KC):
                    for hf in (0, 1):
                        act.wait_ge(S("pj_pe"), n * 8 + c * 2 + hf + 1)
                        act.activation(buf[:, c, hf * HB:(hf + 1) * HB, 2:2 + T],
                                       PS[4 + (c * 2 + hf) % 4][:, 0:HALF].rearrange("p (b t) -> p b t", b=HB), ACT.Silu,
                                       bias=b_qkv[:, w, c:c + 1]).then_inc(S("pj_ev"), 1)

            def silu_out(n, t, squares):
                for c in range(KC):
                    act.wait_ge(S("cv_done"), n * KC + c + 1)
                    last = act.activation(t[:, c], t[:, c], ACT.Silu)
                last.then_inc(S("post_act"), 1)
                if squares:
                    act.wait_ge(S("post_act"), n + 1)
                    if n:
                        act.wait_ge(S("ns_pe"), 2 * n)
                    act.activation(SQ[:], t[:], ACT.Square).then_inc(S("sq_act"), 1)
                    for hf in (0, 1):
                        act.wait_ge(S("ns_pe"), 2 * n + hf + 1)
                        if n and hf == 0:
                            act.wait_ge(S("nrm_done"), n)
                        act.activation(rn[:, hf * HB:(hf + 1) * HB, :], PS[hf][:, 0:HALF].rearrange("p (b t) -> p b t", b=HB),
                                       ACT.Sqrt).then_inc(S("nr_act"), 1)

            silu_in(0, 0, PB)
            for hf in (0, 1):
                act.wait_ge(S("gate_pe"), hf + 1)
                act.activation(gT[:, hf * HB:(hf + 1) * HB, :], PS[2 + hf][0:32, 0:HALF].rearrange("p (b t) -> p b t", b=HB),
                               ACT.Sigmoid, bias=b_ab[:]).then_inc(S("gate_act"), 1)
            silu_in(1, 1, PB2)
            silu_out(0, kT, True)
            act.wait_ge(S("ga_done"), 1)
            act.activation(la[:], la[:], ACT.Ln).then_inc(S("la_done"), 1)
            act.wait_ge(S("cv_done"), KC)
            silu_in(2, 2, PB)
            silu_out(1, qT, True)
            silu_out(2, vT, False)
            for b in range(B):
                p = b % 2
                act.wait_ge(S("ld_pe"), b + 1)
                if b >= 2:
                    act.wait_ge(S(f"ed_out{p}"), 16 * (b // 2))
                for i in range(4):
                    last = act.activation(EB[p][:, 4 * i:4 * i + 4, :], PS[i][0:T, 0:4 * T].rearrange("p (h t) -> p h t", h=4), ACT.Exp)
                last.then_inc(S("ex_act"), 1)
                for n, dst in ((0, Kt), (1, Vt)):
                    act.wait_ge(S("kv_pe"), 2 * b + n + 1)
                    if b == 0:
                        act.wait_ge(S("qkv_done"), 1)
                    act.activation(dst[:, b, :], PS[4 + n][0:T, :], ACT.Copy).then_inc(S("kv_tok"), 1)
            for b0 in range(0, B, 2):
                two = [(b0 + p, p, PS[4 * p:4 * p + 4]) for p in (0, 1)]
                if b0 == 0:
                    act.wait_ge(S("md_out"), 32)
                for i, s0, w in BLK:
                    for b, p, bank in two:
                        act.wait_ge(S("u_pe"), 4 * b0 + 2 * i + p + 1)
                        if b0 and i == 0:
                            act.wait_ge(S("xy_done"), b - 1)
                        last = act.activation(UU[p][s0:s0 + w, :], bank[0][s0:s0 + w, :], ACT.Copy)
                        last.then_inc(S("u_ev"), 1)

                def evacuated(pe_sem, bank, b, p, sem):
                    act.wait_ge(S(pe_sem), b + 1)
                    act.activation(TR[p][:], bank[:, 0:KC * T].rearrange("p (k t) -> p k t", k=KC), ACT.Copy).then_inc(S(sem), 1)

                for b, p, bank in two:
                    evacuated("ut_pe", bank[2], b, p, "ut_ev")
                for b, p, bank in two:
                    act.wait_ge(S("o_pe"), b + 1)
                    act.activation(RR[p][:], bank[0][0:T, :], ACT.Copy).then_inc(S("o_done"), 1)
                for b, p, bank in two:
                    evacuated("ot_pe", bank[1], b, p, "ot_ev")
                for b, p, bank in two:
                    act.wait_ge(S("mv_c"), 2 * b0 + p + 1)
                    act.activation(sd[:, b:b + 1], mv[:, b, 1:2], ACT.Sqrt, bias=eps_ln[0:T, :]).then_inc(S("sd_c"), 1)
                for b, p, bank in two:
                    evacuated("xh_pe", bank[3], b, p, "xh_ev")
                for b, p, bank in two:
                    act.wait_ge(S("sc_dve"), b + 1)
                    act.activation(PR[p][:], PR[p][:], ACT.Exp, bias=nmax[:, b:b + 1], accum_out=rsum[:, b:b + 1]).then_inc(S("pr_done"), 1)
                for b, p, bank in two:
                    act.wait_ge(S("pt_pe"), b + 1)
                    for j, s0, w in S2T:
                        last = act.activation(PT[p][0:w, j, :], bank[2 + j // 4][0:w, (j % 4) * T:(j % 4 + 1) * T], ACT.Copy)
                    last.then_inc(S("pt_ev"), 1)
                for b, p, bank in two:
                    act.wait_ge(S("mv_c"), 2 * b0 + p + 3)
                    act.activation(sd[:, b:b + 1], mv[:, b, 1:2], ACT.Sqrt, bias=eps_ln[0:T, :]).then_inc(S("sd_c"), 1)
                for b, p, bank in two:
                    act.wait_ge(S("y_norm"), b + 1)
                    own(act.activation(RR[p][:], UU[p][:], ACT.Square, accum_out=ss[:, b:b + 1]))
                    act.activation(ss[:, b:b + 1], ss[:, b:b + 1], ACT.Sqrt, bias=eps_rms[0:T, :], scale=1.0 / D).then_inc(S("ss_done"), 1)
                for b, p, bank in two:
                    evacuated("nt_pe", bank[1], b, p, "nt_ev")
                for b, p, bank in two:
                    act.wait_ge(S("lg_pe"), b + 1)
                    act.activation(LG[:, b, :], bank[2][0:T, 0:E], ACT.Copy).then_inc(S("lg_done"), 1)
            act.wait_ge(S("rt_sub"), 1)
            act.activation(rt_p[:], rt_p[:], ACT.Exp).then_inc(S("rt_exp"), 1)
            act.wait_ge(S("nt_set"), 1)

            def rows_high(n):
                act.wait_ge(S("xg_tr"), n)
                act.activation(XTH[:], PS[6][:, :].rearrange("p (k t) -> p k t", k=KC), ACT.Copy).then_inc(S("xt_hi"), 1)

            rows_high(1)
            with act.Fori(0, E) as e:
                nt = act.value_load(nti[0:1, 0, bass.ds(e, 1)], min_val=1, max_val=MAXNT)
                first = act.value_load(nti[0:1, 1, bass.ds(e, 1)], min_val=0, max_val=NITEM - 2)
                free = act.snap(first * 4)
                loads = act.snap(e * (16 * PIECES // SLOTS))

                def weights_high(n):
                    raw, hi, _ = piece(n)
                    act.wait_ge(S(f"w_in{n % SLOTS}"), loads + 16 * (n // SLOTS + 1))
                    if n < 8:
                        act.wait_ge(S("gu_pe"), free + (n // 2 + 1))
                    else:
                        act.wait_ge(S("y_pe"), first + 1)
                    act.activation(hi, raw, ACT.Copy).then_inc(S("hi_done"), 1)

                def tile_of_expert(tile, with_weights):
                    item = act.snap(first + tile)

                    def gated(c):
                        o, w = CH[c]
                        act.wait_ge(S("ht_pe"), item * 4 + (c + 1))
                        act.wait_ge(S("gu_pe"), item * 4 + (c + 5))
                        act.activation(HH[c % 2][:, 0:w], PS[2 * (c % 2)][:, 0:w], ACT.Silu).then_inc(S("silu_done"), 1)

                    def hidden_high(c):
                        o, w = CH[c]
                        act.wait_ge(S("ht_pe"), item * 4 + (c + 3))
                        act.activation(HTH[:, o // P:(o + w) // P, :], PS[4 + c % 2][:, 0:w].rearrange("p (j t) -> p j t", t=P),
                                       ACT.Copy).then_inc(S("ht_hi"), 1)

                    for step in ORDER:
                        if step[0] == "w" and with_weights:
                            weights_high(step[1])
                        elif step[0] == "h":
                            gated(step[1])
                        elif step[0] == "t":
                            hidden_high(step[1])
                        elif step[0] == "x":
                            rows_high(item + 2)

                tile_of_expert(0, True)
                with act.If(nt > 1):
                    with act.Fori(1, nt) as tile:
                        tile_of_expert(tile, False)

        @block.vector
        def _(dve):
            own = Handoff(dve, S("dve_own"))
            tt, ts, stt = dve.tensor_tensor, dve.tensor_scalar, dve.scalar_tensor_tensor
            dve.memset(eps_ln[:], LN_EPS)
            dve.memset(eps_rms[:], RMS_EPS)
            dve.memset(zero_col[:], 0.0).then_inc(S("consts"), 1)
            dve.memset(ZR[:], 0.0).then_inc(S("zr_set"), 1)
            for buf in (PB, PB2):
                dve.memset(buf[:, :, :, 0:2], 0.0)
                last = dve.memset(buf[:, :, :, 2 + T:TP], 0.0)
            last.then_inc(S("pads"), 1)
            for b in range(B):
                dve.wait_ge(S(f"x_in{b}"), 16)
                last = dve.bn_stats(stats[:, b, :], X[:, b, :])
            own(last)
            for b in range(B):
                last = dve.bn_aggr(mv[:, b, :], stats[:, b, :])
            last.then_inc(S("mv_a"), 1)
            dve.wait_ge(S("sd_a"), 1)
            dve.wait_ge(S("mv_a"), 1)
            own(dve.reciprocal(rstd[:], rstd[:]))
            for b in range(B):
                ts(XN[:, b, :], X[:, b, :], mv[:, b, 0:1], rstd[:, b:b + 1], ALU.subtract, ALU.mult).then_inc(S("xn_a"), 1)

            def convolve(n, w, buf, t):
                for c in range(KC):
                    dve.wait_ge(S("pj_ev"), n * 8 + 2 * c + 2)
                    own(ts(t[:, c], buf[:, c, :, 0:T], w_conv[:, w, c, 0:1], None, ALU.mult))
                    for j in range(1, TAPS):
                        last = stt(t[:, c], buf[:, c, :, j:j + T], w_conv[:, w, c, j:j + 1], t[:, c], ALU.mult, ALU.add)
                        if j < TAPS - 1:
                            own(last)
                    last.then_inc(S("cv_done"), 1)

            def normalise(n, t):
                dve.wait_ge(S("nr_act"), 2 * n + 2)
                own(ts(rn[:], rn[:], L2_EPS, None, ALU.add))
                own(dve.reciprocal(rn[:], rn[:]))
                for c in range(KC):
                    last = tt(t[:, c], t[:, c], rn[:], ALU.mult)
                last.then_inc(S("nrm_done"), 1)

            dve.wait_ge(S("small_in"), 16 * 4)
            convolve(0, 0, PB, kT)
            dve.wait_ge(S("gtok_pe"), 1)
            own(dve.tensor_copy(gtok[:], PS[2][0:T, 0:B * 32].rearrange("t (b g) -> t b g", b=B)))
            ts(la[:], gtok[:, :, 0:H], LEAST_DECAY, None, ALU.max).then_inc(S("ga_done"), 1)
            convolve(1, 1, PB2, qT)
            dve.wait_ge(S("post_act"), 1)
            normalise(0, kT)
            convolve(2, 2, PB, vT)
            normalise(1, qT)
            dve.wait_ge(S("post_act"), 3)
            dve.wait_ge(S("nrm_done"), 2)
            dve.sem_inc(S("qkv_done"), 1)
            for b in range(B):
                p = b % 2
                dve.wait_ge(S("ex_act"), b + 1)
                dve.wait_ge(S("mb_done"), b + 1)
                tt(EB[p][:], EB[p][:], MB[p][:], ALU.mult).then_inc(S("e_done"), 1)
                dve.wait_ge(S("g_pe"), b + 1)
                dve.wait_ge(S("e_done"), b + 1)
                if b >= 2:
                    dve.wait_ge(S(f"bd_out{p}"), 16 * (b // 2))
                for g in range(4):
                    sums = PS[4 + g][0:T, 0:4 * T].rearrange("p (c t) -> p c t", c=KC)
                    blocks = BB[p][:, 0:3 * H * 32].rearrange("r (i c g s) -> r g c i s", i=3, c=KC, g=4)[:, g]
                    tt(blocks, sums[:, :, 0:96].rearrange("r c (i s) -> r c i s", i=3),
                       EB[p][:, g::4, 0:96].rearrange("r c (i s) -> r c i s", i=3), ALU.mult)
                    last = tt(diag_cols(BB[p], 3)[:, g::4, :], sums[:, :, 96:T], EB[p][:, g::4, 96:T], ALU.mult)
                last.then_inc(S("bb_done"), 1)
            dve.wait_ge(S("bb_done"), B)
            dve.wait_ge(S("kv_tok"), 2 * B)
            dve.wait_ge(S("g_pe"), B)
            dve.wait_ge(S("ed_out0"), 16 * B // 2)
            dve.wait_ge(S("ed_out1"), 16 * B // 2)
            dve.wait_ge(S("bd_out0"), 16 * B // 2)
            dve.wait_ge(S("bd_out1"), 16 * B // 2)
            dve.memset(MI[:], 0.0)
            own(dve.memset(MI3[:], 0.0))
            dve.memset(MI[:].rearrange("p i r s -> p i (r s)")[:, :, ::33], 1.0)
            own(dve.memset(MI3[:].rearrange("p r s -> p (r s)")[:, ::LAST + 1], 1.0))
            dve.wait_ge(S("dg_in"), 16 * 4 * B)
            for s in range(1, 32):
                tm = TM[:, 0:3 * s * s].rearrange("p (i a r) -> p i a r", i=3, a=s)
                own(tt(tm, MI[:, :, 0:s, 0:s], DG[:, :, 0:s, s].unsqueeze(2).broadcast_to([P, 3, s, s]), ALU.mult))
                last = dve.tensor_reduce(MI[:, :, 0:s, s], tm, AX_X, ALU.add, negate=True)
                own(last)
            for s in range(1, LAST):
                tm = TM[:, 0:s * s].rearrange("p (a r) -> p a r", a=s)
                own(tt(tm, MI3[:, 0:s, 0:s], DG3[:, 0:s, s].unsqueeze(1).broadcast_to([P, s, s]), ALU.mult))
                own(dve.tensor_reduce(MI3[:, 0:s, s], tm, AX_X, ALU.add, negate=True))
            dve.sem_inc(S("mi_done"), 1)
            dve.wait_ge(S("md_out"), 32)
            dve.wait_ge(S("cw_in"), 48)
            for b0 in range(0, B, 2):
                two = [(b0 + p, p, PS[4 * p:4 * p + 4]) for p in (0, 1)]
                for i, s0, w in BLK[1:]:
                    for b, p, bank in two:
                        dve.wait_ge(S("acc_pe"), 3 * b0 + 2 * (i - 1) + p + 1)
                        last = tt(RR[p][s0:s0 + w, :], Vt[s0:s0 + w, b, :], bank[1][s0:s0 + w, :], ALU.subtract)
                        last.then_inc(S("r_done"), 1)
                for b, p, bank in two:
                    dve.wait_ge(S("w_pe"), b + 1)
                    dve.wait_ge(S(f"ee_in{p}"), 16 * (b // 2 + 1))
                    for g in range(4):
                        last = tt(WM[p][:, g::4, :], bank[g][0:T, 0:4 * T].rearrange("p (h t) -> p h t", h=4),
                                  EE[p][:, g::4, :], ALU.mult)
                    last.then_inc(S("wm_done"), 1)

                def layer_norm(b, p):
                    own(dve.bn_stats(stats[:, b, :], X[:, b, :]))
                    dve.bn_aggr(mv[:, b, :], stats[:, b, :]).then_inc(S("mv_c"), 1)

                def normed(b, p, n, sem):
                    dve.wait_ge(S("sd_c"), 2 * b0 + 2 * n + p + 1)
                    dve.wait_ge(S("mv_c"), 2 * b0 + 2 * n + p + 1)
                    own(dve.reciprocal(rstd[:, b:b + 1], sd[:, b:b + 1]))
                    ts(UU[p][:], X[:, b, :], mv[:, b, 0:1], rstd[:, b:b + 1], ALU.subtract, ALU.mult).then_inc(S(sem), 1)

                for b, p, bank in two:
                    dve.wait_ge(S("wo_pe"), b + 1)
                    dve.wait_ge(S("xb_done"), b + 1)
                    own(tt(X[:, b, :], X[:, b, :], bank[2][0:T, :], ALU.add))
                    layer_norm(b, p)
                for b, p, bank in two:
                    normed(b, p, 0, "xh_done")
                for b, p, bank in two:
                    dve.wait_ge(S("sc_pe"), b + 1)
                    dve.wait_ge(S("mn_done"), b + 1)
                    for hf in (0, 1):
                        last = stt(PR[p][:, hf * S2H:(hf + 1) * S2H], bank[hf][0:T, 0:S2H], SCALE, MN[p][:, hf * S2H:(hf + 1) * S2H],
                                   ALU.mult, ALU.add)
                    own(last)
                    dve.tensor_reduce(nmax[:, b:b + 1], PR[p][:], AX_X, ALU.max, negate=True).then_inc(S("sc_dve"), 1)
                for b, p, bank in two:
                    dve.wait_ge(S("pv_pe"), b + 1)
                    own(dve.reciprocal(rsum[:, b:b + 1], rsum[:, b:b + 1]))
                    own(stt(X[:, b, :], bank[0][0:T, :], rsum[:, b:b + 1], X[:, b, :], ALU.mult, ALU.add))
                    layer_norm(b, p)
                for b, p, bank in two:
                    normed(b, p, 1, "y_norm")
                for b, p, bank in two:
                    dve.wait_ge(S("ss_done"), b + 1)
                    dve.wait_ge(S("y_norm"), b + 1)
                    own(dve.reciprocal(ss[:, b:b + 1], ss[:, b:b + 1]))
                    stt(XN[:, b, :], UU[p][:], ss[:, b:b + 1], nw_b[:], ALU.mult, ALU.mult).then_inc(S("xn_all"), 1)

            def bc(col):
                return col.unsqueeze(2).broadcast_to([T, B, E])

            dve.wait_ge(S("lg_done"), B)
            dve.wait_ge(S("iota_e"), 1)
            own(dve.tensor_reduce(rt_m[:, :, 0], LG[:], AX_X, ALU.max))
            tt(rt_p[:], LG[:], bc(rt_m[:, :, 0]), ALU.subtract).then_inc(S("rt_sub"), 1)
            dve.wait_ge(S("rt_exp"), 1)
            own(dve.tensor_reduce(rt_m[:, :, 6], rt_p[:], AX_X, ALU.add))
            own(dve.reciprocal(rt_m[:, :, 6], rt_m[:, :, 6]))
            own(tt(rt_p[:], rt_p[:], bc(rt_m[:, :, 6]), ALU.mult))
            for c, oh in ((0, rt_o0), (1, rt_o1)):
                own(dve.tensor_reduce(rt_m[:, :, 2 * c], rt_p[:], AX_X, ALU.max))
                own(tt(rt_t[:], rt_p[:], bc(rt_m[:, :, 2 * c]), ALU.is_lt))
                own(stt(rt_t[:], rt_t[:], 100.0, rt_io[:], ALU.mult, ALU.add))
                own(dve.tensor_reduce(rt_m[:, :, 2 * c + 1], rt_t[:], AX_X, ALU.min))
                own(tt(oh[:], rt_io[:], bc(rt_m[:, :, 2 * c + 1]), ALU.is_equal))
                if c == 0:
                    own(stt(rt_p[:], oh[:], -2.0, rt_p[:], ALU.mult, ALU.add))
            tt(rt_eq[:], rt_o0[:], rt_o1[:], ALU.add).then_inc(S("sel_done"), 1)
            own(tt(rt_m[:, :, 6], rt_m[:, :, 0], rt_m[:, :, 2], ALU.add))
            own(dve.reciprocal(rt_m[:, :, 6], rt_m[:, :, 6]))
            dve.wait_ge(S("al_in"), 16)
            own(ts(al[:], al[:], -0.5, 2.0, ALU.max, ALU.min))
            own(ts(rt_m[:, :, 6], rt_m[:, :, 6], al[:], None, ALU.mult))
            for c in (0, 1):
                last = tt(wa[:, c, :], rt_m[:, :, 2 * c], rt_m[:, :, 6], ALU.mult)
            own(last)
            dve.wait_ge(S("cnt_pe"), 1)
            own(dve.memset(rt_boff[:, 0, :], 0.0))
            for b in range(B):
                own(tt(rt_boff[:, b + 1, :], rt_boff[:, b, :], PS[1][0:T, b * E:(b + 1) * E], ALU.add))
            own(dve.memset(rt_nt[:], 1.0))
            for m in range(1, MAXNT):
                own(stt(rt_nt[:], rt_boff[:, B, :], float(P * m), rt_nt[:], ALU.is_gt, ALU.add))
            own(dve.memset(rt_bs[:, 0:1], 0.0))
            for e in range(E):
                own(tt(rt_bs[:, e + 1:e + 2], rt_bs[:, e:e + 1], rt_nt[:, e:e + 1], ALU.add))
            dve.tensor_copy(nti[:, 0, :], rt_nt[:])
            dve.tensor_copy(nti[:, 1, :], rt_bs[:, 0:E]).then_inc(S("nt_set"), 1)
            own(tt(rt_pos[:], PS[0][0:T, 0:B * E].rearrange("t (b e) -> t b e", b=B), rt_boff[:, 0:B, :], ALU.add))
            own(stt(rt_pos[:], rt_bs[:, 0:E].unsqueeze(1).broadcast_to([T, B, E]), float(P), rt_pos[:], ALU.mult, ALU.add))
            for c, oh in ((0, rt_o0), (1, rt_o1)):
                own(tt(rt_t[:], rt_pos[:], oh[:], ALU.mult))
                own(dve.tensor_reduce(gf[:, c, :], rt_t[:], AX_X, ALU.add))
            dve.tensor_copy(gi[:], gf[:]).then_inc(S("gi_set"), 1)

            dve.sem_inc(S("h_done"), 2)
            dve.sem_inc(S("y_free"), 2)
            dve.memset(PS[7][:, :], 0.0).then_inc(S("y_zero"), 1)
            dve.wait_ge(S("y_zero"), 1)

            dve.sem_inc(S("lo_done"), SLOTS)
            dve.sem_inc(S("ht_lo"), 2)

            def rows_low(n):
                dve.wait_ge(S("xt_hi"), n)
                tt(XTL[:], PS[6][:, :].rearrange("p (k t) -> p k t", k=KC), XTH[:].bitcast(F32), ALU.subtract).then_inc(S("xt_lo"), 1)

            def y_evacuated(n):
                dve.wait_ge(S("y_free"), n + 1)
                dve.wait_ge(S("y_pe"), n + 1)
                dve.tensor_copy(YS[:], PS[7][:, :]).then_inc(S("y_ev"), 1)

            rows_low(1)
            with dve.Fori(0, E) as e:
                nt = dve.value_load(nti[0:1, 0, bass.ds(e, 1)], min_val=1, max_val=MAXNT)
                first = dve.value_load(nti[0:1, 1, bass.ds(e, 1)], min_val=0, max_val=NITEM - 2)
                split = dve.snap(e * PIECES)

                def weights_low(n):
                    raw, hi, lo = piece(n)
                    dve.wait_ge(S("hi_done"), split + (n + 1))
                    tt(lo, raw, hi.bitcast(F32), ALU.subtract).then_inc(S("lo_done"), 1)

                def tile_of_expert(tile, with_weights):
                    item = dve.snap(first + tile)

                    def gated(c):
                        o, w = CH[c]
                        dve.wait_ge(S("silu_done"), item * 4 + (c + 1))
                        tt(HH[c % 2][:, 0:w], HH[c % 2][:, 0:w], PS[2 * (c % 2) + 1][:, 0:w], ALU.mult).then_inc(S("h_done"), 1)

                    def hidden_low(c):
                        o, w = CH[c]
                        dve.wait_ge(S("ht_hi"), item * 4 + (c + 1))
                        tt(HTL[:, o // P:(o + w) // P, :], PS[4 + c % 2][:, 0:w].rearrange("p (j t) -> p j t", t=P),
                           HTH[:, o // P:(o + w) // P, :].bitcast(F32), ALU.subtract).then_inc(S("ht_lo"), 1)

                    for step in ORDER:
                        if step[0] == "w" and with_weights:
                            weights_low(step[1])
                        elif step[0] == "h":
                            gated(step[1])
                        elif step[0] == "t":
                            hidden_low(step[1])
                        elif step[0] == "x":
                            rows_low(item + 2)
                        elif step[0] == "y":
                            y_evacuated(item)

                tile_of_expert(0, True)
                with dve.If(nt > 1):
                    with dve.Fori(1, nt) as tile:
                        tile_of_expert(tile, False)
                last_item = dve.snap(first + nt)
            y_evacuated(last_item)
            dve.wait_ge(S("xy_done"), B)
            dve.wait_ge(S("y_free"), last_item + 2)
            dve.sem_inc(S("moe_end"), 1)
            for b in range(B):
                dve.wait_ge(S(f"yg_in{b % 2}"), 32 * (b // 2 + 1))
                own(stt(X[:, b, :], YG[:, 0, b, :], wa[:, 0, b:b + 1], X[:, b, :], ALU.mult, ALU.add))
                stt(X[:, b, :], YG[:, 1, b, :], wa[:, 1, b:b + 1], X[:, b, :], ALU.mult, ALU.add).then_inc(S("fin"), 1)


def kernel(x, ctx_1024, mask_Bx1xS2_fk0, L0_attn_Wq, L0_attn_bq, L0_attn_Wk, L0_attn_bk, L0_attn_Wv, L0_attn_bv,
           L0_attn_Wa, L0_attn_ba, L0_attn_Wb, L0_attn_bb, L0_attn_conv_q, L0_attn_conv_k, L0_attn_conv_v, L0_attn_Wo,
           L0_attn_bo, L0_ffn_norm_weight, L0_ffn_router_weight, L0_ffn_gate_up_weight, L0_ffn_down_weight,
           L0_ffn_residual_alpha):
    import numpy as np
    import concourse.bacc as bacc
    from concourse.bass_utils import run_bass_kernel_spmd

    c = np.ascontiguousarray
    D, H, P = 512, 16, 128
    arrays = {
        "x": c(x), "ctx": c(ctx_1024), "ctxT": c(np.transpose(np.asarray(ctx_1024), (0, 2, 1))), "mask": c(mask_Bx1xS2_fk0),
        "WqT": c(np.asarray(L0_attn_Wq).T), "WkT": c(np.asarray(L0_attn_Wk).T), "WvT": c(np.asarray(L0_attn_Wv).T),
        "bqkv": c(np.stack([np.asarray(v).reshape(D // P, P).T for v in (L0_attn_bk, L0_attn_bq, L0_attn_bv)], 1)),
        "WabT": c(np.concatenate([np.asarray(L0_attn_Wa), np.asarray(L0_attn_Wb)], 0).T),
        "bab": c(np.concatenate([np.asarray(L0_attn_ba), np.asarray(L0_attn_bb)])[:, None]),
        "conv": c(np.stack([np.asarray(v).reshape(D // P, P, 4).transpose(1, 0, 2)
                            for v in (L0_attn_conv_k, L0_attn_conv_q, L0_attn_conv_v)], 1)),
        "WoT": c(np.asarray(L0_attn_Wo).T), "bo": c(L0_attn_bo), "norm_w": c(L0_ffn_norm_weight),
        "WrT": c(np.asarray(L0_ffn_router_weight).T),
        "GU": c(np.asarray(L0_ffn_gate_up_weight).transpose(0, 2, 1).reshape(8, D // P, P, -1).transpose(0, 2, 1, 3)),
        "DN": c(np.asarray(L0_ffn_down_weight).transpose(0, 2, 1).reshape(8, -1, P, D).transpose(0, 2, 1, 3)),
        "alpha": c(np.asarray(L0_ffn_residual_alpha).reshape(1)),
    }
    nc = bacc.Bacc("TRN2", target_bir_lowering=False, num_devices=1)
    args = [nc.dram_tensor(f"in_{n}", a.shape, mybir.dt.from_np(a.dtype), kind="ExternalInput").ap() for n, a in arrays.items()]
    out = nc.dram_tensor("out", (8, 100, D), F32, kind="ExternalOutput").ap()
    decoder_layer(nc, *args, out)
    r = run_bass_kernel_spmd(nc, [{f"in_{n}": a for n, a in arrays.items()}], core_ids=[0])
    return r.results[0]["out"]
```

```python
from contextlib import ExitStack

import concourse.bass as bass
from concourse import mybir

ALU = mybir.AluOpType
ACT = mybir.ActivationFunctionType
F32 = mybir.dt.float32
I32 = mybir.dt.int32
F32R = mybir.dt.float32r
AX_X = mybir.AxisListType.X

P = 128
NEG = -1.0e9


class Handoff:

    def __init__(self, eng, sem):
        self.eng, self.sem, self.n = eng, sem, 0

    def __call__(self, ins):
        self.n += 1
        ins.then_inc(self.sem, 1)
        self.eng.wait_ge(self.sem, self.n)


def decoder_layer(nc, x, ctx, ctxT, mask, WqT, WkT, WvT, bqkv, WabT, bab, conv, WoT, bo, norm_w, WrT, GU, DN, alpha, out):
    B, T, D = x.shape
    S2 = ctx.shape[1]
    H, DH = 16, 32
    KC = D // P
    NTOK = B * T
    HALF = NTOK // 2
    HB = B // 2
    TAPS = 4
    TP = T + TAPS - 1
    BLK = [(i, 32 * i, min(32, T - 32 * i)) for i in range(4)]
    LAST = BLK[3][2]
    S2H = S2 // 2
    S2T = [(j, P * j, min(P, S2 - P * j)) for j in range(-(-S2 // P))]
    E, HID = DN.shape[0], DN.shape[2] * P
    HC = HID // P
    CH = [(0, 384), (384, 384), (768, 384), (1152, 256)]
    MAXNT = -(-NTOK // P)
    NITEM = (2 * NTOK + E * (P - 1)) // P + 1
    ZPARTS = 7
    PIECES, SLOTS = 12, 4
    LN_EPS, RMS_EPS, L2_EPS = 1e-5, 1e-6, 1e-6
    SCALE = float(D) ** -0.5
    LEAST_DECAY = 2.0 ** -63

    with ExitStack() as stack:
        sems = {}

        def S(name):
            if name not in sems:
                sems[name] = stack.enter_context(nc.semaphore(name))
            return sems[name]

        base = [16512]

        def at(name, shape, offset, dt=F32):
            return nc.alloc_sbuf_tensor_at(name, list(shape), dt, offset=offset)

        def size(shape):
            n = 4
            for s in shape[1:]:
                n *= s
            return -(-n // 32) * 32

        def place(cursor, name, shape, dt=F32):
            t = at(name, shape, cursor[0], dt)
            cursor[0] += size(shape)
            assert cursor[0] <= 229368, (name, cursor[0])
            return t

        X = place(base, "X", [T, B, D])
        ident = place(base, "ident", [P, P])
        later = place(base, "later", [P, P])
        upto = place(base, "upto", [P, P])
        before = place(base, "before", [P, P])
        ones = place(base, "ones", [P, P])
        eps_ln = place(base, "eps_ln", [P, 1])
        eps_rms = place(base, "eps_rms", [P, 1])
        zero_col = place(base, "zero_col", [P, 1])
        stats = place(base, "stats", [T, B, 6])
        mv = place(base, "mv", [T, B, 2])
        rstd = place(base, "rstd", [T, B])
        gtok = place(base, "gtok", [T, B, 32])
        la = place(base, "la", [T, B, H])
        sd = place(base, "sd", [T, B])
        nmax = place(base, "nmax", [T, B])
        rsum = place(base, "rsum", [T, B])
        ss = place(base, "ss", [T, B])
        LG = place(base, "LG", [T, B, E])
        r_names = "rt_p rt_eq rt_io rt_o0 rt_o1 rt_t rt_pos".split()
        rt_p, rt_eq, rt_io, rt_o0, rt_o1, rt_t, rt_pos = [place(base, n, [T, B, E]) for n in r_names]
        rt_m = place(base, "rt_m", [T, B, 8])
        rt_boff = place(base, "rt_boff", [T, B + 1, E])
        rt_nt = place(base, "rt_nt", [T, E])
        rt_bs = place(base, "rt_bs", [T, E + 1])
        gf = place(base, "gf", [T, 2, B])
        gi = place(base, "gi", [T, 2, B], I32)
        nti = place(base, "nti", [T, 2, E], I32)
        al = place(base, "al", [T, 1])
        wa = place(base, "wa", [T, 2, B])
        XN = place(base, "XN", [T, B, D])
        later_phases = base[0]

        cur = [later_phases]
        qT = place(cur, "qT", [P, KC, B, T])
        Wo = place(cur, "Wo", [P, KC, D])
        Kt = place(cur, "Kt", [T, B, D])
        Vt = place(cur, "Vt", [T, B, D])
        after_b = cur[0]
        kT = place(cur, "kT", [P, KC, B, T])
        vT = at("vT", [P, KC, B, T], after_b)
        xT = place(cur, "xT", [P, KC, B, T])
        Wq = place(cur, "Wq", [P, KC, D])
        Wv = place(cur, "Wv", [P, KC, D])
        rn = place(cur, "rn", [P, B, T])
        b_qkv = place(cur, "b_qkv", [P, 3, KC])
        w_conv = place(cur, "w_conv", [P, 3, KC, TAPS])
        DG = place(cur, "DG", [P, 3, 32, 32])
        DG3 = place(cur, "DG3", [P, LAST, LAST])
        a_b_c = cur[0]
        PBk = at("PBk", [P, KC, B, TP], after_b - 2 * size([T, B, D]))
        SQk = at("SQk", [P, KC, B, T], after_b - size([T, B, D]))
        Wk = place(cur, "Wk", [P, KC, D])
        gT = place(cur, "gT", [32, B, T])
        Wab = place(cur, "Wab", [P, KC, 32])
        b_ab = place(cur, "b_ab", [32, 1])
        ZR = place(cur, "ZR", [P, NITEM * D // ZPARTS])
        cur = [a_b_c]
        LR = [place(cur, f"LR{p}", [T, H, T]) for p in (0, 1)]
        MB = [place(cur, f"MB{p}", [T, H, T]) for p in (0, 1)]
        EB = [place(cur, f"EB{p}", [T, H, T]) for p in (0, 1)]
        BB = [place(cur, f"BB{p}", [T, H * T]) for p in (0, 1)]
        cur = [a_b_c]
        MI = place(cur, "MI", [P, 3, 32, 32])
        MI3 = place(cur, "MI3", [P, LAST, LAST])
        TM = place(cur, "TM", [P, 3 * 32 * 32])
        PBq = place(cur, "PBq", [P, KC, B, TP])
        SQq = at("SQq", [P, KC, B, T], cur[0] - size([P, KC, B, TP]))
        PBv = at("PBv", [P, KC, B, TP], after_b - size([T, B, D]))
        TAP = [[place(cur, f"TAP{p}{j}", [P, B, T]) for j in range(1, TAPS)] for p in (0, 1)]
        cur = [after_b]
        bo_b = place(cur, "bo_b", [T, D])
        nw_b = place(cur, "nw_b", [T, D])
        Wr = place(cur, "Wr", [P, KC, E])
        EE = [place(cur, f"EE{p}", [T, H, T]) for p in (0, 1)]
        BC = [place(cur, f"BC{p}", [T, H * T]) for p in (0, 1)]
        WM = [BC[p][:].rearrange("t (h s) -> t h s", h=H) for p in (0, 1)]
        MT = [place(cur, f"MT{p}", [T, H, 32]) for p in (0, 1)]
        UU = [place(cur, f"UU{p}", [T, D]) for p in (0, 1)]
        RR = [place(cur, f"RR{p}", [T, D]) for p in (0, 1)]
        TR = [place(cur, f"TR{p}", [P, KC, T]) for p in (0, 1)]
        CT = [place(cur, f"CT{p}", [P, KC, S2]) for p in (0, 1)]
        CN = [place(cur, f"CN{p}", [P, len(S2T), D]) for p in (0, 1)]
        MN = [place(cur, f"MN{p}", [T, S2]) for p in (0, 1)]
        PR = [place(cur, f"PR{p}", [T, S2]) for p in (0, 1)]
        PT = [place(cur, f"PT{p}", [P, len(S2T), T]) for p in (0, 1)]
        YN = [place(cur, f"YN{p}", [T, D]) for p in (0, 1)]
        cur = [later_phases]
        GWH = place(cur, "GWH", [P, KC, 2 * HID], F32R)
        GWL = place(cur, "GWL", [P, KC, 2 * HID], F32R)
        DWH = place(cur, "DWH", [P, HC, D], F32R)
        DWL = place(cur, "DWL", [P, HC, D], F32R)
        ST = [place(cur, f"ST{n}", [P, 4 * 384]) for n in range(SLOTS)]
        XG = place(cur, "XG", [P, D])
        HH = [place(cur, f"HH{n}", [P, 384]) for n in (0, 1)]
        YS = place(cur, "YS", [P, D])
        YG = at("YG", [T, 2, B, D], later_phases)
        cur = [later_phases - size([T, B, D])]
        XTH = place(cur, "XTH", [P, KC, P], F32R)
        XTL = place(cur, "XTL", [P, KC, P], F32R)
        HTH = place(cur, "HTH", [P, HC, P], F32R)
        HTL = place(cur, "HTL", [P, HC, P], F32R)
        assert cur[0] <= later_phases

        DOWN = [(1, range(0, 3)), (2, range(3, 6)), (3, range(6, 9)), (4, range(9, HC))]
        AHEAD = 4
        ORDER = [("y", 0), ("w", 4), ("h", 0), ("w", 5), ("w", 6), ("h", 1), ("t", 0),
                 ("w", 7), ("w", 8), ("h", 2), ("t", 1), ("w", 9), ("h", 3), ("t", 2), ("x", 0), ("w", 10), ("t", 3), ("w", 11)]

        def piece(n):
            if n < 8:
                o, w = CH[n // 2]
                o += HID * (n % 2)
                return ST[n % SLOTS][:, 0:KC * w].rearrange("p (k w) -> p k w", k=KC), GWH[:, :, o:o + w], GWL[:, :, o:o + w]
            j = 3 * (n - 8)
            m = min(3, HC - j)
            return ST[n % SLOTS][:, 0:m * D].rearrange("p (j d) -> p j d", j=m), DWH[:, j:j + m, :], DWL[:, j:j + m, :]

        PS = [stack.enter_context(nc.psum_tensor(f"PS{i}", [P, 512], F32)) for i in range(8)]

        def dram(name, shape, dt=F32):
            return nc.dram_tensor(name, list(shape), dt, kind="Internal").ap()

        Ed = dram("Ed", [B, T, H, T])
        Bd = dram("Bd", [B, T, H * T])
        Md = dram("Md", [B * H, 3, 32, 32])
        Md3 = dram("Md3", [B * H, LAST, LAST])
        XGd = dram("XGd", [NITEM * P, D])
        YGd = dram("YGd", [NITEM * P, D])

        def diag_cols(rows, i):
            if i < 3:
                return rows[:, i * H * 32:(i + 1) * H * 32].rearrange("r (h s) -> r h s", h=H)
            return rows[:, 3 * H * 32:].rearrange("r (h s) -> r h s", h=H)

        block = stack.enter_context(nc.Block())

        @block.sync
        def _(sp):
            for b in range(B):
                sp.dma_start(X[:, b, :], x[b]).then_inc(S(f"x_in{b}"), 16)
            sp.dma_start(Wk[:], WkT.rearrange("(k p) n -> p k n", p=P)).then_inc(S("wk_in"), 16)
            sp.dma_start(Wv[:], WvT.rearrange("(k p) n -> p k n", p=P)).then_inc(S("wv_in"), 16)
            sp.dma_start(Wq[:], WqT.rearrange("(k p) n -> p k n", p=P)).then_inc(S("wq_in"), 16)
            sp.dma_start(Wo[:], WoT.rearrange("(k p) n -> p k n", p=P)).then_inc(S("wo_in"), 16)
            sp.wait_ge(S("zr_set"), 1)
            for j in range(ZPARTS):
                n = NITEM * P // ZPARTS
                for rows in (XGd, YGd):
                    sp.dma_start(rows[j * n:(j + 1) * n, :].rearrange("(p r) d -> p (r d)", p=P), ZR[:, :]).then_inc(S("rows_zero"), 16)
            def diagonal_blocks(b):
                sp.wait_ge(S(f"bd_out{b % 2}"), 16 * (b // 2 + 1))
                for i, s0, w in BLK:
                    src = diag_cols(Bd[b], i)[s0:s0 + w].rearrange("r h s -> h r s")
                    dst = DG[b * H:(b + 1) * H, i] if i < 3 else DG3[b * H:(b + 1) * H]
                    sp.dma_start(dst, src).then_inc(S("dg_in"), 16)

            for b in range(B):
                p = b % 2
                sp.wait_ge(S("e_done"), b + 1)
                sp.dma_start(Ed[b], EB[p][:]).then_inc(S(f"ed_out{p}"), 16)
                sp.wait_ge(S("bb_done"), b + 1)
                sp.dma_start(Bd[b], BB[p][:]).then_inc(S(f"bd_out{p}"), 16)
                if b:
                    diagonal_blocks(b - 1)
            diagonal_blocks(B - 1)
            sp.wait_ge(S("mi_done"), 1)
            sp.dma_start(Md[:], MI[:]).then_inc(S("md_out"), 16)
            sp.dma_start(Md3[:], MI3[:]).then_inc(S("md_out"), 16)
            sp.wait_ge(S("vt_ev"), B)
            sp.wait_ge(S("md_out"), 32)

            def inverses(b):
                for i, s0, w in BLK:
                    m = Md[b * H:(b + 1) * H, i] if i < 3 else Md3[b * H:(b + 1) * H]
                    sp.dma_start(MT[b % 2][s0:s0 + w, :, 0:w], m.rearrange("h r s -> r h s")).then_inc(S(f"mt_in{b % 2}"), 16)

            def couplings(b):
                sp.dma_start(BC[b % 2][:], Bd[b]).then_inc(S(f"bc_in{b % 2}"), 16)

            def decays(b):
                sp.dma_start(EE[b % 2][:], Ed[b]).then_inc(S(f"ee_in{b % 2}"), 16)

            for load in (inverses, couplings):
                for b in (0, 1):
                    load(b)
            sp.dma_start(bo_b[:], bo.partition_broadcast(T)).then_inc(S("cw_in"), 16)
            sp.dma_start(nw_b[:], norm_w.partition_broadcast(T)).then_inc(S("cw_in"), 16)
            sp.dma_start(Wr[:], WrT.rearrange("(k p) n -> p k n", p=P)).then_inc(S("cw_in"), 16)
            sp.dma_start(al[:], alpha.partition_broadcast(T)).then_inc(S("al_in"), 16)
            decays(0)
            decays(1)
            sp.wait_ge(S("qkv_done"), 1)
            for b in range(B):
                p = b % 2
                if b >= 2:
                    sp.wait_ge(S("o_pe"), b - 1)
                    inverses(b)
                    couplings(b)
                    decays(b)
                    sp.wait_ge(S("sc_pe"), b - 1)
                    sp.wait_ge(S("sc_dve"), b - 1)
                sp.dma_start(CT[p][:], ctxT[b].rearrange("(k p) s -> p k s", p=P)).then_inc(S(f"ct_in{p}"), 16)
                sp.dma_start(MN[p][:], mask[b].partition_broadcast(T).rearrange("t o s -> t (o s)")).then_inc(S(f"mn_in{p}"), 16)
                if b >= 2:
                    sp.wait_ge(S("pv_pe"), b - 1)
                full = S2T[-1][0]
                sp.dma_start(CN[p][:, 0:full, :], ctx[b][0:full * P, :].rearrange("(j p) d -> p j d", p=P)).then_inc(S(f"cn_in{p}"), 16)
                sp.dma_start(CN[p][0:S2 - full * P, full, :], ctx[b][full * P:S2, :]).then_inc(S(f"cn_in{p}"), 16)

            sp.wait_ge(S("xn_all"), B)
            sp.wait_ge(S("xy_done"), B)
            sp.wait_ge(S("lg_done"), B)
            with sp.Fori(0, E) as e:
                for n in range(PIECES):
                    raw = piece(n)[0]
                    if n < 8:
                        o, w = CH[n // 2]
                        o += HID * (n % 2)
                        src = GU[bass.ds(e, 1), :, :, o:o + w].rearrange("o p k n -> p (o k) n")
                    else:
                        src = DN[bass.ds(e, 1), :, 3 * (n - 8):min(3 * (n - 7), HC), :].rearrange("o p k n -> p (o k) n")
                    sp.wait_ge(S("lo_done"), e * PIECES + (n + 1))
                    sp.dma_start(raw, src).then_inc(S(f"w_in{n % SLOTS}"), 16)
            for b in range(B):
                sp.wait_ge(S("fin"), b + 1)
                sp.dma_start(out[b], X[:, b, :]).then_inc(S("out_st"), 16)
            sp.wait_ge(S("out_st"), 16 * B)

        @block.gpsimd
        def _(pool):
            own = Handoff(pool, S("pool_own"))
            for t, v in ((ident, 0.0), (later, 0.0), (upto, 0.0), (before, 0.0)):
                last = pool.memset(t[:], v)
            own(last)
            for t, sign, op in ((ident, 1, ALU.not_equal), (later, -1, ALU.is_ge), (upto, 1, ALU.is_gt), (before, 1, ALU.is_ge)):
                pool.affine_select(out=t[:], in_=t[:], compare_op=op, fill=1.0, base=0, pattern=[[-sign, P]],
                                   channel_multiplier=sign).then_inc(S("masks"), 1)
            pool.memset(ones[:], 1.0).then_inc(S("masks"), 1)
            pool.iota(rt_io[:], [[0, B], [1, E]], base=0, channel_multiplier=0,
                      allow_small_or_imprecise_dtypes=True).then_inc(S("iota_e"), 1)
            pool.wait_ge(S("la_done"), 1)
            pool.wait_ge(S("masks"), 5)
            pool.wait_ge(S("k_done"), 1)
            pool.wait_ge(S("rows_zero"), 16 * 2 * ZPARTS)
            for b in range(B):
                p = b % 2
                if b >= 2:
                    pool.wait_ge(S("ld_pe"), b - 1)
                pool.tensor_tensor(LR[p][:], la[:, b, :].unsqueeze(2).broadcast_to([T, H, T]),
                                   upto[0:T, 0:T].unsqueeze(1).broadcast_to([T, H, T]), ALU.mult).then_inc(S("lr_done"), 1)
                if b >= 2:
                    pool.wait_ge(S("e_done"), b - 1)
                pool.tensor_tensor(MB[p][:], gtok[:, b, H:].unsqueeze(2).broadcast_to([T, H, T]),
                                   upto[0:T, 0:T].unsqueeze(1).broadcast_to([T, H, T]), ALU.mult).then_inc(S("mb_done"), 1)
            for n, t in ((0, vT), (1, qT)):
                for c in range(KC):
                    one, two, three = TAP[c % 2]
                    pool.wait_ge(S("taps_act"), n * KC + c + 1)
                    pool.tensor_tensor(two[:], two[:], three[:], ALU.add).then_inc(S("tap_a"), 1)
                    pool.tensor_tensor(t[:, c], t[:, c], one[:], ALU.add).then_inc(S("tap_a"), 1)
                    pool.wait_ge(S("tap_a"), 2 * (n * KC + c + 1))
                    pool.tensor_tensor(t[:, c], t[:, c], two[:], ALU.add).then_inc(S("cv_pool"), 1)
            pool.wait_ge(S("cw_in"), 48)
            for b in range(B):
                pool.tensor_tensor(X[:, b, :], X[:, b, :], bo_b[:], ALU.add).then_inc(S("xb_done"), 1)
            for b0 in range(0, B, 2):
                for b, p in ((b0, 0), (b0 + 1, 1)):
                    pool.wait_ge(S(f"mn_in{p}"), 16 * (b // 2 + 1))
                    pool.tensor_scalar(MN[p][:], MN[p][:], NEG, None, ALU.mult).then_inc(S("mn_done"), 1)
                for b, p in ((b0, 0), (b0 + 1, 1)):
                    pool.wait_ge(S("y_norm"), b + 1)
                    pool.tensor_tensor(X[:, b, :], X[:, b, :], YN[p][:], ALU.add).then_inc(S("xy_done"), 1)
            pool.wait_ge(S("rows_zero"), 16 * 2 * ZPARTS)
            pool.wait_ge(S("xn_all"), B)
            pool.wait_ge(S("gi_set"), 1)
            for c in (0, 1):
                for b in range(B):
                    pool.indirect_dma_start(XGd[:, :], bass.IndirectOffsetOnAxis(gi[:, c, b:b + 1], 0), XN[:, b, :], None)\
                        .then_inc(S("xg_scat"), 16)
            pool.wait_ge(S("xg_scat"), 16 * 2 * B)
            pool.dma_start(XG[:], XGd[0:P, :]).then_inc(S("xg_in"), 16)
            pool.wait_ge(S("nt_set"), 1)
            with pool.Fori(0, E) as e:
                nt = pool.value_load(nti[0:1, 0, bass.ds(e, 1)], min_val=1, max_val=MAXNT)
                first = pool.value_load(nti[0:1, 1, bass.ds(e, 1)], min_val=0, max_val=NITEM - 2)
                with pool.Fori(0, nt) as tile:
                    item = nc.s_assert_within(pool.snap(first + tile), 0, NITEM - 2)
                    pool.wait_ge(S("xg_tr"), item + 1)
                    pool.sem_inc(S("pool_io"), 1)
                    pool.dma_start(XG[:], XGd[bass.ds((item + 1) * P, P), :]).then_inc(S("xg_in"), 16)
                    pool.wait_ge(S("y_ev"), item + 2)
                    pool.sem_inc(S("pool_io"), 1)
                    pool.dma_start(YGd[bass.ds(item * P, P), :], YS[:]).then_inc(S("y_stored"), 16)
                    pool.wait_ge(S("y_stored"), item * 16 + 16)
                    pool.sem_inc(S("y_free"), 1)
            pool.wait_ge(S("moe_end"), 1)
            for b in range(B):
                for c in (0, 1):
                    pool.indirect_dma_start(YG[:, c, b, :], None, YGd[:, :], bass.IndirectOffsetOnAxis(gi[:, c, b:b + 1], 0))\
                        .then_inc(S(f"yg_in{b}"), 16)

        @block.tensor
        def _(pe):
            def mm(o, l, r, start, stop):
                return pe.matmul(o, l, r, start=start, stop=stop)

            pe.wait_ge(S("masks"), 5)
            for b in range(B):
                pe.wait_ge(S("xn_a"), b + 1)
                if b >= 2:
                    pe.wait_ge(S("xt_ev"), b - 1)
                for k in range(KC):
                    last = pe.transpose(PS[b % 2][:, k * T:(k + 1) * T], XN[:, b, k * P:(k + 1) * P], ident[0:T, 0:T])
                last.then_inc(S("xt_pe"), 1)
            pe.wait_ge(S("xt_ev"), B)

            def project(n, w, wsem):
                pe.wait_ge(S(wsem), 16)
                for c in range(KC):
                    for hf in (0, 1):
                        g = n * 8 + c * 2 + hf
                        if g >= 4:
                            pe.wait_ge(S("pj_ev"), g - 3)
                        for k in range(KC):
                            last = mm(PS[4 + g % 4][:, 0:HALF], w[:, k, c * P:(c + 1) * P],
                                      xT[:, k, hf * HB:(hf + 1) * HB, :], k == 0, k == KC - 1)
                        last.then_inc(S("pj_pe"), 1)

            def square_sums(n, sq, banks):
                pe.wait_ge(S("sq_act"), n + 1)
                for hf in (0, 1):
                    for k in range(KC):
                        last = mm(banks[hf][:, 0:HALF], ones[:], sq[:, k, hf * HB:(hf + 1) * HB, :], k == 0, k == KC - 1)
                    last.then_inc(S("ns_pe"), 1)

            project(0, Wk, "wk_in")
            pe.wait_ge(S("small_in"), 16 * 4)
            for hf in (0, 1):
                for k in range(KC):
                    last = mm(PS[2 + hf][0:32, 0:HALF], Wab[:, k, :], xT[:, k, hf * HB:(hf + 1) * HB, :], k == 0, k == KC - 1)
                last.then_inc(S("gate_pe"), 1)
            pe.wait_ge(S("gate_act"), 2)
            for b in range(B):
                last = pe.transpose(PS[2][0:T, b * 32:(b + 1) * 32], gT[:, b, :], ident[0:32, 0:32])
            last.then_inc(S("gtok_pe"), 1)
            square_sums(0, SQk, PS[0:2])

            pe.wait_ge(S("k_done"), 1)
            for b in range(B):
                p = b % 2
                pe.wait_ge(S("lr_done"), b + 1)
                if b >= 1:
                    pe.wait_ge(S("ex_act"), b)
                for i in range(4):
                    last = mm(PS[i][0:T, 0:4 * T], later[0:T, 0:T], LR[p][:, 4 * i:4 * i + 4, :], True, True)
                last.then_inc(S("ld_pe"), 1)
                if b >= 1:
                    pe.wait_ge(S("bb_done"), b)
                for i in range(4):
                    for c in range(KC):
                        kk = kT[32 * i:32 * i + 32, c, b, :]
                        last = pe.matmul(PS[4 + i][0:T, c * T:(c + 1) * T], kk, kk, start=True, stop=True)
                last.then_inc(S("g_pe"), 1)

            for b in range(B):
                if b >= 2:
                    pe.wait_ge(S("k_tok"), b - 1)
                else:
                    pe.wait_ge(S("ex_act"), B)
                for c in range(KC):
                    last = pe.transpose(PS[2 + b % 2][0:T, c * P:(c + 1) * P], kT[:, c, b, :], ident[:])
                last.then_inc(S("k_pe"), 1)
            pe.wait_ge(S("bb_done"), B)
            project(1, Wv, "wv_in")
            project(2, Wq, "wq_in")
            pe.wait_ge(S("post_act"), 2)
            for b in range(B):
                if b >= 2:
                    pe.wait_ge(S("vt_ev"), b - 1)
                for c in range(KC):
                    last = pe.transpose(PS[2 + b % 2][0:T, c * P:(c + 1) * P], vT[:, c, b, :], ident[:])
                last.then_inc(S("vt_pe"), 1)
            pe.wait_ge(S("pj_ev"), 24)
            square_sums(1, SQq, PS[6:8])

            pe.wait_ge(S("wo_in"), 16)

            def transposed(src, b, bank, sem):
                for k in range(KC):
                    last = pe.transpose(bank[:, k * T:(k + 1) * T], src[:, k * P:(k + 1) * P], ident[0:T, 0:T])
                last.then_inc(S(sem), 1)

            def pair(b0):
                return [(b0 + p, p, PS[4 * p:4 * p + 4]) for p in (0, 1)]

            def earlier_blocks(b0, i, s0, w):
                for b, p, bank in pair(b0):
                    pe.wait_ge(S(f"bc_in{p}"), 16 * (b // 2 + 1))
                    pe.wait_ge(S("u_ev"), 4 * b0 + 2 * (i - 1) + p + 1)
                    for h in range(H):
                        last = mm(bank[3][s0:s0 + w, h * DH:(h + 1) * DH], diag_cols(BC[p], i)[0:s0, h, :],
                                  UU[p][0:s0, h * DH:(h + 1) * DH], True, True)
                    last.then_inc(S("acc_pe"), 1)

            def block_of_u(b0, i, s0, w):
                for b, p, bank in pair(b0):
                    if i:
                        pe.wait_ge(S("r_done"), 3 * b0 + 2 * (i - 1) + p + 1)
                    else:
                        pe.wait_ge(S(f"mt_in{p}"), 64 * (b // 2 + 1))
                        if b0:
                            pe.wait_ge(S("mv_c"), 2 * b0 + p - 1)
                    for h in range(H):
                        rhs = RR[p][s0:s0 + w, h * DH:(h + 1) * DH] if i else Vt[0:w, b, h * DH:(h + 1) * DH]
                        last = mm(bank[0][s0:s0 + w, h * DH:(h + 1) * DH], MT[p][s0:s0 + w, h, 0:w], rhs, True, True)
                    last.then_inc(S("u_pe"), 1)

            block_of_u(0, *BLK[0])
            earlier_blocks(0, *BLK[1])
            for b0 in range(0, B, 2):
                two = pair(b0)
                block_of_u(b0, *BLK[1])
                for blk in BLK[2:]:
                    earlier_blocks(b0, *blk)
                    block_of_u(b0, *blk)
                for b, p, bank in two:
                    pe.wait_ge(S("u_ev"), 4 * b0 + 6 + p + 1)
                    transposed(UU[p], b, bank[2], "ut_pe")
                for b, p, bank in two:
                    pe.wait_ge(S("ut_ev"), b + 1)
                    for g in range(4):
                        for c in range(KC):
                            last = pe.matmul(bank[g][0:T, c * T:(c + 1) * T], TR[p][32 * g:32 * g + 32, c, :],
                                             qT[32 * g:32 * g + 32, c, b, :], start=True, stop=True)
                    last.then_inc(S("w_pe"), 1)
                for b, p, bank in two:
                    pe.wait_ge(S("wm_done"), b + 1)
                    for h in range(H):
                        c, g = h // 4, h % 4
                        last = mm(bank[0][32 * g:32 * g + DH, c * T:(c + 1) * T], Kt[:, b, h * DH:(h + 1) * DH], WM[p][:, h, :], True, True)
                    last.then_inc(S("o_pe"), 1)
                for b, p, bank in two:
                    pe.wait_ge(S("ot_ev"), b + 1)
                    for k in range(KC):
                        last = mm(bank[2][0:T, :], TR[p][:, k, :], Wo[:, k, :], k == 0, k == KC - 1)
                    last.then_inc(S("wo_pe"), 1)
                for b, p, bank in two:
                    pe.wait_ge(S("xh_done"), b + 1)
                    transposed(UU[p], b, bank[3], "xh_pe")
                for b, p, bank in two:
                    pe.wait_ge(S("xh_ev"), b + 1)
                    pe.wait_ge(S(f"ct_in{p}"), 16 * (b // 2 + 1))
                    for hf in (0, 1):
                        for k in range(KC):
                            last = mm(bank[hf][0:T, 0:S2H], TR[p][:, k, :], CT[p][:, k, hf * S2H:(hf + 1) * S2H], k == 0, k == KC - 1)
                    last.then_inc(S("sc_pe"), 1)
                for b, p, bank in two:
                    pe.wait_ge(S("pr_done"), b + 1)
                    for j, s0, w in S2T:
                        last = pe.transpose(bank[2 + j // 4][0:w, (j % 4) * T:(j % 4 + 1) * T], PR[p][:, s0:s0 + w], ident[0:T, 0:T])
                    last.then_inc(S("pt_pe"), 1)
                for b, p, bank in two:
                    pe.wait_ge(S("pt_ev"), b + 1)
                    pe.wait_ge(S(f"cn_in{p}"), 32 * (b // 2 + 1))
                    for j, s0, w in S2T:
                        last = mm(bank[0][0:T, :], PT[p][0:w, j, :], CN[p][0:w, j, :], j == 0, j == len(S2T) - 1)
                    last.then_inc(S("pv_pe"), 1)
                if b0 + 2 < B:
                    block_of_u(b0 + 2, *BLK[0])
                for b, p, bank in two:
                    pe.wait_ge(S("xn_all"), b + 1)
                    for k in range(KC):
                        last = pe.transpose(bank[1][:, k * T:(k + 1) * T], XN[:, b, k * P:(k + 1) * P], ident[0:T, 0:T])
                    last.then_inc(S("nt_pe"), 1)
                if b0 + 2 < B:
                    earlier_blocks(b0 + 2, *BLK[1])
                if b0 == 0:
                    pe.wait_ge(S("cw_in"), 48)
                for b, p, bank in two:
                    pe.wait_ge(S("nt_ev"), b + 1)
                    for k in range(KC):
                        last = mm(bank[2][0:T, 0:E], TR[p][:, k, :], Wr[:, k, :], k == 0, k == KC - 1)
                    last.then_inc(S("lg_pe"), 1)

            pe.wait_ge(S("sel_done"), 1)
            mm(PS[0][0:T, 0:B * E], before[0:T, 0:T], rt_eq[:].rearrange("t b e -> t (b e)"), True, True)
            mm(PS[1][0:T, 0:B * E], ones[0:T, 0:T], rt_eq[:].rearrange("t b e -> t (b e)"), True, True).then_inc(S("cnt_pe"), 1)

            def tile_transposed():
                for k in range(KC):
                    last = pe.transpose(PS[6][:, k * P:(k + 1) * P], XG[:, k * P:(k + 1) * P], ident[:])
                last.then_inc(S("xg_tr"), 1)

            pe.sem_inc(S("gu_pe"), 4)
            pe.sem_inc(S("y_pe"), 1)
            pe.sem_inc(S("ht_pe"), 2)
            pe.wait_ge(S("nt_set"), 1)
            pe.wait_ge(S("xg_in"), 16)
            tile_transposed()
            with pe.Fori(0, E) as e:
                nt = pe.value_load(nti[0:1, 0, bass.ds(e, 1)], min_val=1, max_val=MAXNT)
                first = pe.value_load(nti[0:1, 1, bass.ds(e, 1)], min_val=0, max_val=NITEM - 2)
                split = pe.snap(e * PIECES + SLOTS)
                with pe.Fori(0, nt) as tile:
                    item = pe.snap(first + tile, min_val=0, max_val=NITEM - 2)

                    def product(o, xh, xl, wh, wl, start, stop):
                        mm(o, xh, wh, start, False)
                        mm(o, xh, wl, False, False)
                        return mm(o, xl, wh, False, stop)

                    def hidden_transposed(c):
                        o, w = CH[c]
                        pe.wait_ge(S("h_done"), item * 4 + (c + 3))
                        pe.wait_ge(S("ht_lo"), item * 4 + (c + 1))
                        for j in range(w // P):
                            last = pe.transpose(PS[4 + c % 2][:, j * P:(j + 1) * P], HH[c % 2][:, j * P:(j + 1) * P], ident[:])
                        last.then_inc(S("ht_pe"), 1)

                    pe.wait_ge(S("xt_lo"), item + 1)
                    for c, (o, w) in enumerate(CH):
                        pe.wait_ge(S("lo_done"), split + (2 * c + 2))
                        pe.wait_ge(S("h_done"), item * 4 + (c + 1))
                        for half in (0, 1):
                            at_w = half * HID + o
                            for k in range(KC):
                                last = product(PS[2 * (c % 2) + half][:, 0:w], XTH[:, k, :], XTL[:, k, :],
                                               GWH[:, k, at_w:at_w + w], GWL[:, k, at_w:at_w + w], k == 0, k == KC - 1)
                        last.then_inc(S("gu_pe"), 1)
                        if c:
                            hidden_transposed(c - 1)
                    pe.wait_ge(S("xg_in"), (item + 2) * 16)
                    tile_transposed()
                    pe.wait_ge(S("y_ev"), item + 1)
                    for n, (chunks, rows) in enumerate(DOWN):
                        pe.wait_ge(S("ht_lo"), item * 4 + (chunks + 2))
                        pe.wait_ge(S("lo_done"), split + (9 + n))
                        for j in rows:
                            last = product(PS[7][:, :], HTH[:, j, :], HTL[:, j, :], DWH[:, j, :], DWL[:, j, :], j == 0, j == HC - 1)
                        if n == 1:
                            hidden_transposed(3)
                    last.then_inc(S("y_pe"), 1)

        @block.scalar
        def _(act):
            own = Handoff(act, S("act_own"))
            act.dma_start(Wab[:], WabT.rearrange("(k p) n -> p k n", p=P)).then_inc(S("small_in"), 16)
            act.dma_start(b_ab[:], bab).then_inc(S("small_in"), 16)
            act.dma_start(b_qkv[:], bqkv).then_inc(S("small_in"), 16)
            act.dma_start(w_conv[:], conv).then_inc(S("small_in"), 16)
            act.wait_ge(S("consts"), 1)
            act.wait_ge(S("mv_a"), 1)
            act.activation(rstd[:], mv[:, :, 1], ACT.Sqrt, bias=eps_ln[0:T, :]).then_inc(S("sd_a"), 1)
            for b in range(B):
                act.wait_ge(S("xt_pe"), b + 1)
                act.activation(xT[:, :, b, :], PS[b % 2][:, 0:KC * T].rearrange("p (k t) -> p k t", k=KC), ACT.Copy).then_inc(S("xt_ev"), 1)
            act.wait_ge(S("small_in"), 16 * 4)
            act.wait_ge(S("pads"), 1)

            def silu_in(n, w, buf, c):
                for hf in (0, 1):
                    act.wait_ge(S("pj_pe"), n * 8 + c * 2 + hf + 1)
                    act.activation(buf[:, c, hf * HB:(hf + 1) * HB, 2:2 + T],
                                   PS[4 + (c * 2 + hf) % 4][:, 0:HALF].rearrange("p (b t) -> p b t", b=HB), ACT.Silu,
                                   bias=b_qkv[:, w, c:c + 1]).then_inc(S("pj_ev"), 1)

            def taps(n, w, buf, t, c):
                act.wait_ge(S("pj_ev"), 8 * (n + 1) + 2 * c + 2)
                act.activation(t[:, c], buf[:, c, :, 0:T], ACT.Copy, scale=w_conv[:, w, c, 0:1])
                if n * KC + c >= 2:
                    act.wait_ge(S("cv_pool"), n * KC + c - 1)
                for j in range(1, TAPS):
                    last = act.activation(TAP[c % 2][j - 1][:], buf[:, c, :, j:j + T], ACT.Copy, scale=w_conv[:, w, c, j:j + 1])
                last.then_inc(S("taps_act"), 1)

            def norms(n, t, sq, banks):
                act.wait_ge(S("post_act"), 2 * n + 1)
                act.activation(sq[:], t[:], ACT.Square).then_inc(S("sq_act"), 1)
                for hf in (0, 1):
                    act.wait_ge(S("ns_pe"), 2 * n + hf + 1)
                    act.activation(rn[:, hf * HB:(hf + 1) * HB, :], banks[hf][:, 0:HALF].rearrange("p (b t) -> p b t", b=HB),
                                   ACT.Sqrt).then_inc(S("nr_act"), 1)

            for c in range(KC):
                silu_in(0, 0, PBk, c)
            for hf in (0, 1):
                act.wait_ge(S("gate_pe"), hf + 1)
                act.activation(gT[:, hf * HB:(hf + 1) * HB, :], PS[2 + hf][0:32, 0:HALF].rearrange("p (b t) -> p b t", b=HB),
                               ACT.Sigmoid, bias=b_ab[:]).then_inc(S("gate_act"), 1)
            for c in range(KC):
                act.wait_ge(S("cv_done"), c + 1)
                last = act.activation(kT[:, c], kT[:, c], ACT.Silu)
            last.then_inc(S("post_act"), 1)
            norms(0, kT, SQk, PS[0:2])
            act.wait_ge(S("ga_done"), 1)
            act.activation(la[:], la[:], ACT.Ln).then_inc(S("la_done"), 1)
            for b in range(B):
                p = b % 2
                act.wait_ge(S("ld_pe"), b + 1)
                if b >= 2:
                    act.wait_ge(S(f"ed_out{p}"), 16 * (b // 2))
                for i in range(4):
                    last = act.activation(EB[p][:, 4 * i:4 * i + 4, :], PS[i][0:T, 0:4 * T].rearrange("p (h t) -> p h t", h=4), ACT.Exp)
                last.then_inc(S("ex_act"), 1)
            for b in range(B):
                act.wait_ge(S("k_pe"), b + 1)
                act.activation(Kt[:, b, :], PS[2 + b % 2][0:T, :], ACT.Copy).then_inc(S("k_tok"), 1)
            act.wait_ge(S("pads_qv"), 1)
            for c in range(KC):
                silu_in(1, 2, PBv, c)
            for c in range(KC):
                silu_in(2, 1, PBq, c)
                taps(0, 2, PBv, vT, c)
            for c in range(KC):
                taps(1, 1, PBq, qT, c)
                act.wait_ge(S("cv_pool"), c + 1)
                last = act.activation(vT[:, c], vT[:, c], ACT.Silu)
            last.then_inc(S("post_act"), 1)
            for c in range(KC):
                act.wait_ge(S("cv_pool"), KC + c + 1)
                last = act.activation(qT[:, c], qT[:, c], ACT.Silu)
            last.then_inc(S("post_act"), 1)
            for b in range(B):
                act.wait_ge(S("vt_pe"), b + 1)
                act.activation(Vt[:, b, :], PS[2 + b % 2][0:T, :], ACT.Copy).then_inc(S("vt_ev"), 1)
            norms(1, qT, SQq, PS[6:8])
            def block_of_u(b0, i, s0, w):
                for p in (0, 1):
                    act.wait_ge(S("u_pe"), 4 * b0 + 2 * i + p + 1)
                    act.activation(UU[p][s0:s0 + w, :], PS[4 * p][s0:s0 + w, :], ACT.Copy).then_inc(S("u_ev"), 1)

            for b0 in range(0, B, 2):
                two = [(b0 + p, p, PS[4 * p:4 * p + 4]) for p in (0, 1)]
                if b0 == 0:
                    act.wait_ge(S("md_out"), 32)
                    block_of_u(0, *BLK[0])
                for blk in BLK[1:]:
                    block_of_u(b0, *blk)

                def evacuated(pe_sem, bank, b, p, sem):
                    act.wait_ge(S(pe_sem), b + 1)
                    act.activation(TR[p][:], bank[:, 0:KC * T].rearrange("p (k t) -> p k t", k=KC), ACT.Copy).then_inc(S(sem), 1)

                for b, p, bank in two:
                    evacuated("ut_pe", bank[2], b, p, "ut_ev")
                for b, p, bank in two:
                    evacuated("o_pe", bank[0], b, p, "ot_ev")
                for b, p, bank in two:
                    act.wait_ge(S("mv_c"), 2 * b0 + p + 1)
                    act.activation(sd[:, b:b + 1], mv[:, b, 1:2], ACT.Sqrt, bias=eps_ln[0:T, :]).then_inc(S("sd_c"), 1)
                for b, p, bank in two:
                    evacuated("xh_pe", bank[3], b, p, "xh_ev")
                for b, p, bank in two:
                    act.wait_ge(S("sc_dve"), b + 1)
                    act.activation(PR[p][:], PR[p][:], ACT.Exp, bias=nmax[:, b:b + 1], accum_out=rsum[:, b:b + 1]).then_inc(S("pr_done"), 1)
                for b, p, bank in two:
                    act.wait_ge(S("pt_pe"), b + 1)
                    full, rest = len(S2T) - 1, S2T[-1][2]
                    act.activation(PT[p][:, 0:4, :], bank[2][:, 0:4 * T].rearrange("p (j t) -> p j t", t=T), ACT.Copy)
                    act.activation(PT[p][:, 4:full, :], bank[3][:, 0:(full - 4) * T].rearrange("p (j t) -> p j t", t=T), ACT.Copy)
                    act.activation(PT[p][0:rest, full, :], bank[3][0:rest, (full - 4) * T:(full - 3) * T], ACT.Copy).then_inc(S("pt_ev"), 1)
                for b, p, bank in two:
                    act.wait_ge(S("mv_c"), 2 * b0 + p + 3)
                    act.activation(sd[:, b:b + 1], mv[:, b, 1:2], ACT.Sqrt, bias=eps_ln[0:T, :]).then_inc(S("sd_c"), 1)
                for b, p, bank in two:
                    act.wait_ge(S("y_norm"), b + 1)
                    own(act.activation(RR[p][:], YN[p][:], ACT.Square, accum_out=ss[:, b:b + 1]))
                    act.activation(ss[:, b:b + 1], ss[:, b:b + 1], ACT.Sqrt, bias=eps_rms[0:T, :], scale=1.0 / D).then_inc(S("ss_done"), 1)
                if b0 + 2 < B:
                    block_of_u(b0 + 2, *BLK[0])
                for b, p, bank in two:
                    evacuated("nt_pe", bank[1], b, p, "nt_ev")
                for b, p, bank in two:
                    act.wait_ge(S("lg_pe"), b + 1)
                    act.activation(LG[:, b, :], bank[2][0:T, 0:E], ACT.Copy).then_inc(S("lg_done"), 1)
            act.wait_ge(S("rt_sub"), 1)
            act.activation(rt_p[:], rt_p[:], ACT.Exp).then_inc(S("rt_exp"), 1)
            act.wait_ge(S("nt_set"), 1)

            def rows_high(n):
                act.wait_ge(S("xg_tr"), n)
                act.activation(XTH[:], PS[6][:, :].rearrange("p (k t) -> p k t", k=KC), ACT.Copy).then_inc(S("xt_hi"), 1)

            def weights_high(n, loads, free, no_tile):
                raw, hi, _ = piece(n)
                act.wait_ge(S(f"w_in{n % SLOTS}"), loads + 16 * (n // SLOTS + 1))
                if n < 8:
                    act.wait_ge(S("gu_pe"), free + (n // 2 + 1))
                else:
                    act.wait_ge(S("y_pe"), no_tile + 1)
                act.activation(hi, raw, ACT.Copy).then_inc(S("hi_done"), 1)

            for n in range(AHEAD):
                weights_high(n, 0, 0, 0)
            rows_high(1)
            with act.Fori(0, E) as e:
                nt = act.value_load(nti[0:1, 0, bass.ds(e, 1)], min_val=1, max_val=MAXNT)
                first = act.value_load(nti[0:1, 1, bass.ds(e, 1)], min_val=0, max_val=NITEM - 2)
                free = act.snap(first * 4)
                loads = act.snap(e * (16 * PIECES // SLOTS))

                def tile_of_expert(tile, with_weights):
                    item = act.snap(first + tile)

                    def gated(c):
                        o, w = CH[c]
                        act.wait_ge(S("ht_pe"), item * 4 + (c + 1))
                        act.wait_ge(S("gu_pe"), item * 4 + (c + 5))
                        act.activation(HH[c % 2][:, 0:w], PS[2 * (c % 2)][:, 0:w], ACT.Silu).then_inc(S("silu_done"), 1)

                    def hidden_high(c):
                        o, w = CH[c]
                        act.wait_ge(S("ht_pe"), item * 4 + (c + 3))
                        act.activation(HTH[:, o // P:(o + w) // P, :], PS[4 + c % 2][:, 0:w].rearrange("p (j t) -> p j t", t=P),
                                       ACT.Copy).then_inc(S("ht_hi"), 1)

                    for step in ORDER:
                        if step[0] == "w" and with_weights:
                            weights_high(step[1], loads, free, first)
                        elif step[0] == "h":
                            gated(step[1])
                        elif step[0] == "t":
                            hidden_high(step[1])
                        elif step[0] == "x":
                            rows_high(item + 2)

                tile_of_expert(0, True)
                with act.If(nt > 1):
                    with act.Fori(1, nt) as tile:
                        tile_of_expert(tile, False)
                with act.If(e < E - 1):
                    for n in range(AHEAD):
                        weights_high(n, loads + 16 * PIECES // SLOTS, free + nt * 4, 0)

        @block.vector
        def _(dve):
            own = Handoff(dve, S("dve_own"))
            tt, ts, stt = dve.tensor_tensor, dve.tensor_scalar, dve.scalar_tensor_tensor
            dve.memset(eps_ln[:], LN_EPS)
            dve.memset(eps_rms[:], RMS_EPS)
            dve.memset(zero_col[:], 0.0).then_inc(S("consts"), 1)
            dve.memset(ZR[:], 0.0).then_inc(S("zr_set"), 1)
            dve.memset(PBk[:, :, :, 0:2], 0.0)
            dve.memset(PBk[:, :, :, 2 + T:TP], 0.0).then_inc(S("pads"), 1)
            for b in range(B):
                dve.wait_ge(S(f"x_in{b}"), 16)
                last = dve.bn_stats(stats[:, b, :], X[:, b, :])
            own(last)
            for b in range(B):
                last = dve.bn_aggr(mv[:, b, :], stats[:, b, :])
            last.then_inc(S("mv_a"), 1)
            dve.wait_ge(S("sd_a"), 1)
            dve.wait_ge(S("mv_a"), 1)
            own(dve.reciprocal(rstd[:], rstd[:]))
            for b in range(B):
                ts(XN[:, b, :], X[:, b, :], mv[:, b, 0:1], rstd[:, b:b + 1], ALU.subtract, ALU.mult).then_inc(S("xn_a"), 1)

            def normalise(n, t, sem):
                dve.wait_ge(S("nr_act"), 2 * n + 2)
                own(ts(rn[:], rn[:], L2_EPS, None, ALU.add))
                own(dve.reciprocal(rn[:], rn[:]))
                for c in range(KC):
                    last = tt(t[:, c], t[:, c], rn[:], ALU.mult)
                last.then_inc(S(sem), 1)

            dve.wait_ge(S("small_in"), 16 * 4)
            for c in range(KC):
                dve.wait_ge(S("pj_ev"), 2 * c + 2)
                own(ts(kT[:, c], PBk[:, c, :, 0:T], w_conv[:, 0, c, 0:1], None, ALU.mult))
                for j in range(1, TAPS):
                    last = stt(kT[:, c], PBk[:, c, :, j:j + T], w_conv[:, 0, c, j:j + 1], kT[:, c], ALU.mult, ALU.add)
                    if j < TAPS - 1:
                        own(last)
                last.then_inc(S("cv_done"), 1)
            dve.wait_ge(S("gtok_pe"), 1)
            own(dve.tensor_copy(gtok[:], PS[2][0:T, 0:B * 32].rearrange("t (b g) -> t b g", b=B)))
            ts(la[:], gtok[:, :, 0:H], LEAST_DECAY, None, ALU.max).then_inc(S("ga_done"), 1)
            normalise(0, kT, "k_done")
            for b in range(B):
                p = b % 2
                dve.wait_ge(S("ex_act"), b + 1)
                dve.wait_ge(S("mb_done"), b + 1)
                tt(EB[p][:], EB[p][:], MB[p][:], ALU.mult).then_inc(S("e_done"), 1)
                dve.wait_ge(S("g_pe"), b + 1)
                dve.wait_ge(S("e_done"), b + 1)
                if b >= 2:
                    dve.wait_ge(S(f"bd_out{p}"), 16 * (b // 2))
                for g in range(4):
                    sums = PS[4 + g][0:T, 0:4 * T].rearrange("p (c t) -> p c t", c=KC)
                    blocks = BB[p][:, 0:3 * H * 32].rearrange("r (i c g s) -> r g c i s", i=3, c=KC, g=4)[:, g]
                    tt(blocks, sums[:, :, 0:96].rearrange("r c (i s) -> r c i s", i=3),
                       EB[p][:, g::4, 0:96].rearrange("r c (i s) -> r c i s", i=3), ALU.mult)
                    last = tt(diag_cols(BB[p], 3)[:, g::4, :], sums[:, :, 96:T], EB[p][:, g::4, 96:T], ALU.mult)
                last.then_inc(S("bb_done"), 1)
            dve.wait_ge(S("bb_done"), B)
            dve.wait_ge(S("g_pe"), B)
            dve.wait_ge(S("ed_out0"), 16 * B // 2)
            dve.wait_ge(S("ed_out1"), 16 * B // 2)
            dve.wait_ge(S("bd_out0"), 16 * B // 2)
            dve.wait_ge(S("bd_out1"), 16 * B // 2)
            for buf in (PBq, PBv):
                dve.memset(buf[:, :, :, 0:2], 0.0)
                last = dve.memset(buf[:, :, :, 2 + T:TP], 0.0)
            last.then_inc(S("pads_qv"), 1)
            dve.memset(MI[:], 0.0)
            own(dve.memset(MI3[:], 0.0))
            dve.memset(MI[:].rearrange("p i r s -> p i (r s)")[:, :, ::33], 1.0)
            own(dve.memset(MI3[:].rearrange("p r s -> p (r s)")[:, ::LAST + 1], 1.0))
            dve.wait_ge(S("dg_in"), 16 * 4 * B)
            for s in range(1, 32):
                tm = TM[:, 0:3 * s * s].rearrange("p (i a r) -> p i a r", i=3, a=s)
                own(tt(tm, MI[:, :, 0:s, 0:s], DG[:, :, 0:s, s].unsqueeze(2).broadcast_to([P, 3, s, s]), ALU.mult))
                last = dve.tensor_reduce(MI[:, :, 0:s, s], tm, AX_X, ALU.add, negate=True)
                own(last)
            for s in range(1, LAST):
                tm = TM[:, 0:s * s].rearrange("p (a r) -> p a r", a=s)
                own(tt(tm, MI3[:, 0:s, 0:s], DG3[:, 0:s, s].unsqueeze(1).broadcast_to([P, s, s]), ALU.mult))
                own(dve.tensor_reduce(MI3[:, 0:s, s], tm, AX_X, ALU.add, negate=True))
            dve.sem_inc(S("mi_done"), 1)
            normalise(1, qT, "qkv_done")
            dve.wait_ge(S("md_out"), 32)
            dve.wait_ge(S("qkv_done"), 1)
            for b0 in range(0, B, 2):
                two = [(b0 + p, p, PS[4 * p:4 * p + 4]) for p in (0, 1)]
                for i, s0, w in BLK[1:]:
                    for b, p, bank in two:
                        dve.wait_ge(S("acc_pe"), 3 * b0 + 2 * (i - 1) + p + 1)
                        last = tt(RR[p][s0:s0 + w, :], Vt[s0:s0 + w, b, :], bank[3][s0:s0 + w, :], ALU.subtract)
                        last.then_inc(S("r_done"), 1)
                for b, p, bank in two:
                    dve.wait_ge(S("w_pe"), b + 1)
                    dve.wait_ge(S(f"ee_in{p}"), 16 * (b // 2 + 1))
                    for g in range(4):
                        last = tt(WM[p][:, g::4, :], bank[g][0:T, 0:4 * T].rearrange("p (h t) -> p h t", h=4),
                                  EE[p][:, g::4, :], ALU.mult)
                    last.then_inc(S("wm_done"), 1)

                def layer_norm(b, p):
                    own(dve.bn_stats(stats[:, b, :], X[:, b, :]))
                    dve.bn_aggr(mv[:, b, :], stats[:, b, :]).then_inc(S("mv_c"), 1)

                def normed(b, p, n, dst, sem):
                    dve.wait_ge(S("sd_c"), 2 * b0 + 2 * n + p + 1)
                    dve.wait_ge(S("mv_c"), 2 * b0 + 2 * n + p + 1)
                    own(dve.reciprocal(rstd[:, b:b + 1], sd[:, b:b + 1]))
                    ts(dst[:], X[:, b, :], mv[:, b, 0:1], rstd[:, b:b + 1], ALU.subtract, ALU.mult).then_inc(S(sem), 1)

                for b, p, bank in two:
                    dve.wait_ge(S("wo_pe"), b + 1)
                    dve.wait_ge(S("xb_done"), b + 1)
                    own(tt(X[:, b, :], X[:, b, :], bank[2][0:T, :], ALU.add))
                    layer_norm(b, p)
                for b, p, bank in two:
                    normed(b, p, 0, UU[p], "xh_done")
                for b, p, bank in two:
                    dve.wait_ge(S("sc_pe"), b + 1)
                    dve.wait_ge(S("mn_done"), b + 1)
                    for hf in (0, 1):
                        last = stt(PR[p][:, hf * S2H:(hf + 1) * S2H], bank[hf][0:T, 0:S2H], SCALE, MN[p][:, hf * S2H:(hf + 1) * S2H],
                                   ALU.mult, ALU.add)
                    own(last)
                    dve.tensor_reduce(nmax[:, b:b + 1], PR[p][:], AX_X, ALU.max, negate=True).then_inc(S("sc_dve"), 1)
                for b, p, bank in two:
                    dve.wait_ge(S("pv_pe"), b + 1)
                    own(dve.reciprocal(rsum[:, b:b + 1], rsum[:, b:b + 1]))
                    own(stt(X[:, b, :], bank[0][0:T, :], rsum[:, b:b + 1], X[:, b, :], ALU.mult, ALU.add))
                    layer_norm(b, p)
                for b, p, bank in two:
                    if b0:
                        dve.wait_ge(S("xy_done"), b - 1)
                    normed(b, p, 1, YN[p], "y_norm")
                if b0 == 0:
                    dve.wait_ge(S("cw_in"), 48)
                for b, p, bank in two:
                    dve.wait_ge(S("ss_done"), b + 1)
                    dve.wait_ge(S("y_norm"), b + 1)
                    own(dve.reciprocal(ss[:, b:b + 1], ss[:, b:b + 1]))
                    stt(XN[:, b, :], YN[p][:], ss[:, b:b + 1], nw_b[:], ALU.mult, ALU.mult).then_inc(S("xn_all"), 1)

            def bc(col):
                return col.unsqueeze(2).broadcast_to([T, B, E])

            dve.sem_inc(S("lo_done"), SLOTS)
            dve.wait_ge(S("lg_done"), B)
            dve.wait_ge(S("iota_e"), 1)
            own(dve.tensor_reduce(rt_m[:, :, 0], LG[:], AX_X, ALU.max))
            tt(rt_p[:], LG[:], bc(rt_m[:, :, 0]), ALU.subtract).then_inc(S("rt_sub"), 1)
            dve.wait_ge(S("rt_exp"), 1)
            own(dve.tensor_reduce(rt_m[:, :, 6], rt_p[:], AX_X, ALU.add))
            own(dve.reciprocal(rt_m[:, :, 6], rt_m[:, :, 6]))
            own(tt(rt_p[:], rt_p[:], bc(rt_m[:, :, 6]), ALU.mult))
            for c, oh in ((0, rt_o0), (1, rt_o1)):
                own(dve.tensor_reduce(rt_m[:, :, 2 * c], rt_p[:], AX_X, ALU.max))
                own(tt(rt_t[:], rt_p[:], bc(rt_m[:, :, 2 * c]), ALU.is_lt))
                own(stt(rt_t[:], rt_t[:], 100.0, rt_io[:], ALU.mult, ALU.add))
                own(dve.tensor_reduce(rt_m[:, :, 2 * c + 1], rt_t[:], AX_X, ALU.min))
                own(tt(oh[:], rt_io[:], bc(rt_m[:, :, 2 * c + 1]), ALU.is_equal))
                if c == 0:
                    own(stt(rt_p[:], oh[:], -2.0, rt_p[:], ALU.mult, ALU.add))
            tt(rt_eq[:], rt_o0[:], rt_o1[:], ALU.add).then_inc(S("sel_done"), 1)
            own(tt(rt_m[:, :, 6], rt_m[:, :, 0], rt_m[:, :, 2], ALU.add))
            own(dve.reciprocal(rt_m[:, :, 6], rt_m[:, :, 6]))
            dve.wait_ge(S("al_in"), 16)
            own(ts(al[:], al[:], -0.5, 2.0, ALU.max, ALU.min))
            own(ts(rt_m[:, :, 6], rt_m[:, :, 6], al[:], None, ALU.mult))
            for c in (0, 1):
                last = tt(wa[:, c, :], rt_m[:, :, 2 * c], rt_m[:, :, 6], ALU.mult)
            own(last)
            dve.wait_ge(S("cnt_pe"), 1)
            own(dve.memset(rt_boff[:, 0, :], 0.0))
            for b in range(B):
                own(tt(rt_boff[:, b + 1, :], rt_boff[:, b, :], PS[1][0:T, b * E:(b + 1) * E], ALU.add))
            own(dve.memset(rt_nt[:], 1.0))
            for m in range(1, MAXNT):
                own(stt(rt_nt[:], rt_boff[:, B, :], float(P * m), rt_nt[:], ALU.is_gt, ALU.add))
            own(dve.memset(rt_bs[:, 0:1], 0.0))
            for e in range(E):
                own(tt(rt_bs[:, e + 1:e + 2], rt_bs[:, e:e + 1], rt_nt[:, e:e + 1], ALU.add))
            dve.tensor_copy(nti[:, 0, :], rt_nt[:])
            dve.tensor_copy(nti[:, 1, :], rt_bs[:, 0:E]).then_inc(S("nt_set"), 1)
            own(tt(rt_pos[:], PS[0][0:T, 0:B * E].rearrange("t (b e) -> t b e", b=B), rt_boff[:, 0:B, :], ALU.add))
            own(stt(rt_pos[:], rt_bs[:, 0:E].unsqueeze(1).broadcast_to([T, B, E]), float(P), rt_pos[:], ALU.mult, ALU.add))
            for c, oh in ((0, rt_o0), (1, rt_o1)):
                own(tt(rt_t[:], rt_pos[:], oh[:], ALU.mult))
                own(dve.tensor_reduce(gf[:, c, :], rt_t[:], AX_X, ALU.add))
            dve.tensor_copy(gi[:], gf[:]).then_inc(S("gi_set"), 1)

            dve.sem_inc(S("h_done"), 2)
            dve.sem_inc(S("y_free"), 2)
            dve.memset(PS[7][:, :], 0.0).then_inc(S("y_zero"), 1)
            dve.wait_ge(S("y_zero"), 1)

            dve.sem_inc(S("ht_lo"), 2)

            def rows_low(n):
                dve.wait_ge(S("xt_hi"), n)
                tt(XTL[:], PS[6][:, :].rearrange("p (k t) -> p k t", k=KC), XTH[:].bitcast(F32), ALU.subtract).then_inc(S("xt_lo"), 1)

            def y_evacuated(n):
                dve.wait_ge(S("y_free"), n + 1)
                dve.wait_ge(S("y_pe"), n + 1)
                dve.tensor_copy(YS[:], PS[7][:, :]).then_inc(S("y_ev"), 1)

            def weights_low(n, split):
                raw, hi, lo = piece(n)
                dve.wait_ge(S("hi_done"), split + (n + 1))
                tt(lo, raw, hi.bitcast(F32), ALU.subtract).then_inc(S("lo_done"), 1)

            for n in range(AHEAD):
                weights_low(n, 0)
            rows_low(1)
            with dve.Fori(0, E) as e:
                nt = dve.value_load(nti[0:1, 0, bass.ds(e, 1)], min_val=1, max_val=MAXNT)
                first = dve.value_load(nti[0:1, 1, bass.ds(e, 1)], min_val=0, max_val=NITEM - 2)
                split = dve.snap(e * PIECES)

                def tile_of_expert(tile, with_weights):
                    item = dve.snap(first + tile)

                    def gated(c):
                        o, w = CH[c]
                        dve.wait_ge(S("silu_done"), item * 4 + (c + 1))
                        tt(HH[c % 2][:, 0:w], HH[c % 2][:, 0:w], PS[2 * (c % 2) + 1][:, 0:w], ALU.mult).then_inc(S("h_done"), 1)

                    def hidden_low(c):
                        o, w = CH[c]
                        dve.wait_ge(S("ht_hi"), item * 4 + (c + 1))
                        tt(HTL[:, o // P:(o + w) // P, :], PS[4 + c % 2][:, 0:w].rearrange("p (j t) -> p j t", t=P),
                           HTH[:, o // P:(o + w) // P, :].bitcast(F32), ALU.subtract).then_inc(S("ht_lo"), 1)

                    for step in ORDER:
                        if step[0] == "w" and with_weights:
                            weights_low(step[1], split)
                        elif step[0] == "h":
                            gated(step[1])
                        elif step[0] == "t":
                            hidden_low(step[1])
                        elif step[0] == "x":
                            rows_low(item + 2)
                        elif step[0] == "y":
                            y_evacuated(item)

                tile_of_expert(0, True)
                with dve.If(nt > 1):
                    with dve.Fori(1, nt) as tile:
                        tile_of_expert(tile, False)
                with dve.If(e < E - 1):
                    for n in range(AHEAD):
                        weights_low(n, split + PIECES)
                last_item = dve.snap(first + nt)
            y_evacuated(last_item)
            dve.wait_ge(S("xy_done"), B)
            dve.wait_ge(S("y_free"), last_item + 2)
            dve.sem_inc(S("moe_end"), 1)
            for b in range(B):
                dve.wait_ge(S(f"yg_in{b}"), 32)
                own(stt(X[:, b, :], YG[:, 0, b, :], wa[:, 0, b:b + 1], X[:, b, :], ALU.mult, ALU.add))
                stt(X[:, b, :], YG[:, 1, b, :], wa[:, 1, b:b + 1], X[:, b, :], ALU.mult, ALU.add).then_inc(S("fin"), 1)


def kernel(x, ctx_1024, mask_Bx1xS2_fk0, L0_attn_Wq, L0_attn_bq, L0_attn_Wk, L0_attn_bk, L0_attn_Wv, L0_attn_bv,
           L0_attn_Wa, L0_attn_ba, L0_attn_Wb, L0_attn_bb, L0_attn_conv_q, L0_attn_conv_k, L0_attn_conv_v, L0_attn_Wo,
           L0_attn_bo, L0_ffn_norm_weight, L0_ffn_router_weight, L0_ffn_gate_up_weight, L0_ffn_down_weight,
           L0_ffn_residual_alpha):
    import numpy as np
    import concourse.bacc as bacc
    from concourse.bass_utils import run_bass_kernel_spmd

    c = np.ascontiguousarray
    D, H, P = 512, 16, 128
    arrays = {
        "x": c(x), "ctx": c(ctx_1024), "ctxT": c(np.transpose(np.asarray(ctx_1024), (0, 2, 1))), "mask": c(mask_Bx1xS2_fk0),
        "WqT": c(np.asarray(L0_attn_Wq).T), "WkT": c(np.asarray(L0_attn_Wk).T), "WvT": c(np.asarray(L0_attn_Wv).T),
        "bqkv": c(np.stack([np.asarray(v).reshape(D // P, P).T for v in (L0_attn_bk, L0_attn_bq, L0_attn_bv)], 1)),
        "WabT": c(np.concatenate([np.asarray(L0_attn_Wa), np.asarray(L0_attn_Wb)], 0).T),
        "bab": c(np.concatenate([np.asarray(L0_attn_ba), np.asarray(L0_attn_bb)])[:, None]),
        "conv": c(np.stack([np.asarray(v).reshape(D // P, P, 4).transpose(1, 0, 2)
                            for v in (L0_attn_conv_k, L0_attn_conv_q, L0_attn_conv_v)], 1)),
        "WoT": c(np.asarray(L0_attn_Wo).T), "bo": c(L0_attn_bo), "norm_w": c(L0_ffn_norm_weight),
        "WrT": c(np.asarray(L0_ffn_router_weight).T),
        "GU": c(np.asarray(L0_ffn_gate_up_weight).transpose(0, 2, 1).reshape(8, D // P, P, -1).transpose(0, 2, 1, 3)),
        "DN": c(np.asarray(L0_ffn_down_weight).transpose(0, 2, 1).reshape(8, -1, P, D).transpose(0, 2, 1, 3)),
        "alpha": c(np.asarray(L0_ffn_residual_alpha).reshape(1)),
    }
    nc = bacc.Bacc("TRN2", target_bir_lowering=False, num_devices=1)
    args = [nc.dram_tensor(f"in_{n}", a.shape, mybir.dt.from_np(a.dtype), kind="ExternalInput").ap() for n, a in arrays.items()]
    out = nc.dram_tensor("out", (8, 100, D), F32, kind="ExternalOutput").ap()
    decoder_layer(nc, *args, out)
    r = run_bass_kernel_spmd(nc, [{f"in_{n}": a for n, a in arrays.items()}], core_ids=[0])
    return r.results[0]["out"]
```
